# Optimizing a Trainium2 kernel written in Bass

```python
import numpy as np
import jax
import jax.numpy as jnp

def _softmax(x, axis=-1):
    return jax.nn.softmax(x, axis=axis)

def _gelu(x):
    return jax.nn.gelu(x, approximate=True)

def _silu(x):
    return jax.nn.silu(x)

def _sigmoid(x):
    return jax.nn.sigmoid(x)

def _layernorm(x, axis=-1, eps=1e-05):
    m = jnp.mean(x, axis=axis, keepdims=True)
    v = jnp.var(x, axis=axis, keepdims=True)
    return (x - m) / jnp.sqrt(v + eps)

def _scatter_add(tgt, idx, src, axis=0):
    return tgt.at[idx].add(src)

def _segment_sum(src, seg, n):
    return jax.ops.segment_sum(src, seg, n)
kernel_name = 'mk_xattn_ffn_d2_seqx_r4_0d2c97'

def setup_inputs(seed: int=0):
    np.random.seed(seed)
    _w = jnp.asarray

    def _rec_inputs():
        import jax
        import jax.numpy as jnp
        _rk = jax.random.key(seed)
        x = 7.22e-05 + 1 * jax.random.normal(jax.random.fold_in(_rk, 1), (4, 512, 256), jnp.float32)
        _lenS = 512 - jax.random.randint(jax.random.fold_in(_rk, 7), (4,), 0, max(1, 512 // 4) + 1, jnp.int32)
        _lenS2 = 1601 - jax.random.randint(jax.random.fold_in(_rk, 8), (4,), 0, max(1, 1601 // 4) + 1, jnp.int32)
        _ctx_768P = jax.random.normal(jax.random.fold_in(_rk, 11), (4, 16, 192), jnp.float32)
        _ctx_768c = jax.random.dirichlet(jax.random.fold_in(_rk, 511), 0.3 * jnp.ones((16,), jnp.float32), (4, 1601))
        _ctx_768t = jnp.einsum('bsk,bkd->bsd', _ctx_768c, _ctx_768P)
        _ctx_768t = _ctx_768t * jax.lax.rsqrt(jnp.mean(jnp.square(_ctx_768t)) + 1e-12) * 0.953939
        ctx_768 = -0.000191848 + 0.999787 * (_ctx_768t + 0.3 * jax.random.normal(jax.random.fold_in(_rk, 611), (4, 1601, 192), jnp.float32))
        _validS = jnp.arange(512)[None, :] < _lenS[:, None]
        _validS2 = jnp.arange(1601)[None, :] < _lenS2[:, None]
        _causal = jnp.tril(jnp.ones((512, 512), dtype=bool))
        mask_BxS_bf1 = jnp.ones((4, 512), dtype=bool)
        mask_BxS2_bf1 = jnp.ones((4, 1601), dtype=bool)
        return (x, ctx_768, mask_BxS_bf1, mask_BxS2_bf1)
    x, ctx_768, mask_BxS_bf1, mask_BxS2_bf1 = _rec_inputs()

    def _L0_xattn_setup():
        import jax, jax.numpy as jnp
        import numpy as np
        NUM_HEADS = 16
        CLAMP = 10000.0
        key = jax.random.key(seed)
        ks = jax.random.split(key, 8)
        B, Nq, Nkv, Cq, Ckv = (4, 512, 512, 256, 192)
        s_q = 1.0 / np.sqrt(Cq)
        s_kv = 1.0 / np.sqrt(Ckv)
        return {'query': jax.random.normal(ks[0], (B, Nq, Cq), jnp.float32), 'key_value': jax.random.normal(ks[1], (B, Nkv, Ckv), jnp.float32), 'Wq': jax.random.normal(ks[2], (Cq, Cq), jnp.float32) * s_q, 'bq': jnp.zeros((Cq,), jnp.float32), 'Wk': jax.random.normal(ks[3], (Ckv, Cq), jnp.float32) * s_kv, 'bk': jnp.zeros((Cq,), jnp.float32), 'Wv': jax.random.normal(ks[4], (Ckv, Cq), jnp.float32) * s_kv, 'bv': jnp.zeros((Cq,), jnp.float32), 'Wo': jax.random.normal(ks[5], (Cq, Cq), jnp.float32) * s_q, 'bo': jnp.zeros((Cq,), jnp.float32)}
    _L0_xattn_all = _L0_xattn_setup()
    _L0_xattn_in = {k: v for k, v in _L0_xattn_all.items() if k in ('Wq', 'bq', 'Wk', 'bk', 'Wv', 'bv', 'Wo', 'bo')}
    del _L0_xattn_all

    def _L0_ffn_setup():
        import jax, jax.numpy as jnp
        import numpy as np
        B, S, H, I, E, K = (2, 512, 256, 512, 8, 2)
        key = jax.random.key(seed)
        k1, k2, k3, k4, k5 = jax.random.split(key, 5)
        scale_h = 1.0 / np.sqrt(H)
        scale_i = 1.0 / np.sqrt(I)
        return {'x': jax.random.normal(k1, (B, S, H), dtype=jnp.float32), 'Wg': jax.random.normal(k2, (H, E), dtype=jnp.float32) * scale_h, 'W11': jax.random.normal(k3, (E, H, I), dtype=jnp.float32) * scale_h, 'W12': jax.random.normal(k4, (E, H, I), dtype=jnp.float32) * scale_h, 'W2': jax.random.normal(k5, (E, I, H), dtype=jnp.float32) * scale_i}
    _L0_ffn_all = _L0_ffn_setup()
    _L0_ffn_in = {k: v for k, v in _L0_ffn_all.items() if k in ('Wg', 'W11', 'W12', 'W2')}
    del _L0_ffn_all

    def _L1_xattn_setup():
        import jax, jax.numpy as jnp
        import numpy as np
        B, T, DT, G, DV = (16, 128, 256, 144, 192)
        H, DH = (4, 32)
        INNER = H * DH
        HID = 4 * DT
        N_STATE = 64
        K_TOP = 32

        def layernorm(x, g, b, eps=1e-05):
            m = x.mean(-1, keepdims=True)
            v = x.var(-1, keepdims=True)
            return (x - m) * jax.lax.rsqrt(v + eps) * g + b

        def s4d(x, log_dt, A_re, A_im, C_re, C_im, D_skip):
            Bb, L, D = x.shape
            dt = jnp.exp(log_dt)
            A = A_re + 1j * A_im
            C = C_re + 1j * C_im
            dtA = dt[:, None] * A
            dC = C * (jnp.exp(dtA) - 1.0) / A
            powers = jnp.exp(dtA[:, :, None] * jnp.arange(L))
            K = 2.0 * jnp.einsum('dn,dnl->dl', dC, powers).real
            n = 2 * L
            Kf = jnp.fft.rfft(K, n=n, axis=-1)
            xf = jnp.fft.rfft(x, n=n, axis=1)
            y = jnp.fft.irfft(xf * Kf.T[None], n=n, axis=1)[:, :L]
            return y + x * D_skip
        key = jax.random.key(seed)
        ks = jax.random.split(key, 16)
        s = 0.02
        inp = {'x_text': jax.random.normal(ks[0], (B, T, DT), jnp.float32), 'x_vision': jax.random.normal(ks[1], (B, G, DV), jnp.float32), 'text_mask': jnp.ones((B, T), bool), 'vision_mask': jnp.ones((B, G), bool), 'Wq': jax.random.normal(ks[2], (DT, INNER), jnp.float32) * s, 'Wk': jax.random.normal(ks[3], (DV, INNER), jnp.float32) * s, 'Wv': jax.random.normal(ks[4], (DV, DT), jnp.float32) * s, 'W_film_in': jax.random.normal(ks[5], (DT, 2 * DT), jnp.float32) * s, 'b_film_in': jnp.zeros((2 * DT,), jnp.float32), 'W_film_out': jax.random.normal(ks[6], (DT, 2 * DT), jnp.float32) * s, 'b_film_out': jnp.zeros((2 * DT,), jnp.float32), 'g_norm_in': jnp.ones((DT,), jnp.float32), 'b_norm_in': jnp.zeros((DT,), jnp.float32), 'g_norm_out': jnp.ones((DT,), jnp.float32), 'b_norm_out': jnp.zeros((DT,), jnp.float32), 'g_ffn': jnp.ones((DT,), jnp.float32), 'b_ffn': jnp.zeros((DT,), jnp.float32), 'W1': jax.random.normal(ks[7], (DT, HID), jnp.float32) * s, 'b1': jnp.zeros((HID,), jnp.float32), 'W2': jax.random.normal(ks[8], (HID, DT), jnp.float32) * s, 'b2': jnp.zeros((DT,), jnp.float32), 'log_dt': jnp.log(0.001) + jax.random.uniform(ks[9], (DT,), jnp.float32) * (jnp.log(0.1) - jnp.log(0.001)), 'A_re': -0.5 * jnp.ones((DT, N_STATE), jnp.float32), 'A_im': jnp.tile(jnp.pi * jnp.arange(N_STATE, dtype=jnp.float32), (DT, 1)), 'C_re': jax.random.normal(ks[10], (DT, N_STATE), jnp.float32) * 0.5 ** 0.5, 'C_im': jax.random.normal(ks[11], (DT, N_STATE), jnp.float32) * 0.5 ** 0.5, 'D_skip': jax.random.normal(ks[12], (DT,), jnp.float32), 'mod_gate': jnp.array(0.5, jnp.float32)}
        return inp
    _L1_xattn_all = _L1_xattn_setup()
    _L1_xattn_in = {k: v for k, v in _L1_xattn_all.items() if k in ('Wq', 'Wk', 'Wv', 'W_film_in', 'b_film_in', 'W_film_out', 'b_film_out', 'g_norm_in', 'b_norm_in', 'g_norm_out', 'b_norm_out', 'g_ffn', 'b_ffn', 'W1', 'b1', 'W2', 'b2', 'log_dt', 'A_re', 'A_im', 'C_re', 'C_im', 'D_skip', 'mod_gate')}
    del _L1_xattn_all

    def _L1_ffn_setup():
        import jax, jax.numpy as jnp
        import numpy as np
        B, T, DIM = (2, 512, 256)
        H, DH, E, K = (16, 64, 8, 2)
        key = jax.random.key(seed)
        ks = jax.random.split(key, 7)
        s = 0.02
        return {'x': jax.random.normal(ks[0], (B, T, DIM), jnp.float32), 'Wq': jax.random.normal(ks[1], (H, DH, DIM), jnp.float32) * s, 'Wk': jax.random.normal(ks[2], (H, DH, DIM), jnp.float32) * s, 'Wv': jax.random.normal(ks[3], (E, DH, DIM), jnp.float32) * s, 'Ws': jax.random.normal(ks[4], (H, E, DIM), jnp.float32) * s, 'Wd': jax.random.normal(ks[5], (H, E, DIM), jnp.float32) * s, 'Wo': jax.random.normal(ks[6], (E, DIM, DH), jnp.float32) * s}
    _L1_ffn_all = _L1_ffn_setup()
    _L1_ffn_in = {k: v for k, v in _L1_ffn_all.items() if k in ('Wq', 'Wk', 'Wv', 'Ws', 'Wd', 'Wo')}
    del _L1_ffn_all
    return {'x': x, 'ctx_768': ctx_768, 'mask_BxS_bf1': mask_BxS_bf1, 'mask_BxS2_bf1': mask_BxS2_bf1, 'L0_xattn_Wq': _L0_xattn_in['Wq'], 'L0_xattn_bq': _L0_xattn_in['bq'], 'L0_xattn_Wk': _L0_xattn_in['Wk'], 'L0_xattn_bk': _L0_xattn_in['bk'], 'L0_xattn_Wv': _L0_xattn_in['Wv'], 'L0_xattn_bv': _L0_xattn_in['bv'], 'L0_xattn_Wo': _L0_xattn_in['Wo'], 'L0_xattn_bo': _L0_xattn_in['bo'], 'L0_ffn_Wg': _L0_ffn_in['Wg'], 'L0_ffn_W11': _L0_ffn_in['W11'], 'L0_ffn_W12': _L0_ffn_in['W12'], 'L0_ffn_W2': _L0_ffn_in['W2'], 'L1_xattn_Wq': _L1_xattn_in['Wq'], 'L1_xattn_Wk': _L1_xattn_in['Wk'], 'L1_xattn_Wv': _L1_xattn_in['Wv'], 'L1_xattn_W_film_in': _L1_xattn_in['W_film_in'], 'L1_xattn_b_film_in': _L1_xattn_in['b_film_in'], 'L1_xattn_W_film_out': _L1_xattn_in['W_film_out'], 'L1_xattn_b_film_out': _L1_xattn_in['b_film_out'], 'L1_xattn_g_norm_in': _L1_xattn_in['g_norm_in'], 'L1_xattn_b_norm_in': _L1_xattn_in['b_norm_in'], 'L1_xattn_g_norm_out': _L1_xattn_in['g_norm_out'], 'L1_xattn_b_norm_out': _L1_xattn_in['b_norm_out'], 'L1_xattn_g_ffn': _L1_xattn_in['g_ffn'], 'L1_xattn_b_ffn': _L1_xattn_in['b_ffn'], 'L1_xattn_W1': _L1_xattn_in['W1'], 'L1_xattn_b1': _L1_xattn_in['b1'], 'L1_xattn_W2': _L1_xattn_in['W2'], 'L1_xattn_b2': _L1_xattn_in['b2'], 'L1_xattn_log_dt': _L1_xattn_in['log_dt'], 'L1_xattn_A_re': _L1_xattn_in['A_re'], 'L1_xattn_A_im': _L1_xattn_in['A_im'], 'L1_xattn_C_re': _L1_xattn_in['C_re'], 'L1_xattn_C_im': _L1_xattn_in['C_im'], 'L1_xattn_D_skip': _L1_xattn_in['D_skip'], 'L1_xattn_mod_gate': _L1_xattn_in['mod_gate'], 'L1_ffn_Wq': _L1_ffn_in['Wq'], 'L1_ffn_Wk': _L1_ffn_in['Wk'], 'L1_ffn_Wv': _L1_ffn_in['Wv'], 'L1_ffn_Ws': _L1_ffn_in['Ws'], 'L1_ffn_Wd': _L1_ffn_in['Wd'], 'L1_ffn_Wo': _L1_ffn_in['Wo']}

def reference(x, ctx_768, mask_BxS_bf1, mask_BxS2_bf1, L0_xattn_Wq, L0_xattn_bq, L0_xattn_Wk, L0_xattn_bk, L0_xattn_Wv, L0_xattn_bv, L0_xattn_Wo, L0_xattn_bo, L0_ffn_Wg, L0_ffn_W11, L0_ffn_W12, L0_ffn_W2, L1_xattn_Wq, L1_xattn_Wk, L1_xattn_Wv, L1_xattn_W_film_in, L1_xattn_b_film_in, L1_xattn_W_film_out, L1_xattn_b_film_out, L1_xattn_g_norm_in, L1_xattn_b_norm_in, L1_xattn_g_norm_out, L1_xattn_b_norm_out, L1_xattn_g_ffn, L1_xattn_b_ffn, L1_xattn_W1, L1_xattn_b1, L1_xattn_W2, L1_xattn_b2, L1_xattn_log_dt, L1_xattn_A_re, L1_xattn_A_im, L1_xattn_C_re, L1_xattn_C_im, L1_xattn_D_skip, L1_xattn_mod_gate, L1_ffn_Wq, L1_ffn_Wk, L1_ffn_Wv, L1_ffn_Ws, L1_ffn_Wd, L1_ffn_Wo):
    import jax
    import jax.numpy as jnp

    def _L0_xattn_ref(query, key_value, Wq, bq, Wk, bk, Wv, bv, Wo, bo):
        import jax, jax.numpy as jnp
        import numpy as np
        NUM_HEADS = 16
        CLAMP = 10000.0
        B, Nq, Cq = query.shape
        Nkv = key_value.shape[1]
        H = NUM_HEADS
        D = Cq // H
        scale = D ** (-0.5)
        q = (query @ Wq + bq).reshape(B, Nq, H, D).transpose(0, 2, 1, 3)
        k = (key_value @ Wk + bk).reshape(B, Nkv, H, D).transpose(0, 2, 1, 3)
        v = (key_value @ Wv + bv).reshape(B, Nkv, H, D).transpose(0, 2, 1, 3)
        attn = jnp.einsum('bhqd,bhkd->bhqk', q, k) * scale
        attn = jnp.clip(attn, -CLAMP, CLAMP)
        attn = jax.nn.softmax(attn, axis=-1)
        attn = jnp.where(jnp.any(jnp.isnan(attn)), jnp.asarray(1.0 / Nkv, attn.dtype), attn)
        x = jnp.einsum('bhqk,bhkd->bqhd', attn, v).reshape(B, Nq, Cq)
        return x @ Wo + bo

    def _L0_ffn_ref(x, Wg, W11, W12, W2):
        import jax, jax.numpy as jnp
        import numpy as np
        B, S, H, I, E, K = (2, 512, 256, 512, 8, 2)
        gate_scores = jax.nn.softmax(x @ Wg, axis=-1)
        topk_scores, topk_idx = jax.lax.top_k(gate_scores, K)
        topk_scores = topk_scores / (topk_scores.sum(-1, keepdims=True) + 1e-08)
        gate = jnp.einsum('bsh,ehi->bsei', x, W11)
        value = jnp.einsum('bsh,ehi->bsei', x, W12)
        fused = gate * jax.nn.sigmoid(gate) * value
        expert_out = jnp.einsum('bsei,eih->bseh', fused, W2)
        gathered = jnp.take_along_axis(expert_out, topk_idx[..., None], axis=2)
        out = jnp.sum(topk_scores[..., None] * gathered, axis=2)
        return out

    def _L1_xattn_ref(x_text, x_vision, text_mask, vision_mask, Wq, Wk, Wv, W_film_in, b_film_in, W_film_out, b_film_out, g_norm_in, b_norm_in, g_norm_out, b_norm_out, g_ffn, b_ffn, W1, b1, W2, b2, log_dt, A_re, A_im, C_re, C_im, D_skip, mod_gate):
        import jax, jax.numpy as jnp
        import numpy as np
        B, T, DT, G, DV = (16, 128, 256, 144, 192)
        H, DH = (4, 32)
        INNER = H * DH
        HID = 4 * DT
        N_STATE = 64
        K_TOP = 32

        def layernorm(x, g, b, eps=1e-05):
            m = x.mean(-1, keepdims=True)
            v = x.var(-1, keepdims=True)
            return (x - m) * jax.lax.rsqrt(v + eps) * g + b

        def s4d(x, log_dt, A_re, A_im, C_re, C_im, D_skip):
            Bb, L, D = x.shape
            dt = jnp.exp(log_dt)
            A = A_re + 1j * A_im
            C = C_re + 1j * C_im
            dtA = dt[:, None] * A
            dC = C * (jnp.exp(dtA) - 1.0) / A
            powers = jnp.exp(dtA[:, :, None] * jnp.arange(L))
            K = 2.0 * jnp.einsum('dn,dnl->dl', dC, powers).real
            n = 2 * L
            Kf = jnp.fft.rfft(K, n=n, axis=-1)
            xf = jnp.fft.rfft(x, n=n, axis=1)
            y = jnp.fft.irfft(xf * Kf.T[None], n=n, axis=1)[:, :L]
            return y + x * D_skip
        Bb, Tt, D = x_text.shape
        Gg = x_vision.shape[1]
        Q = (x_text @ Wq).reshape(Bb, Tt, H, DH)
        K = (x_vision @ Wk).reshape(Bb, Gg, H, DH)
        scores = jnp.einsum('bthd,bghd->bhtg', Q, K) / np.sqrt(DH).astype(np.float32)
        scores = jnp.where(vision_mask[:, None, None, :], scores, -jnp.inf)
        topv, topi = jax.lax.top_k(scores, K_TOP)
        probs = jax.nn.softmax(topv, axis=-1)
        bi = jnp.arange(Bb)[:, None, None, None]
        hi = jnp.arange(H)[None, :, None, None]
        ti = jnp.arange(Tt)[None, None, :, None]
        attn = jnp.zeros_like(scores).at[bi, hi, ti, topi].set(probs)
        attn_mean = attn.mean(axis=1)
        V = x_vision @ Wv
        c_t = jnp.einsum('btg,bgd->btd', attn_mean, V)
        c_t = c_t * text_mask[..., None]
        x = layernorm(x_text, g_norm_in, b_norm_in)
        scale_in, shift_in = jnp.split(c_t @ W_film_in + b_film_in, 2, axis=-1)
        x = x * (1.0 + mod_gate * scale_in) + mod_gate * shift_in
        y = s4d(x, log_dt, A_re, A_im, C_re, C_im, D_skip)
        scale_out, shift_out = jnp.split(c_t @ W_film_out + b_film_out, 2, axis=-1)
        y = y * (1.0 + mod_gate * scale_out) + mod_gate * shift_out
        xt = x_text + y
        h = layernorm(xt, g_ffn, b_ffn)
        h = jax.nn.gelu(h @ W1 + b1, approximate=False) @ W2 + b2
        xt = xt + h
        return layernorm(xt, g_norm_out, b_norm_out)

    def _L1_ffn_ref(x, Wq, Wk, Wv, Ws, Wd, Wo):
        import jax, jax.numpy as jnp
        import numpy as np
        B, T, DIM = (2, 512, 256)
        H, DH, E, K = (16, 64, 8, 2)
        scale = DH ** (-0.5)
        q = jnp.einsum('btc,hdc->bhtd', x, Wq)
        k = jnp.einsum('btc,hdc->bhtd', x, Wk)
        gate_v = jnp.einsum('btc,hec->bthe', x, Ws)
        w, sel = jax.lax.top_k(gate_v, K)
        wsig = jax.nn.sigmoid(w)
        oh = jax.nn.one_hot(sel, E, dtype=x.dtype)
        mix_v = jnp.einsum('bthk,bthke->bthe', wsig, oh)
        proj_v = jnp.einsum('btc,edc->bted', x, Wv)
        v = jnp.einsum('bthe,bted->bhtd', mix_v, proj_v)
        scores = jnp.einsum('bhid,bhjd->bhij', q * scale, k)
        probs = jax.nn.softmax(scores, axis=-1)
        attn = jnp.einsum('bhij,bhjd->bihd', probs, v)
        gate_o = jnp.einsum('btc,hec->bthe', x, Wd)
        _, sel_o = jax.lax.top_k(gate_o, K)
        mask_o = jax.nn.one_hot(sel_o, E, dtype=x.dtype).sum(axis=3)
        res = jnp.einsum('bthe,bthd,efd->bthf', mask_o, attn, Wo)
        return res.sum(axis=2)
    x = x + _L0_xattn_ref(_layernorm(x, axis=-1), ctx_768, L0_xattn_Wq, L0_xattn_bq, L0_xattn_Wk, L0_xattn_bk, L0_xattn_Wv, L0_xattn_bv, L0_xattn_Wo, L0_xattn_bo)
    x = x + _L0_ffn_ref(_layernorm(x, axis=-1), L0_ffn_Wg, L0_ffn_W11, L0_ffn_W12, L0_ffn_W2)
    x = x + _L1_xattn_ref(_layernorm(x, axis=-1), ctx_768, mask_BxS_bf1, mask_BxS2_bf1, L1_xattn_Wq, L1_xattn_Wk, L1_xattn_Wv, L1_xattn_W_film_in, L1_xattn_b_film_in, L1_xattn_W_film_out, L1_xattn_b_film_out, L1_xattn_g_norm_in, L1_xattn_b_norm_in, L1_xattn_g_norm_out, L1_xattn_b_norm_out, L1_xattn_g_ffn, L1_xattn_b_ffn, L1_xattn_W1, L1_xattn_b1, L1_xattn_W2, L1_xattn_b2, L1_xattn_log_dt, L1_xattn_A_re, L1_xattn_A_im, L1_xattn_C_re, L1_xattn_C_im, L1_xattn_D_skip, L1_xattn_mod_gate)
    x = x + _L1_ffn_ref(_layernorm(x, axis=-1), L1_ffn_Wq, L1_ffn_Wk, L1_ffn_Wv, L1_ffn_Ws, L1_ffn_Wd, L1_ffn_Wo)
    return x

_drawn_inputs = setup_inputs


def setup_inputs(seed=0):
    import zlib

    import numpy as np

    out = dict(_drawn_inputs(seed))
    spreads = {'L0_xattn_bq': (0.0, 0.1),
     'L0_xattn_bk': (0.0, 0.8),
     'L0_xattn_bv': (0.0, 0.1),
     'L0_xattn_bo': (0.0, 0.1),
     'L1_xattn_b_film_in': (0.0, 0.1),
     'L1_xattn_b_film_out': (0.0, 0.318),
     'L1_xattn_g_norm_in': (1.0, 0.2),
     'L1_xattn_b_norm_in': (0.0, 0.1),
     'L1_xattn_g_norm_out': (1.0, 0.2),
     'L1_xattn_b_norm_out': (0.0, 0.1),
     'L1_xattn_g_ffn': (1.0, 0.6),
     'L1_xattn_b_ffn': (0.0, 0.8),
     'L1_xattn_b1': (0.0, 0.798),
     'L1_xattn_b2': (0.0, 0.282),
     'L1_xattn_A_re': (-0.5, 0.2)}
    factors = {'L1_xattn_Wq': 5.038,
     'L1_xattn_Wk': 5.081,
     'L1_xattn_W_film_in': 3.212,
     'L1_xattn_W_film_out': 4.293,
     'L1_ffn_Wq': 8.0,
     'L1_ffn_Wk': 8.0,
     'L1_ffn_Ws': 3.952}
    for name, (base, spread) in spreads.items():
        noise = np.random.default_rng([zlib.crc32(name.encode()), seed]).standard_normal(out[name].shape)
        drawn = base * np.exp(spread * noise) if base else spread * noise
        out[name] = jnp.asarray(drawn.astype(out[name].dtype))
    for name, factor in factors.items():
        out[name] = (out[name] * factor).astype(out[name].dtype)
    return out
```

```python
from contextlib import ExitStack

import numpy as np

import concourse.bass as bass
from concourse import mybir

F32 = mybir.dt.float32
BF16 = mybir.dt.bfloat16
U8 = mybir.dt.uint8
ALU = mybir.AluOpType
ACT = mybir.ActivationFunctionType
AX = mybir.AxisListType

P = 128
NBATCH, SEQ, DIM = 4, 512, 256
TILES = SEQ // P
DCH = DIM // P
GKEYS, DCTX = 1601, 192
CTXP, CTXCH = 96, 2
KCH = (GKEYS + P - 1) // P
KW = [min(P, GKEYS - P * k) for k in range(KCH)]
COLS = [(c, min(512, GKEYS - c)) for c in range(0, GKEYS, 512)]
H0, D0 = 16, 16
V0W = 32
CLAMP = 10000.0
SPLIT_Q = [0, 0, 1, 0, 2, 1]
SPLIT_K = [0, 1, 0, 2, 0, 1]
NSPLIT = len(SPLIT_Q) * D0
NEXP, INNER = 8, 512
ICH = INNER // P
H1, D1, TOPK = 4, 32, 32
DROPPED = -3.4e38
MASKED = 3.0e38
NSTATE = 64
LB, LA = 32, 16
FCH = 2 * SEQ // P
HID = 4 * DIM
HCH = HID // P
H2, D2, E2 = 16, 64, 8
TWO_ONES = float(np.array(0x3F803F80, np.uint32).view(np.float32))
MAGIC = 12582912.0
TWO_PI = 6.283185307179586
LN_EPS = 1e-5
ARENA = 34912


def program(nc, a, dbg=None):
    ctx = ExitStack()
    with ctx:
        def sb(name, shape, dt=F32):
            return ctx.enter_context(nc.sbuf_tensor("sb_" + name, shape, dt))

        sems = []

        def sem(name):
            s = ctx.enter_context(nc.semaphore(name))
            sems.append(s)
            return s

        x = sb("x", [P, TILES, DIM])
        xt = sb("xt", [P, TILES, DIM])
        xn = sb("xn", [P, TILES, DIM])
        xnT = sb("xnT", [P, DCH, SEQ])
        key_bias = sb("key_bias", [P, GKEYS])
        wq0 = sb("wq0", [P, DCH, DIM])
        wk0 = sb("wk0", [CTXP, CTXCH, DIM])
        wv0 = sb("wv0", [CTXP, CTXCH, H0 * V0W])
        wo0 = sb("wo0", [P, DCH, DIM])
        bv0 = sb("bv0", [P, H0 * V0W])
        bo0 = sb("bo0", [P, DIM])
        bq0 = sb("bq0", [P, DCH])
        bk0 = sb("bk0", [P, DCH])
        wg = sb("wg", [P, DCH, NEXP])
        wq1 = sb("wq1", [P, DCH, H1 * D1])
        wk1 = sb("wk1", [CTXP, CTXCH, H1 * D1])
        wv1 = sb("wv1", [CTXP, CTXCH, DIM])
        film_w = sb("film_w", [P, 2, DCH, 2 * DIM])
        film_b = sb("film_b", [P, 2, 2 * DIM])
        norm_g = sb("norm_g", [P, 3, DIM])
        norm_b = sb("norm_b", [P, 3, DIM])
        b1 = sb("b1", [P, HCH])
        b2 = sb("b2", [P, DIM])
        d_skip = sb("d_skip", [P, DIM])
        mod_gate = sb("mod_gate", [P, 1])
        k_cos = sb("k_cos", [P, FCH // 2, DIM])
        k_sin = sb("k_sin", [P, FCH // 2, DIM])
        k_cos0 = sb("k_cos0", [P, DIM])
        ident = sb("ident", [P, P])
        fold = sb("fold", [P, V0W])
        max_rows = sb("max_rows", [P, P], BF16)
        prio = sb("prio", [P, NEXP])
        phase = sb("phase", [P, 4])
        eps = sb("eps", [P, 1])
        ln_stats = sb("ln_stats", [P, TILES, 6])
        ln_mv = sb("ln_mv", [P, TILES, 2])
        ln_std = sb("ln_std", [P, TILES])
        ln_rstd = sb("ln_rstd", [P, TILES])
        tmask = sb("tmask", [P, TILES])
        tmask8 = sb("tmask8", [P, TILES], U8)
        small = sb("small", [P, 256])

        arena = sb("arena", [P, ARENA])

        def at(off, shape, dt=F32):
            n = int(np.prod(shape))
            words = n if dt == F32 else (n + 1) // 2 if dt == BF16 else (n + 3) // 4
            v = arena[:, off:off + words]
            if dt != F32:
                v = v.bitcast(dt)[:, 0:n]
            if len(shape) == 2:
                v = v.rearrange("p (a b) -> p a b", b=shape[1])
            elif len(shape) == 3:
                v = v.rearrange("p (a b c) -> p a b c", b=shape[1], c=shape[2])
            return v

        ps = ctx.enter_context(nc.psum_tensor("ps", [P, 8, 512], F32))

        def wide(bank, n):
            return ps[:, bank:bank + (n + 511) // 512, :].rearrange("p a b -> p (a b)")[:, 0:n]

        ctxT = at(0, [CTXCH, GKEYS])
        KPAD = 2 * ((GKEYS + 1) // 2)
        o = 3204
        k_stack = at(o, [H0, KPAD], BF16); o += H0 * KPAD // 2
        q_stack = at(o, [H0, SEQ], BF16); o += H0 * SEQ // 2
        o_tr = o
        v0 = at(o, [KCH, H0 * V0W]); o += KCH * H0 * V0W
        probs0 = at(o, [4, SEQ]); o += 4 * SEQ
        o_part = at(o, [2, SEQ]); o += 2 * SEQ
        low = at(o, [2, SEQ]); o += 2 * SEQ
        nm_f = at(o, [SEQ]); o += SEQ
        nm_r = at(o, [SEQ]); o += SEQ
        nm_p = at(o, [3, SEQ], BF16); o += 3 * SEQ // 2
        attn0 = at(o, [TILES, DIM]); o += TILES * DIM
        row_max = at(o, [TILES, H0]); o += TILES * H0
        neg_max = at(o, [TILES, H0]); o += TILES * H0
        assert o <= ARENA
        o = o_tr
        k_f = at(o, [DCH, GKEYS]); o += DCH * GKEYS
        k_r = at(o, [DCH, GKEYS]); o += DCH * GKEYS
        k_p = at(o, [3, DCH, KPAD], BF16); o += 3 * DCH * KPAD // 2
        q_f = at(o, [DCH, SEQ]); o += DCH * SEQ
        q_r = at(o, [DCH, SEQ]); o += DCH * SEQ
        q_p = at(o, [3, DCH, SEQ], BF16); o += 3 * DCH * SEQ // 2
        assert o <= ARENA
        o = 3204
        w_exp = [at(o + 3072 * i, [3072]) for i in range(2)]; o += 2 * 3072
        w11 = [w[:, 0:1024].rearrange("p (c i) -> p c i", c=DCH) for w in w_exp]
        w12 = [w[:, 1024:2048].rearrange("p (c i) -> p c i", c=DCH) for w in w_exp]
        w2e = [w[:, 2048:3072].rearrange("p (c d) -> p c d", c=ICH) for w in w_exp]
        silu = at(o, [2, SEQ]); o += 2 * SEQ
        fused = at(o, [2, ICH * SEQ]); o += 2 * ICH * SEQ
        gl = at(o, [TILES, NEXP]); o += 32
        g_tmp = [at(o + 32 * i, [TILES, NEXP]) for i in range(6)]; o += 32 * 6
        g_red = [at(o + 8 * i, [TILES]) for i in range(6)]; o += 48
        g_w = at(o, [TILES, NEXP]); o += 32
        o = 3204
        KS = 1602
        s_sb = at(o, [2, KS]); o += 2 * KS
        s_cut = at(o, [2, KS]); o += 2 * KS
        probs1 = at(o, [H1, KS]); o += H1 * KS
        attnT = at(o, [KCH, SEQ]); o += KCH * SEQ
        kT1 = at(o, [GKEYS]); o += KS
        v1 = at(o, [KCH, DIM]); o += KCH * DIM
        q1z = at(o, [H1, SEQ]); o += H1 * SEQ
        scaled_eye = at(o, [H1, P]); o += H1 * P
        top = at(o, [2, TOPK]); o += 2 * TOPK
        top_e = at(o, [2, TOPK]); o += 2 * TOPK
        stat1 = at(o, [2, 8]); o += 16
        mask8 = at(o, [GKEYS], U8); o += 402
        c_tT = at(ARENA - 1024, [DCH, SEQ])
        assert o <= ARENA - 1024
        o = 0
        dft = at(o, [SEQ // P, 2 * SEQ]); o += SEQ // P * 2 * SEQ
        idft = at(o, [FCH, SEQ]); o += FCH * SEQ
        u = at(o, [TILES, DIM]); o += TILES * DIM
        f_in = at(o, [TILES, 2 * DIM]); f_out = at(o + 2048, [TILES, 2 * DIM]); o += 4096
        spec = at(o, [FCH, DIM]); o += FCH * DIM
        ptmp = at(o, [2, 4, DIM]); o += 8 * DIM
        dtmp = at(o, [TILES, DIM]); o += TILES * DIM
        wf1 = at(o, [DCH, HID]); o += DCH * HID
        wf2 = at(o, [HCH, DIM]); o += HCH * DIM
        assert o <= ARENA - 1024 - 6656
        hid = at(0, [HCH, SEQ])
        o = ARENA - 1024 - 6656
        wq2 = at(o, [DCH, H2 * D2]); o += DCH * H2 * D2
        wk2 = at(o, [DCH, H2 * D2]); o += DCH * H2 * D2
        wsd = at(o, [DCH, 2 * H2 * E2]); o += DCH * 2 * H2 * E2
        wv2 = at(o, [DCH, E2 * D2]); o += DCH * E2 * D2
        wo2 = at(o, [E2 * D2 // P, DIM]); o += E2 * D2 // P * DIM
        z = at(o, [E2 * D2]); o += 512
        z_tmp = at(o, [E2 * D2]); o += 512
        assert o == ARENA
        o = 0
        q2z = at(o, [H2, SEQ]); o += H2 * SEQ
        kT2 = at(o, [H2 // 2, SEQ]); o += H2 // 2 * SEQ
        proj_v = at(o, [TILES, E2 * D2]); o += TILES * E2 * D2
        v2 = at(o, [TILES, H2 * D2]); o += TILES * H2 * D2
        NG = TILES * H2
        gate_v = at(o, [NG, E2]); o += NG * E2
        gate_o = at(o, [NG, E2]); o += NG * E2
        sig_v = at(o, [NG, E2]); o += NG * E2
        t_oh1 = at(o, [NG, E2]); o += NG * E2
        t_oh2 = at(o, [NG, E2]); o += NG * E2
        t_a = at(o, [NG, E2]); o += NG * E2
        t_b = at(o, [NG, E2]); o += NG * E2
        t_m = at(o, [NG]); o += NG
        sums2 = at(o, [TILES, H2]); o += NG
        rs2 = at(o, [TILES, H2]); o += NG
        nmax2 = at(o, [TILES, H2]); o += NG
        p2 = at(o, [2, SEQ]); o += 2 * SEQ
        pT2 = at(o, [2, SEQ]); o += 2 * SEQ
        zT = at(o, [E2 * D2]); o += 512
        v_tmp = at(o, [H2 * D2]); o += H2 * D2
        v_tmp2 = at(o, [H2 * D2]); o += H2 * D2
        assert o <= ARENA - 1024 - 6656, o
        o = 0
        NW, NPW = DIM * LB, DIM * LA
        k_w = at(o, [DIM, LB]); o += NW
        s_n = at(o, [NW]); o += NW
        s_x = at(o, [NPW]); o += NPW
        s_y = at(o, [NPW]); o += NPW
        s_t = [at(o + DIM * i, [DIM]) for i in range(18)]; o += 18 * DIM
        ramp = at(o, [LB + LA]); o += LB + LA
        k_time = at(o, [SEQ // P, DIM]); o += SEQ // P * DIM
        dft_s = at(o, [SEQ // P, 2 * SEQ]); o += SEQ // P * 2 * SEQ
        assert o <= ARENA
        k_spill = nc.dram_tensor("k_spill", [3, DIM, GKEYS], BF16).ap()
        q_spill = nc.dram_tensor("q_spill", [3, DIM, SEQ], BF16).ap()

        consts = ctx.enter_context(nc.semaphore("consts"))
        setup_v = ctx.enter_context(nc.semaphore("setup_v"))
        setup_a = ctx.enter_context(nc.semaphore("setup_a"))
        setup_p = ctx.enter_context(nc.semaphore("setup_p"))
        setup_done = ctx.enter_context(nc.semaphore("setup_done"))
        engine_ended = ctx.enter_context(nc.semaphore("engine_ended"))
        batch_closed = ctx.enter_context(nc.semaphore("batch_closed"))
        batch_opened = ctx.enter_context(nc.semaphore("batch_opened"))
        loaded = sem("loaded")
        pads_ready = sem("pads_ready")
        v_step = sem("v_step")
        ln_var = sem("ln_var")
        ln_dev = sem("ln_dev")
        xn_ready = sem("xn_ready")
        xT_done = sem("xT_done")
        xT_ready = sem("xT_ready")
        k0_done = sem("k0_done")
        k0_ready = sem("k0_ready")
        k_parts = sem("k_parts")
        k_spilled = sem("k_spilled")
        k_stacked = sem("k_stacked")
        q0_done = sem("q0_done")
        q0_ready = sem("q0_ready")
        q_parts = sem("q_parts")
        q_spilled = sem("q_spilled")
        q_stacked = sem("q_stacked")
        v0_done = sem("v0_done")
        v0_ready = sem("v0_ready")
        s0_ready = sem("s0_ready")
        s0_read = sem("s0_read")
        nmax_ready = sem("nmax_ready")
        nmaxT_done = sem("nmaxT_done")
        nmax_parts = sem("nmax_parts")
        nmax_stacked = sem("nmax_stacked")
        low_done = sem("low_done")
        low_ready = sem("low_ready")
        t0_ready = sem("t0_ready")
        t0_clipped = sem("t0_clipped")
        p0_ready = sem("p0_ready")
        pv0_done = sem("pv0_done")
        o0_ready = sem("o0_ready")
        o0_turned = sem("o0_turned")
        attn0_ready = sem("attn0_ready")
        y0_done = sem("y0_done")
        x1_ready = sem("x1_ready")
        gl_done = sem("gl_done")
        gl_ready = sem("gl_ready")
        g_exp = sem("g_exp")
        w_loaded = [sem("w_loaded0"), sem("w_loaded1")]
        gv_done = sem("gv_done")
        silu_ready = sem("silu_ready")
        fused_ready = sem("fused_ready")
        down_done = sem("down_done")
        down_read = sem("down_read")
        c_done = sem("c_done")
        c_ready = sem("c_ready")
        q1_clear = sem("q1_clear")
        q1_done = sem("q1_done")
        q1_ready = sem("q1_ready")
        s1_done = sem("s1_done")
        s1_ready = sem("s1_ready")
        top_ready = sem("top_ready")
        e1_ready = sem("e1_ready")
        sum1_ready = sem("sum1_ready")
        p1_ready = sem("p1_ready")
        eye_ready = sem("eye_ready")
        aT_done = sem("aT_done")
        aT_ready = sem("aT_ready")
        ctx_done = sem("ctx_done")
        ctx_ready = sem("ctx_ready")
        w_late = sem("w_late")
        film_done = sem("film_done")
        film_read = sem("film_read")
        u_ready = sem("u_ready")
        spec_done = sem("spec_done")
        spec_ready = sem("spec_ready")
        y1_done = sem("y1_done")
        xt2_ready = sem("xt2_ready")
        h_done = sem("h_done")
        h_ready = sem("h_ready")
        f_done = sem("f_done")
        f_read = sem("f_read")
        x3_ready = sem("x3_ready")
        q2_clear = sem("q2_clear")
        qk2_done = sem("qk2_done")
        qk2_ready = sem("qk2_ready")
        g2_done = sem("g2_done")
        g2_read = sem("g2_read")
        sig_ready = sem("sig_ready")
        pv_done = sem("pv_done")
        pv_ready = sem("pv_ready")
        mix_ready = sem("mix_ready")
        v2_ready = sem("v2_ready")
        v2_ready_p = sem("v2_ready_p")
        p_step = sem("p_step")
        s2_done = sem("s2_done")
        s2_max = sem("s2_max")
        p2_ready = sem("p2_ready")
        p2T_done = sem("p2T_done")
        p2T_act = sem("p2T_act")
        p2T_dve = sem("p2T_dve")
        o2_done = sem("o2_done")
        z_ready = sem("z_ready")
        zT_done = sem("zT_done")
        zT_ready = sem("zT_ready")
        r_done = sem("r_done")
        out_ready = sem("out_ready")
        stored = sem("stored")

        NLOADS = []

        block = ctx.enter_context(nc.Block())

        @block.sync
        def _(sp):
            def const(dst, src):
                sp.dma_start(dst, src).then_inc(consts, 16)
                NLOADS.append(1)

            def bcast(dst, src):
                const(dst, src.partition_broadcast(P))

            for i, name in enumerate(["A_re", "A_im", "C_re", "C_im"]):
                for half in range(2):
                    const(s_t[i][half * NSTATE:(half + 1) * NSTATE, :], a["s4d"][i])
            bcast(s_t[4][:, :], a["log_dt"])
            bcast(ramp[:, :], a["ramp"])
            const(phase[:, :], a["phase"])
            const(dft_s[:, :, :], a["dft"].rearrange("(c p) f -> p c f", p=P))
            const(ident[:, :], a["ident"])
            const(fold[:, :], a["fold"])
            const(max_rows[:, :].bitcast(mybir.dt.uint16), a["max_rows"])
            bcast(prio[:, :], a["prio"])
            const(wq0[:, :, :], a["wq0"].rearrange("(c p) n -> p c n", p=P))
            const(wk0[:, :, :], a["wk0"].rearrange("(c p) n -> p c n", p=CTXP))
            const(wv0[:, :, :], a["wv0"].rearrange("(c p) n -> p c n", p=CTXP))
            const(wo0[:, :, :], a["wo0"].rearrange("(c p) n -> p c n", p=P))
            bcast(bv0[:, :], a["bv0"])
            bcast(bo0[:, :], a["bo0"])
            const(bq0[:, :], a["bq0"])
            const(bk0[:, :], a["bk0"])
            const(wg[:, :, :], a["wg"].rearrange("(c p) n -> p c n", p=P))
            const(wq1[:, :, :], a["wq1"].rearrange("(c p) n -> p c n", p=P))
            const(wk1[:, :, :], a["wk1"].rearrange("(c p) n -> p c n", p=CTXP))
            const(wv1[:, :, :], a["wv1"].rearrange("(c p) n -> p c n", p=CTXP))
            for i in range(2):
                const(film_w[:, i, :, :], a["film_w"][i].rearrange("(c p) n -> p c n", p=P))
                bcast(film_b[:, i, :], a["film_b"][i])
            for i in range(3):
                bcast(norm_g[:, i, :], a["norm_g"][i])
                bcast(norm_b[:, i, :], a["norm_b"][i])
            const(b1[:, :], a["b1"])
            bcast(b2[:, :], a["b2"])
            bcast(d_skip[:, :], a["d_skip"])
            bcast(mod_gate[:, :], a["mod_gate"])
            sp.wait_ge(setup_done, 1)

            with sp.Fori(0, NBATCH) as b:
                sp.dma_start(x[:, :, :], a["x"][b].rearrange("(t p) d -> p t d", p=P)).then_inc(loaded, 16)
                sp.dma_start(ctxT[0:CTXP, :, :], a["ctxT"][b].rearrange("(c p) k -> p c k", p=CTXP)).then_inc(loaded, 16)
                sp.dma_start(tmask8[:, :], a["tmask"][b].rearrange("p t -> p t")).then_inc(loaded, 16)

                sp.wait_ge(k_parts, DCH)
                for i in range(3):
                    sp.dma_start(k_spill[i].rearrange("(c p) k -> p c k", p=P), k_p[:, i, :, 0:GKEYS]).then_inc(k_spilled, 16)
                sp.wait_ge(k_spilled, 48)
                for i, part in enumerate(SPLIT_K):
                    sp.dma_start(k_stack[i * D0:(i + 1) * D0, :, 0:GKEYS],
                                 k_spill[part].rearrange("(h d) k -> d h k", d=D0)).then_inc(k_stacked, 16)
                sp.wait_ge(q_parts, 1)
                for i in range(3):
                    sp.dma_start(q_spill[i].rearrange("(c p) k -> p c k", p=P), q_p[:, i, :, :]).then_inc(q_spilled, 16)
                sp.wait_ge(q_spilled, 48)
                for i, part in enumerate(SPLIT_Q):
                    sp.dma_start(q_stack[i * D0:(i + 1) * D0, :, :],
                                 q_spill[part].rearrange("(h d) k -> d h k", d=D0)).then_inc(q_stacked, 16)
                sp.wait_ge(pads_ready, 3)
                sp.wait_ge(nmax_parts, 1)
                for i in range(3):
                    sp.dma_start(q_stack[NSPLIT + i:NSPLIT + i + 1, :, :], nm_p[0:H0, i, :]).then_inc(nmax_stacked, 16)

                for e in range(NEXP):
                    if e == 0:
                        sp.wait_ge(pv0_done, H0 * KCH)
                    if e >= 2:
                        sp.wait_ge(down_done, TILES * (e - 1))
                    sp.dma_start(w11[e % 2], a["w11"][e].rearrange("(c p) n -> p c n", p=P)).then_inc(w_loaded[e % 2], 16)
                    sp.dma_start(w12[e % 2], a["w12"][e].rearrange("(c p) n -> p c n", p=P)).then_inc(w_loaded[e % 2], 16)
                    sp.dma_start(w2e[e % 2], a["w2e"][e].rearrange("(c p) n -> p c n", p=P)).then_inc(w_loaded[e % 2], 16)

                sp.wait_ge(down_done, TILES * NEXP)
                sp.wait_ge(fused_ready, ICH * NEXP)
                sp.dma_start(mask8[:, :], a["vmask"][b].partition_broadcast(P)).then_inc(loaded, 16)
                sp.wait_ge(ctx_done, DCH)
                sp.wait_ge(aT_ready, 4 * TILES)
                sp.dma_start(dft[:, :, :], a["dft"].rearrange("(c p) f -> p c f", p=P)).then_inc(w_late, 16)
                sp.dma_start(idft[:, :, :], a["idft"].rearrange("(c p) f -> p c f", p=P)).then_inc(w_late, 16)
                sp.dma_start(wf1[:, :, :], a["wf1"].rearrange("(c p) f -> p c f", p=P)).then_inc(w_late, 16)
                sp.dma_start(wf2[:, :, :], a["wf2"].rearrange("(c p) f -> p c f", p=P)).then_inc(w_late, 16)
                sp.dma_start(wq2[:, :, :], a["wq2"].rearrange("(c p) f -> p c f", p=P)).then_inc(w_late, 16)
                sp.dma_start(wk2[:, :, :], a["wk2"].rearrange("(c p) f -> p c f", p=P)).then_inc(w_late, 16)
                sp.dma_start(wsd[:, :, :], a["wsd"].rearrange("(c p) f -> p c f", p=P)).then_inc(w_late, 16)
                sp.dma_start(wv2[:, :, :], a["wv2"].rearrange("(c p) f -> p c f", p=P)).then_inc(w_late, 16)
                sp.dma_start(wo2[:, :, :], a["wo2"].rearrange("(c p) f -> p c f", p=P)).then_inc(w_late, 16)

                for t in range(TILES):
                    sp.wait_ge(out_ready, t + 1)
                    sp.dma_start(a["out"][b].rearrange("(t p) d -> p t d", p=P)[:, t, :], x[:, t, :]).then_inc(stored, 16)
                if dbg is not None:
                    pass
                sp.wait_ge(stored, 16 * TILES)

                sp.wait_ge(engine_ended, 4 * b + 4)
                sp.sem_inc(batch_closed, 1)
                for s in sems:
                    sp.sem_clear(s)
                sp.sem_inc(batch_opened, 1)

        def end_of_batch(eng, b):
            eng.drain().then_inc(engine_ended, 1)
            eng.wait_ge(batch_opened, b + 1)

        def as_words(v):
            return v.rearrange("p a b -> p (a b)").bitcast(F32)

        @block.gpsimd
        def _(pool):
            pool.wait_ge(setup_done, 1)
            with pool.Fori(0, NBATCH) as b:
                nc.gpsimd.memset(as_words(q_stack[NSPLIT:P, :, :]), 0.0).then_inc(pads_ready, 1)
                nc.gpsimd.memset(as_words(k_stack[NSPLIT:P, :, :]), 0.0).then_inc(pads_ready, 1)
                pool.wait_ge(pads_ready, 2)
                nc.gpsimd.memset(as_words(k_stack[NSPLIT:NSPLIT + 3, :, :]), TWO_ONES).then_inc(pads_ready, 1)
                pool.wait_ge(down_read, TILES * NEXP)
                pool.wait_ge(fused_ready, ICH * NEXP)
                nc.gpsimd.memset(q1z[:, :, :], 0.0).then_inc(q1_clear, 1)
                for n in range(TILES * H1):
                    h = n % H1
                    pool.wait_ge(e1_ready, 2 * n + 2)
                    nc.gpsimd.tensor_tensor(probs1[:, h, 0:GKEYS], probs1[:, h, 0:GKEYS], s_cut[:, n % 2, 0:GKEYS],
                                            ALU.subtract).then_inc(p1_ready, 1)
                pool.wait_ge(f_done, TILES)
                nc.gpsimd.memset(q2z[0:D2, 1:H2:2, :], 0.0).then_inc(q2_clear, 1)
                nc.gpsimd.memset(q2z[D2:P, 0:H2:2, :], 0.0).then_inc(q2_clear, 1)
                pool.wait_ge(mix_ready, 1)
                pool.wait_ge(pv_ready, TILES)
                t = TILES - 1
                k = 0
                for e in range(E2):
                    src = proj_v[:, t, e * D2:(e + 1) * D2].unsqueeze(1).to_broadcast([P, H2, D2])
                    mix = t_b[:, t * H2:(t + 1) * H2, e].unsqueeze(2).to_broadcast([P, H2, D2])
                    dst = v2[:, t, :] if e == 0 else v_tmp2
                    nc.gpsimd.tensor_tensor(dst.rearrange("p (h d) -> p h d", d=D2), src, mix, ALU.mult).then_inc(p_step, 1)
                    k += 1
                    pool.wait_ge(p_step, k)
                    if e:
                        nc.gpsimd.tensor_tensor(v2[:, t, :], v2[:, t, :], v_tmp2, ALU.add).then_inc(p_step, 1)
                        k += 1
                        pool.wait_ge(p_step, k)
                pool.drain().then_inc(v2_ready_p, 1)
                end_of_batch(pool, b)

        def attn_turned(act, A, t):
            for j in range(4):
                act.wait_ge(aT_done, 4 * t + j + 1)
                k0, k1 = 4 * j, min(4 * j + 4, KCH)
                if k1 == KCH and KW[-1] < P:
                    A(attnT[0:KW[-1], KCH - 1, t * P:(t + 1) * P], ps[0:KW[-1], 4 + j, (KCH - 1 - k0) * P:(KCH - k0) * P],
                      ACT.Copy).then_inc(aT_ready, 1)
                    k1 -= 1
                if k1 > k0:
                    A(attnT[:, k0:k1, t * P:(t + 1) * P], ps[:, 4 + j, 0:(k1 - k0) * P].rearrange("p (k q) -> p k q", q=P),
                      ACT.Copy).then_inc(aT_ready, 1)

        @block.scalar
        def _(act):
            A = nc.scalar.activation
            act.wait_ge(setup_v, 1)
            A(s_t[5], s_t[4], ACT.Exp).then_inc(setup_a, 1)
            act.wait_ge(setup_v, 2)
            A(s_t[8], s_t[6], ACT.Exp).then_inc(setup_a, 1)
            act.wait_ge(setup_v, 3)
            A(s_t[9], s_t[9], ACT.Sin).then_inc(setup_a, 1)
            A(s_t[10], s_t[10], ACT.Sin).then_inc(setup_a, 1)
            act.wait_ge(setup_v, 4)
            A(k_w.rearrange("p a b -> p (a b)"), k_w.rearrange("p a b -> p (a b)"), ACT.Sin).then_inc(setup_a, 1)
            act.wait_ge(setup_v, 5)
            A(s_n, s_n, ACT.Exp).then_inc(setup_a, 1)
            act.wait_ge(setup_v, 6)
            A(s_x, s_x, ACT.Sin).then_inc(setup_a, 1)
            act.wait_ge(setup_v, 7)
            A(s_y, s_y, ACT.Sin).then_inc(setup_a, 1)
            act.wait_ge(setup_v, 8)
            A(s_n[:, 0:NPW], s_n[:, 0:NPW], ACT.Exp).then_inc(setup_a, 1)
            act.wait_ge(setup_done, 1)

            with act.Fori(0, NBATCH) as b:
                n_ln = [0]
                n_xT = [0]

                def deviation():
                    n_ln[0] += 1
                    act.wait_ge(ln_var, TILES * n_ln[0])
                    A(ln_std[:, :], ln_mv[:, :, 1], ACT.Sqrt, bias=eps[:, 0:1]).then_inc(ln_dev, 1)

                def turned():
                    for c in range(DCH):
                        n_xT[0] += 1
                        act.wait_ge(xT_done, n_xT[0])
                        A(xnT[:, c, :], ps[:, 4 + c, :], ACT.Copy).then_inc(xT_ready, 1)

                n = 0
                for g in range(DCH):
                    for c0, w in COLS:
                        act.wait_ge(k0_done, n + 1)
                        A(k_f[:, g, c0:c0 + w], ps[:, n % 4, 0:w], ACT.Identity, bias=bk0[:, g:g + 1]).then_inc(k0_ready, 1)
                        n += 1
                deviation()
                turned()
                for g in range(DCH):
                    act.wait_ge(q0_done, g + 1)
                    A(q_f[:, g, :], ps[:, 6 + g, :], ACT.Identity, bias=bq0[:, g:g + 1], scale=D0 ** -0.5).then_inc(q0_ready, 1)
                for h in range(H0):
                    for k in range(KCH):
                        n = h * KCH + k
                        act.wait_ge(t0_clipped, n + 1)
                        A(probs0[0:KW[k], n % 4, :], probs0[0:KW[k], n % 4, :], ACT.Exp).then_inc(p0_ready, 1)
                        if h >= 1 and k == 2:
                            act.wait_ge(pv0_done, h * KCH)
                            if h >= 3:
                                act.wait_ge(o0_turned, h - 2)
                            A(o_part[:, (h - 1) % 2, :], ps[:, 4 + (h - 1) % 2, :], ACT.Copy).then_inc(o0_ready, 1)
                act.wait_ge(pv0_done, H0 * KCH)
                act.wait_ge(o0_turned, H0 - 2)
                A(o_part[:, (H0 - 1) % 2, :], ps[:, 4 + (H0 - 1) % 2, :], ACT.Copy).then_inc(o0_ready, 1)
                turned()

                deviation()
                turned()
                act.wait_ge(gl_ready, 1)
                A(g_tmp[5], g_tmp[4], ACT.Exp).then_inc(g_exp, 1)
                for n in range(NEXP * ICH):
                    act.wait_ge(gv_done, n + 1)
                    if n >= 2:
                        act.wait_ge(fused_ready, n - 1)
                    A(silu[:, n % 2, :], ps[:, 2 * (n % 2), :], ACT.Silu).then_inc(silu_ready, 1)

                for n, (c0, w) in enumerate(COLS):
                    act.wait_ge(c_done, n + 1)
                    A(kT1[:, c0:c0 + w], ps[:, n % 4, 0:w], ACT.Copy).then_inc(c_ready, 1)
                for k in range(KCH):
                    n = len(COLS) + k
                    act.wait_ge(c_done, n + 1)
                    A(v1[0:KW[k], k, :], ps[0:KW[k], n % 4, 0:DIM], ACT.Copy).then_inc(c_ready, 1)
                deviation()
                turned()
                act.wait_ge(q1_clear, 1)
                act.wait_ge(q1_done, 1)
                for h in range(H1):
                    r = slice(h * D1, (h + 1) * D1)
                    A(q1z[r, h, :], ps[r, 6, :], ACT.Copy, scale=float(np.float32(1) / np.sqrt(np.float32(D1)))).then_inc(q1_ready, 1)
                for n in range(TILES * H1):
                    act.wait_ge(top_ready, n + 1)
                    if n >= H1:
                        act.wait_ge(aT_done, 4 * (n // H1))
                    A(probs1[:, n % H1, 0:GKEYS], s_sb[:, n % 2, 0:GKEYS], ACT.Exp, bias=stat1[:, n % 2, 0:1]).then_inc(e1_ready, 1)
                    A(s_cut[:, n % 2, 0:GKEYS], s_cut[:, n % 2, 0:GKEYS], ACT.Exp, bias=stat1[:, n % 2, 0:1]).then_inc(e1_ready, 1)
                    A(top_e[:, n % 2, :], top[:, n % 2, :], ACT.Exp, bias=stat1[:, n % 2, 0:1],
                      accum_out=stat1[:, n % 2, 1:2]).then_inc(sum1_ready, 1)
                    if n % H1 == 0 and n >= H1:
                        attn_turned(act, A, n // H1 - 1)
                attn_turned(act, A, TILES - 1)
                for c in range(DCH):
                    act.wait_ge(ctx_done, c + 1)
                    A(c_tT[:, c, :], ps[:, c, :], ACT.Copy).then_inc(ctx_ready, 1)
                deviation()
                deviation()
                turned()
                for i in range(HCH):
                    act.wait_ge(h_done, i + 1)
                    A(hid[:, i, :], ps[:, i % 4, :], ACT.Gelu, bias=b1[:, i:i + 1]).then_inc(h_ready, 1)
                deviation()
                deviation()
                turned()
                act.wait_ge(q2_clear, 2)
                for i in range(H2 // 2):
                    act.wait_ge(qk2_done, 2 * i + 1)
                    for j in range(2):
                        r = slice(j * D2, (j + 1) * D2)
                        ins = A(q2z[r, 2 * i + j, :], ps[r, (2 * i) % 4, :], ACT.Copy, scale=D2 ** -0.5)
                    ins.then_inc(qk2_ready, 1)
                    act.wait_ge(qk2_done, 2 * i + 2)
                    A(kT2[:, i, :], ps[:, (2 * i + 1) % 4, :], ACT.Copy).then_inc(qk2_ready, 1)
                for t in range(TILES):
                    act.wait_ge(pv_done, t + 1)
                    A(proj_v[:, t, :], ps[:, t, :], ACT.Copy).then_inc(pv_ready, 1)
                act.wait_ge(g2_read, 1)
                A(sig_v, gate_v, ACT.Sigmoid).then_inc(sig_ready, 1)
                for n in range(NG + 1):
                    if n < NG:
                        t, h = n // H2, n % H2
                        act.wait_ge(s2_max, n + 1)
                        if n >= 2:
                            act.wait_ge(p2T_done, n - 1)
                        A(p2[:, n % 2, :], ps[:, n % 2, :], ACT.Exp, bias=nmax2[:, t, h:h + 1],
                          accum_out=sums2[:, t, h:h + 1]).then_inc(p2_ready, 1)
                    if n >= 1 and (n - 1) % 2 == 1:
                        m = n - 1
                        act.wait_ge(p2T_done, m + 1)
                        if m >= 2:
                            act.wait_ge(o2_done, m - 1)
                        A(pT2[:, m % 2, :], ps[:, 2 + m % 2, :], ACT.Copy).then_inc(p2T_act, 1)
                end_of_batch(act, b)

        @block.tensor
        def _(pe):
            mm, tr = nc.tensor.matmul, nc.tensor.transpose
            pe.wait_ge(setup_v, 9)
            kw_p = s_x.rearrange("p (d a) -> p d a", a=LA)
            for d in range(DIM):
                for j in range(4):
                    ins = mm(ps[32 * j:32 * j + 32, d // P, 4 * (d % P):4 * (d % P) + 4], k_w[:, d, :], kw_p[:, d, j::4],
                             start=True, stop=True)
            ins.then_inc(setup_p, 1)
            pe.wait_ge(setup_v, 10)
            for j in range(FCH):
                for c in range(SEQ // P):
                    ins = mm(ps[:, 2 + j // 2, (j % 2) * DIM:(j % 2 + 1) * DIM], dft_s[:, c, j * P:(j + 1) * P], k_time[:, c, :],
                             start=(c == 0), stop=(c == SEQ // P - 1))
            ins.then_inc(setup_p, 1)
            pe.wait_ge(setup_done, 1)

            with pe.Fori(0, NBATCH) as b:
                n_xT = [0]
                n_src = [0]

                def turn(src):
                    for c in range(DCH):
                        for t in range(TILES):
                            ins = tr(ps[:, 4 + c, t * P:(t + 1) * P], src[:, t, c * P:(c + 1) * P], ident[:, :])
                        ins.then_inc(xT_done, 1)
                    n_xT[0] += DCH

                pe.wait_ge(loaded, 48)
                n = 0
                for g in range(DCH):
                    for c0, w in COLS:
                        if n >= 4:
                            pe.wait_ge(k0_ready, n - 3)
                        for c in range(CTXCH):
                            ins = mm(ps[:, n % 4, 0:w], wk0[:, c, g * P:(g + 1) * P], ctxT[0:CTXP, c, c0:c0 + w],
                                     start=(c == 0), stop=(c == CTXCH - 1))
                        ins.then_inc(k0_done, 1)
                        n += 1
                pe.wait_ge(xn_ready, 1 * TILES)
                turn(xn)
                pe.wait_ge(xT_ready, n_xT[0])
                for g in range(DCH):
                    for c in range(DCH):
                        ins = mm(ps[:, 6 + g, :], wq0[:, c, g * P:(g + 1) * P], xnT[:, c, :], start=(c == 0), stop=(c == DCH - 1))
                    ins.then_inc(q0_done, 1)
                pe.wait_ge(k0_ready, 8)
                for k in range(KCH):
                    if k >= 4:
                        pe.wait_ge(v0_ready, k - 3)
                    for c in range(CTXCH):
                        ins = mm(ps[0:KW[k], k % 4, :], ctxT[0:CTXP, c, k * P:k * P + KW[k]], wv0[:, c, :],
                                 start=(c == 0), stop=(c == CTXCH - 1))
                    ins.then_inc(v0_done, 1)
                pe.wait_ge(v0_ready, KCH)
                pe.wait_ge(k_stacked, 96)
                pe.wait_ge(q_stacked, 96)
                for n in range(H0 * TILES):
                    h, t = n // TILES, n % TILES
                    if n >= 2:
                        pe.wait_ge(s0_read, n - 1)
                    for j, (c0, w) in enumerate(COLS):
                        ins = mm(ps[:, 4 * (n % 2) + j, 0:w], q_stack[0:NSPLIT, h, t * P:(t + 1) * P],
                                 k_stack[0:NSPLIT, h, c0:c0 + w], start=True, stop=True)
                    ins.then_inc(s0_ready, 1)
                pe.wait_ge(nmax_ready, 1)
                for t in range(TILES):
                    ins = tr(ps[0:H0, 0, t * P:(t + 1) * P], neg_max[:, t, :], ident[:, :])
                ins.then_inc(nmaxT_done, 1)
                pe.wait_ge(nmax_stacked, 48)

                def value_product(n):
                    h, k = n // KCH, n % KCH
                    j = k % 4
                    pe.wait_ge(p0_ready, n + 1)
                    if k == 0 and h >= 2:
                        pe.wait_ge(o0_ready, h - 1)
                    mm(ps[32 * j:32 * j + 32, 4 + h % 2, :], v0[0:KW[k], k, h * V0W:(h + 1) * V0W], probs0[0:KW[k], n % 4, :],
                       start=(k < 4), stop=(k >= KCH - 4)).then_inc(pv0_done, 1)

                def turn_head(h):
                    pe.wait_ge(o0_ready, h + 1)
                    if h >= 4:
                        pe.wait_ge(attn0_ready, h - 3)
                    for t in range(TILES):
                        ins = mm(ps[:, 7, (h % 4) * P + t * V0W:(h % 4) * P + (t + 1) * V0W], o_part[:, h % 2, t * P:(t + 1) * P],
                                 fold[:, :], start=True, stop=True)
                    ins.then_inc(o0_turned, 1)

                LAG = 3
                NCK = H0 * KCH
                for n in range(NCK + LAG):
                    if n < NCK:
                        h, k = n // KCH, n % KCH
                        if k == 0:
                            if h >= 1:
                                pe.wait_ge(low_ready, h)
                            mm(ps[:, 6, :], max_rows[:, :], q_stack[:, h, :], start=True, stop=True).then_inc(low_done, 1)
                        if n >= 4:
                            pe.wait_ge(t0_clipped, n - 3)
                        mm(ps[0:KW[k], n % 4, :], k_stack[:, h, k * P:k * P + KW[k]], q_stack[:, h, :],
                           start=True, stop=True).then_inc(t0_ready, 1)
                        if h >= 1 and k == 7:
                            turn_head(h - 1)
                    if n >= LAG:
                        value_product(n - LAG)
                turn_head(H0 - 1)
                pe.wait_ge(attn0_ready, H0)
                turn(attn0)
                pe.wait_ge(xT_ready, n_xT[0])
                for t in range(TILES):
                    for c in range(DCH):
                        ins = mm(ps[:, t, 0:DIM], xnT[:, c, t * P:(t + 1) * P], wo0[:, c, :], start=(c == 0), stop=(c == DCH - 1))
                    ins.then_inc(y0_done, 1)

                pe.wait_ge(xn_ready, 2 * TILES)
                turn(xn)
                pe.wait_ge(xT_ready, n_xT[0])
                for t in range(TILES):
                    for c in range(DCH):
                        ins = mm(ps[:, 6, t * NEXP:(t + 1) * NEXP], xnT[:, c, t * P:(t + 1) * P], wg[:, c, :],
                                 start=(c == 0), stop=(c == DCH - 1))
                ins.then_inc(gl_done, 1)
                pe.wait_ge(x1_ready, TILES)

                def expert_down(e):
                    for t in range(TILES):
                        pe.wait_ge(fused_ready, ICH * (e + 1))
                        m = e * TILES + t
                        if m >= 4:
                            pe.wait_ge(down_read, m - 3)
                        for i in range(ICH):
                            ins = mm(ps[:, 4 + m % 4, 0:DIM], fused[:, e % 2, i * SEQ + t * P:i * SEQ + (t + 1) * P], w2e[e % 2][:, i, :],
                                     start=(i == 0), stop=(i == ICH - 1))
                        ins.then_inc(down_done, 1)

                pe.wait_ge(gl_ready, 1)
                for e in range(NEXP):
                    pe.wait_ge(w_loaded[e % 2], 48 * (e // 2 + 1))
                    for i in range(ICH):
                        n = e * ICH + i
                        if n >= 2:
                            pe.wait_ge(fused_ready, n - 1)
                        for j, w in enumerate((w11, w12)):
                            for c in range(DCH):
                                ins = mm(ps[:, 2 * (n % 2) + j, :], w[e % 2][:, c, i * P:(i + 1) * P], xnT[:, c, :],
                                         start=(c == 0), stop=(c == DCH - 1))
                        ins.then_inc(gv_done, 1)
                        if i == 1 and e >= 1:
                            expert_down(e - 1)
                expert_down(NEXP - 1)

                pe.wait_ge(fused_ready, NEXP * ICH)
                for n in range(len(COLS) + KCH):
                    if n >= 4:
                        pe.wait_ge(c_ready, n - 3)
                    for c in range(CTXCH):
                        if n < len(COLS):
                            c0, w = COLS[n]
                            ins = mm(ps[:, n % 4, 0:w], wk1[:, c, :], ctxT[0:CTXP, c, c0:c0 + w], start=(c == 0), stop=(c == CTXCH - 1))
                        else:
                            k = n - len(COLS)
                            ins = mm(ps[0:KW[k], n % 4, 0:DIM], ctxT[0:CTXP, c, k * P:k * P + KW[k]], wv1[:, c, :],
                                     start=(c == 0), stop=(c == CTXCH - 1))
                    ins.then_inc(c_done, 1)
                pe.wait_ge(down_read, NEXP * TILES)
                pe.wait_ge(xn_ready, 3 * TILES)
                turn(xt)
                pe.wait_ge(xT_ready, n_xT[0])
                for c in range(DCH):
                    ins = mm(ps[:, 6, :], wq1[:, c, :], xnT[:, c, :], start=(c == 0), stop=(c == DCH - 1))
                ins.then_inc(q1_done, 1)
                pe.wait_ge(c_ready, len(COLS) + KCH)
                pe.wait_ge(q1_ready, H1)

                def turn_probs(t):
                    pe.wait_ge(p1_ready, H1 * (t + 1))
                    pe.wait_ge(eye_ready, H1 * (t + 1))
                    if t >= 1:
                        pe.wait_ge(aT_ready, 4 * t)
                    for k in range(KCH):
                        for h in range(H1):
                            ins = mm(ps[0:KW[k], 4 + k // 4, (k % 4) * P:(k % 4 + 1) * P], probs1[:, h, k * P:k * P + KW[k]],
                                     scaled_eye[:, h, :], start=(h == 0), stop=(h == H1 - 1))
                        if k % 4 == 3 or k == KCH - 1:
                            ins.then_inc(aT_done, 1)

                for n in range(TILES * H1):
                    t, h = n // H1, n % H1
                    if n >= 1:
                        pe.wait_ge(s1_ready, n)
                    for j, (c0, w) in enumerate(COLS):
                        ins = mm(ps[:, j, 0:w], q1z[:, h, t * P:(t + 1) * P], kT1[:, c0:c0 + w], start=True, stop=True)
                    ins.then_inc(s1_done, 1)
                    if h == 0 and t >= 1:
                        turn_probs(t - 1)
                turn_probs(TILES - 1)
                pe.wait_ge(aT_ready, 4 * TILES)
                for c in range(DCH):
                    for k in range(KCH):
                        ins = mm(ps[:, c, :], v1[0:KW[k], k, c * P:(c + 1) * P], attnT[0:KW[k], k, :], start=(k == 0), stop=(k == KCH - 1))
                    ins.then_inc(ctx_done, 1)

                pe.wait_ge(ctx_ready, DCH)
                for i in range(2):
                    for t in range(TILES):
                        n = i * TILES + t
                        if n >= 4:
                            pe.wait_ge(film_read, n - 3)
                        for c in range(DCH):
                            ins = mm(ps[:, n % 4, :], c_tT[:, c, t * P:(t + 1) * P], film_w[:, i, c, :], start=(c == 0), stop=(c == DCH - 1))
                        ins.then_inc(film_done, 1)
                pe.wait_ge(u_ready, TILES)
                pe.wait_ge(w_late, 16 * 9)
                for j in range(FCH // 2):
                    for half in range(2):
                        for c in range(SEQ // P):
                            ins = mm(ps[:, 4 + j, half * DIM:(half + 1) * DIM], dft[:, c, (half * (FCH // 2) + j) * P:(half * (FCH // 2) + j + 1) * P],
                                     u[:, c, :], start=(c == 0), stop=(c == SEQ // P - 1))
                    ins.then_inc(spec_done, 1)
                pe.wait_ge(spec_ready, FCH // 2)
                pe.wait_ge(film_read, 2 * TILES)
                for t in range(TILES):
                    for j in range(FCH):
                        ins = mm(ps[:, t, 0:DIM], idft[:, j, t * P:(t + 1) * P], spec[:, j, :], start=(j == 0), stop=(j == FCH - 1))
                    ins.then_inc(y1_done, 1)

                pe.wait_ge(xn_ready, 4 * TILES)
                turn(xn)
                pe.wait_ge(xT_ready, n_xT[0])
                for i in range(HCH):
                    if i >= 4:
                        pe.wait_ge(h_ready, i - 3)
                    for c in range(DCH):
                        ins = mm(ps[:, i % 4, :], wf1[:, c, i * P:(i + 1) * P], xnT[:, c, :], start=(c == 0), stop=(c == DCH - 1))
                    ins.then_inc(h_done, 1)
                pe.wait_ge(h_ready, HCH)
                for t in range(TILES):
                    for i in range(HCH):
                        ins = mm(ps[:, 4 + t, 0:DIM], hid[:, i, t * P:(t + 1) * P], wf2[:, i, :], start=(i == 0), stop=(i == HCH - 1))
                    ins.then_inc(f_done, 1)

                pe.wait_ge(xn_ready, 5 * TILES)
                turn(xn)
                pe.wait_ge(xT_ready, n_xT[0])
                for i in range(H2):
                    w = wk2 if i % 2 else wq2
                    if i >= 4:
                        pe.wait_ge(qk2_ready, i - 3)
                    for c in range(DCH):
                        ins = mm(ps[:, i % 4, :], w[:, c, (i // 2) * P:(i // 2 + 1) * P], xnT[:, c, :], start=(c == 0), stop=(c == DCH - 1))
                    ins.then_inc(qk2_done, 1)
                for t in range(TILES):
                    for j in range(2):
                        for c in range(DCH):
                            ins = mm(ps[:, 6 + j, t * P:(t + 1) * P], xnT[:, c, t * P:(t + 1) * P], wsd[:, c, j * P:(j + 1) * P],
                                     start=(c == 0), stop=(c == DCH - 1))
                ins.then_inc(g2_done, 1)
                pe.wait_ge(qk2_ready, H2)
                for t in range(TILES):
                    for c in range(DCH):
                        ins = mm(ps[:, t, :], xnT[:, c, t * P:(t + 1) * P], wv2[:, c, :], start=(c == 0), stop=(c == DCH - 1))
                    ins.then_inc(pv_done, 1)
                pe.wait_ge(pv_ready, TILES)
                pe.wait_ge(g2_read, 2)

                def turn_p2(n):
                    pe.wait_ge(p2_ready, n + 1)
                    if n >= 2:
                        if n % 2:
                            pe.wait_ge(p2T_act, n // 2)
                        else:
                            pe.wait_ge(p2T_dve, n // 2)
                    for j in range(TILES):
                        ins = tr(ps[:, 2 + n % 2, j * P:(j + 1) * P], p2[:, n % 2, j * P:(j + 1) * P], ident[:, :])
                    ins.then_inc(p2T_done, 1)

                def value2(n):
                    t, h = n // H2, n % H2
                    if n == 0:
                        pe.wait_ge(v2_ready, TILES - 1)
                        pe.wait_ge(v2_ready_p, 1)
                    if n % 2:
                        pe.wait_ge(p2T_act, n // 2 + 1)
                    else:
                        pe.wait_ge(p2T_dve, n // 2 + 1)
                    if h == 0 and t >= 1:
                        pe.wait_ge(z_ready, t)
                    for j in range(TILES):
                        ins = mm(ps[:, 4 + h // 8, (h % 8) * D2:(h % 8 + 1) * D2], pT2[:, n % 2, j * P:(j + 1) * P],
                                 v2[:, j, h * D2:(h + 1) * D2], start=(j == 0), stop=(j == TILES - 1))
                    ins.then_inc(o2_done, 1)

                def result(t):
                    pe.wait_ge(z_ready, t + 1)
                    if t >= 1:
                        pe.wait_ge(out_ready, t)
                    for c in range(TILES):
                        ins = tr(ps[:, 6, c * P:(c + 1) * P], z[:, c * P:(c + 1) * P], ident[:, :])
                    ins.then_inc(zT_done, 1)
                    pe.wait_ge(zT_ready, t + 1)
                    for c in range(TILES):
                        ins = mm(ps[:, 7, 0:DIM], zT[:, c * P:(c + 1) * P], wo2[:, c, :], start=(c == 0), stop=(c == TILES - 1))
                    ins.then_inc(r_done, 1)

                for n in range(NG + 2):
                    if n < NG:
                        h, t = n % H2, n // H2
                        if n >= 2:
                            pe.wait_ge(p2_ready, n - 1)
                        mm(ps[:, n % 2, :], q2z[:, h, t * P:(t + 1) * P], kT2[:, h // 2, :], start=True, stop=True).then_inc(s2_done, 1)
                    if 1 <= n <= NG:
                        turn_p2(n - 1)
                    if n >= 2:
                        value2(n - 2)
                        if (n - 2) % H2 == H2 - 1:
                            result((n - 2) // H2)
                end_of_batch(pe, b)

        def weights(dve, V, link, n):
            t, h = n // H1, n % H1
            dve.wait_ge(sum1_ready, n + 1)
            if n >= H1:
                dve.wait_ge(aT_done, 4 * t)
            link(V.reciprocal(stat1[:, n % 2, 2:3], stat1[:, n % 2, 1:2]))
            link(V.tensor_scalar(stat1[:, n % 2, 2:3], stat1[:, n % 2, 2:3], tmask[:, t:t + 1], 1.0 / H1, ALU.mult, ALU.mult))
            V.tensor_scalar(scaled_eye[:, h, :], ident[:, :], stat1[:, n % 2, 2:3], None, ALU.mult).then_inc(eye_ready, 1)

        @block.vector
        def _(dve):
            V = nc.vector
            steps = [0]
            step_sem = [setup_v]

            def setup_program():
                count = [0]
                own = [0]
                chain = ctx.enter_context(nc.semaphore("setup_step"))

                def link(ins):
                    own[0] += 1
                    ins.then_inc(chain, 1)
                    dve.wait_ge(chain, own[0])

                def done(n):
                    count[0] += 1
                    assert count[0] == n
                    dve.drain().then_inc(setup_v, 1)

                link(V.memset(eps[:, :], LN_EPS))
                dve.wait_ge(consts, 16 * len(NLOADS))
                link(V.tensor_scalar(bq0[:, :], bq0[:, :], D0 ** -0.5, None, ALU.mult))
                done(1)
                ar, ai, dt = s_t[6], s_t[7], s_t[5]
                dve.wait_ge(setup_a, 1)
                link(V.tensor_tensor(ar, s_t[0], dt, ALU.mult))
                link(V.tensor_tensor(ai, s_t[1], dt, ALU.mult))
                done(2)
                C1 = 6.28125
                C2 = TWO_PI - C1

                def reduce_angle(out, n, theta, turns, col):
                    link(V.tensor_scalar(n, theta, 1.0 / TWO_PI, turns, ALU.mult, ALU.add))
                    link(V.tensor_scalar(n, n, MAGIC, MAGIC, ALU.add, ALU.subtract))
                    link(V.scalar_tensor_tensor(theta, n, -C1, theta, ALU.mult, ALU.add))
                    link(V.scalar_tensor_tensor(theta, n, -C2, theta, ALU.mult, ALU.add))
                    link(V.tensor_scalar(out, theta, col, 3.14159, ALU.add, ALU.min))
                    link(V.tensor_scalar(out, out, -3.14159, None, ALU.max))

                link(V.tensor_copy(s_t[11], ai))
                reduce_angle(s_t[9], s_t[12], s_t[11], 0.25, float(TWO_PI / 4))
                link(V.tensor_copy(s_t[11], ai))
                reduce_angle(s_t[10], s_t[12], s_t[11], 0.0, 0.0)
                done(3)
                dve.wait_ge(setup_a, 4)
                er, ei, den, br, bi, t0, t1 = s_t[9], s_t[10], s_t[11], s_t[12], s_t[13], s_t[14], s_t[15]
                link(V.tensor_tensor(er, er, s_t[8], ALU.mult))
                link(V.tensor_scalar(er, er, -1.0, None, ALU.add))
                link(V.tensor_tensor(ei, ei, s_t[8], ALU.mult))
                link(V.tensor_tensor(den, s_t[0], s_t[0], ALU.mult))
                link(V.tensor_tensor(t0, s_t[1], s_t[1], ALU.mult))
                link(V.tensor_tensor(den, den, t0, ALU.add))
                link(V.reciprocal(den, den))

                def cmul(out, p, q, r, s, sign):
                    link(V.tensor_tensor(t0, p, q, ALU.mult))
                    link(V.tensor_tensor(t1, r, s, ALU.mult))
                    link(V.tensor_tensor(out, t0, t1, ALU.add if sign > 0 else ALU.subtract))

                cmul(br, er, s_t[0], ei, s_t[1], 1)
                cmul(bi, ei, s_t[0], er, s_t[1], -1)
                link(V.tensor_tensor(br, br, den, ALU.mult))
                link(V.tensor_tensor(bi, bi, den, ALU.mult))
                g1, g2 = s_t[16], s_t[17]
                cmul(g1, s_t[2], br, s_t[3], bi, -1)
                cmul(g2, s_t[2], bi, s_t[3], br, 1)
                link(V.tensor_scalar(g1[0:NSTATE, :], g1[0:NSTATE, :], 2.0, None, ALU.mult))
                link(V.tensor_scalar(g1[NSTATE:P, :], g1[NSTATE:P, :], -2.0, None, ALU.mult))
                link(V.tensor_scalar(g2, g2, -2.0, None, ALU.mult))
                kb = ramp[:, 0:LB].unsqueeze(1).to_broadcast([P, DIM, LB])
                ka = ramp[:, LB:LB + LA].unsqueeze(1).to_broadcast([P, DIM, LA])
                kw = k_w.rearrange("p a b -> p (a b)")
                link(V.tensor_tensor(k_w, ai.unsqueeze(2).to_broadcast([P, DIM, LB]), kb, ALU.mult))
                reduce_angle(kw, s_n, kw, phase[:, 2:3], phase[:, 0:1])
                done(4)
                link(V.tensor_tensor(s_n.rearrange("p (a b) -> p a b", b=LB), ar.unsqueeze(2).to_broadcast([P, DIM, LB]), kb, ALU.mult))
                done(5)
                dve.wait_ge(setup_a, 6)
                link(V.tensor_tensor(kw, kw, s_n, ALU.mult))
                sx3, sy3 = (v.rearrange("p (d a) -> p d a", a=LA) for v in (s_x, s_y))
                ai3 = ai.unsqueeze(2).to_broadcast([P, DIM, LA])
                link(V.tensor_tensor(sx3, ai3, ka, ALU.mult))
                reduce_angle(s_x, s_n[:, 0:NPW], s_x, phase[:, 2:3], phase[:, 0:1])
                done(6)
                link(V.tensor_tensor(sy3, ai3, ka, ALU.mult))
                reduce_angle(s_y, s_n[:, 0:NPW], s_y, phase[:, 3:4], phase[:, 1:2])
                done(7)
                link(V.tensor_tensor(s_n[:, 0:NPW].rearrange("p (d a) -> p d a", a=LA), ar.unsqueeze(2).to_broadcast([P, DIM, LA]), ka, ALU.mult))
                done(8)
                dve.wait_ge(setup_a, 9)
                link(V.tensor_tensor(sx3, sx3, g1.unsqueeze(2).to_broadcast([P, DIM, LA]), ALU.mult))
                link(V.tensor_tensor(sy3, sy3, g2.unsqueeze(2).to_broadcast([P, DIM, LA]), ALU.mult))
                link(V.tensor_tensor(s_x, s_x, s_y, ALU.add))
                link(V.tensor_tensor(s_x, s_x, s_n[:, 0:NPW], ALU.mult))
                done(9)
                dve.wait_ge(setup_p, 1)
                for bank in range(2):
                    link(V.tensor_copy(k_time[:, :, bank * P:(bank + 1) * P], ps[:, bank, :].rearrange("p (d a) -> p a d", a=4)))
                done(10)
                dve.wait_ge(setup_p, 2)
                half = FCH // 2
                spec_k = ps[:, 2:6, :].rearrange("p b (j d) -> p (b j) d", d=DIM)
                link(V.tensor_copy(k_cos[:, :, :], spec_k[:, 0:half, :]))
                link(V.tensor_copy(k_sin[:, :, :], spec_k[:, half:FCH, :]))
                link(V.tensor_copy(k_cos0[:, :], k_cos[:, 0, :]))
                link(V.tensor_copy(k_cos0[0:1, :], k_sin[0:1, 0, :]))
                link(V.memset(k_sin[0:1, 0, :], 0.0))
                dve.drain().then_inc(setup_done, 1)

            setup_program()

            with dve.Fori(0, NBATCH) as b:
                steps = [0]
                n_ln = [0]

                def link(ins):
                    steps[0] += 1
                    ins.then_inc(v_step, 1)
                    dve.wait_ge(v_step, steps[0])

                def layernorm(dst, src, event):
                    n_ln[0] += 1
                    for t in range(TILES):
                        link(V.bn_stats(ln_stats[:, t, :], src[:, t, :]))
                    for t in range(TILES):
                        V.bn_aggr(ln_mv[:, t, :], ln_stats[:, t, :]).then_inc(ln_var, 1)
                    dve.wait_ge(ln_dev, n_ln[0])
                    link(V.reciprocal(ln_rstd[:, :], ln_std[:, :]))
                    for t in range(TILES):
                        ins = V.tensor_scalar(dst[:, t, :], src[:, t, :], ln_mv[:, t, 0:1], ln_rstd[:, t:t + 1], ALU.subtract, ALU.mult)
                        if event:
                            ins.then_inc(xn_ready, 1)
                        else:
                            link(ins)

                def rows(v):
                    return v.unsqueeze(1).to_broadcast([P, TILES, DIM])

                def per(v, n):
                    return v.unsqueeze(2).to_broadcast([P, v.shape[1], n])

                def top2(vals, m, oh1, oh2, tmp):
                    n = vals.shape[1]
                    first = prio[:, :].unsqueeze(1).to_broadcast([P, n, NEXP])
                    for k, oh in enumerate((oh1, oh2)):
                        src = vals if k == 0 else tmp
                        link(V.tensor_reduce(m, src, AX.X, ALU.max))
                        link(V.tensor_tensor(oh, src, per(m, NEXP), ALU.is_equal))
                        link(V.tensor_tensor(oh, oh, first, ALU.mult))
                        link(V.tensor_reduce(m, oh, AX.X, ALU.max))
                        link(V.tensor_tensor(oh, oh, per(m, NEXP), ALU.is_equal))
                        if k == 0:
                            link(V.scalar_tensor_tensor(tmp, oh, DROPPED, vals, ALU.mult, ALU.add))

                dve.wait_ge(loaded, 48)
                layernorm(xn, x, True)
                for g in range(DCH):
                    dve.wait_ge(k0_ready, len(COLS) * (g + 1))
                    link(V.tensor_copy(k_p[:, 0, g, 0:GKEYS], k_f[:, g, :]))
                    link(V.tensor_tensor(k_r[:, g, :], k_f[:, g, :], k_p[:, 0, g, 0:GKEYS], ALU.subtract))
                    link(V.tensor_copy(k_p[:, 1, g, 0:GKEYS], k_r[:, g, :]))
                    V.tensor_tensor(k_p[:, 2, g, 0:GKEYS], k_r[:, g, :], k_p[:, 1, g, 0:GKEYS], ALU.subtract).then_inc(k_parts, 1)
                dve.wait_ge(q0_ready, DCH)
                link(V.tensor_copy(q_p[:, 0], q_f))
                link(V.tensor_tensor(q_r, q_f, q_p[:, 0], ALU.subtract))
                link(V.tensor_copy(q_p[:, 1], q_r))
                V.tensor_tensor(q_p[:, 2], q_r, q_p[:, 1], ALU.subtract).then_inc(q_parts, 1)
                link(V.tensor_copy(tmask[:, :], tmask8[:, :]))
                dve.wait_ge(k_spilled, 48)
                dve.wait_ge(q_spilled, 48)
                for k in range(KCH):
                    dve.wait_ge(v0_done, k + 1)
                    V.tensor_tensor(v0[0:KW[k], k, :], ps[0:KW[k], k % 4, :], bv0[0:KW[k], :], ALU.add).then_inc(v0_ready, 1)
                for n in range(H0 * TILES):
                    h, t = n // TILES, n % TILES
                    dve.wait_ge(s0_ready, n + 1)
                    V.tensor_reduce(row_max[:, t, h:h + 1], wide(4 * (n % 2), GKEYS), AX.X, ALU.max).then_inc(s0_read, 1)
                dve.wait_ge(s0_read, H0 * TILES)
                link(V.tensor_scalar(neg_max, row_max, -CLAMP, CLAMP, ALU.max, ALU.min))
                V.tensor_scalar(neg_max, neg_max, -1.0, None, ALU.mult).then_inc(nmax_ready, 1)
                dve.wait_ge(nmaxT_done, 1)
                link(V.tensor_copy(nm_f[0:H0, :], ps[0:H0, 0, :]))
                link(V.tensor_copy(nm_p[0:H0, 0, :], nm_f[0:H0, :]))
                link(V.tensor_tensor(nm_r[0:H0, :], nm_f[0:H0, :], nm_p[0:H0, 0, :], ALU.subtract))
                link(V.tensor_copy(nm_p[0:H0, 1, :], nm_r[0:H0, :]))
                V.tensor_tensor(nm_p[0:H0, 2, :], nm_r[0:H0, :], nm_p[0:H0, 1, :], ALU.subtract).then_inc(nmax_parts, 1)

                def head_rows(h):
                    dve.wait_ge(o0_turned, h + 1)
                    o4 = ps[:, 7, (h % 4) * P:(h % 4 + 1) * P].rearrange("p (t d) -> p t d", d=V0W)
                    r = small[:, 0:TILES]
                    link(V.reciprocal(r, o4[:, :, D0]))
                    V.tensor_tensor(attn0[:, :, h * D0:(h + 1) * D0], o4[:, :, 0:D0], per(r, D0), ALU.mult).then_inc(attn0_ready, 1)

                for h in range(H0):
                    dve.wait_ge(low_done, h + 1)
                    V.tensor_scalar(low[:, h % 2, :], ps[:, 6, :], -CLAMP, None, ALU.add).then_inc(low_ready, 1)
                    dve.wait_ge(low_ready, h + 1)
                    for k in range(KCH):
                        n = h * KCH + k
                        dve.wait_ge(t0_ready, n + 1)
                        if n >= 4:
                            dve.wait_ge(pv0_done, n - 3)
                        w = KW[k]
                        V.scalar_tensor_tensor(probs0[0:w, n % 4, :], ps[0:w, n % 4, :], 0.0, low[0:w, h % 2, :],
                                               ALU.min, ALU.max).then_inc(t0_clipped, 1)
                        if h >= 1 and k == 11:
                            head_rows(h - 1)
                head_rows(H0 - 1)
                for t in range(TILES):
                    dve.wait_ge(y0_done, t + 1)
                    link(V.tensor_tensor(x[:, t, :], x[:, t, :], ps[:, t, 0:DIM], ALU.add))
                    V.tensor_tensor(x[:, t, :], x[:, t, :], bo0[:, :], ALU.add).then_inc(x1_ready, 1)
                dve.wait_ge(x1_ready, TILES)

                layernorm(xn, x, True)
                dve.wait_ge(gl_done, 1)
                link(V.tensor_copy(gl, ps[:, 6, 0:TILES * NEXP].rearrange("p (t e) -> p t e", e=NEXP)))
                link(V.tensor_reduce(g_red[0], gl, AX.X, ALU.max))
                V.tensor_tensor(g_tmp[4], gl, per(g_red[0], NEXP), ALU.subtract).then_inc(gl_ready, 1)
                top2(gl, g_red[1], g_tmp[0], g_tmp[1], g_tmp[2])
                dve.wait_ge(g_exp, 1)
                link(V.tensor_reduce(g_red[2], g_tmp[5], AX.X, ALU.add))
                link(V.reciprocal(g_red[2], g_red[2]))
                link(V.tensor_tensor(g_tmp[5], g_tmp[5], per(g_red[2], NEXP), ALU.mult))
                link(V.tensor_tensor(g_tmp[0], g_tmp[0], g_tmp[1], ALU.add))
                link(V.tensor_tensor(g_w, g_tmp[0], g_tmp[5], ALU.mult))
                link(V.tensor_reduce(g_red[3], g_w, AX.X, ALU.add))
                link(V.tensor_scalar(g_red[3], g_red[3], 1e-8, None, ALU.add))
                link(V.reciprocal(g_red[3], g_red[3]))
                link(V.tensor_tensor(g_w, g_w, per(g_red[3], NEXP), ALU.mult))

                def expert_sum(e):
                    for t in range(TILES):
                        m = e * TILES + t
                        dve.wait_ge(down_done, m + 1)
                        if e:
                            dve.wait_ge(down_read, m - TILES + 1)
                        V.scalar_tensor_tensor(x[:, t, :], ps[:, 4 + m % 4, 0:DIM], g_w[:, t, e:e + 1], x[:, t, :],
                                               ALU.mult, ALU.add).then_inc(down_read, 1)

                for e in range(NEXP):
                    for i in range(ICH):
                        n = e * ICH + i
                        dve.wait_ge(silu_ready, n + 1)
                        if e >= 2 and i == 0:
                            dve.wait_ge(down_done, TILES * (e - 1))
                        V.tensor_tensor(fused[:, e % 2, i * SEQ:(i + 1) * SEQ], silu[:, n % 2, :], ps[:, 2 * (n % 2) + 1, :],
                                        ALU.mult).then_inc(fused_ready, 1)
                        if e >= 1 and i == 3:
                            expert_sum(e - 1)
                expert_sum(NEXP - 1)
                dve.wait_ge(down_read, TILES * NEXP)

                layernorm(xt, x, True)
                dve.wait_ge(loaded, 64)
                link(V.tensor_scalar(key_bias[:, :], mask8[:, :], MASKED, MASKED, ALU.mult, ALU.subtract))
                for n in range(TILES * H1):
                    t, h = n // H1, n % H1
                    i = n % 2
                    dve.wait_ge(s1_done, n + 1)
                    if n >= 2:
                        dve.wait_ge(sum1_ready, n - 1)
                        dve.wait_ge(p1_ready, n - 1)
                    s = s_sb[:, i, 0:GKEYS]
                    cut = s_cut[:, i, 0:GKEYS]
                    V.tensor_tensor(s, wide(0, GKEYS), key_bias[:, :], ALU.add).then_inc(s1_ready, 1)
                    dve.wait_ge(s1_ready, n + 1)
                    for r in range(TOPK // 8):
                        eight = top[:, i, 8 * r:8 * r + 8]
                        link(V.max(eight, s if r == 0 else cut))
                        ins = V.match_replace(cut, eight, s if r == 0 else cut, DROPPED)
                        link(ins)
                    V.tensor_scalar(stat1[:, i, 0:1], top[:, i, 0:1], -1.0, None, ALU.mult).then_inc(top_ready, 1)
                    if n >= 1:
                        weights(dve, V, link, n - 1)
                weights(dve, V, link, TILES * H1 - 1)

                layernorm(xn, xt, False)
                link(V.tensor_tensor(xn[:, :, :], xn[:, :, :], rows(norm_g[:, 0, :]), ALU.mult))
                link(V.tensor_tensor(xn[:, :, :], xn[:, :, :], rows(norm_b[:, 0, :]), ALU.add))
                dve.wait_ge(ctx_done, DCH)
                dve.wait_ge(aT_ready, 4 * TILES)
                for i, f in enumerate((f_in, f_out)):
                    for t in range(TILES):
                        n = i * TILES + t
                        dve.wait_ge(film_done, n + 1)
                        V.tensor_tensor(f[:, t, :], ps[:, n % 4, :], film_b[:, i, :], ALU.add).then_inc(film_read, 1)
                        dve.wait_ge(film_read, n + 1)
                        link(V.tensor_scalar(f[:, t, :], f[:, t, :], mod_gate[:, 0:1], None, ALU.mult))
                        if i == 0:
                            link(V.scalar_tensor_tensor(u[:, t, :], f[:, t, 0:DIM], 1.0, xn[:, t, :], ALU.add, ALU.mult))
                            V.tensor_tensor(u[:, t, :], u[:, t, :], f[:, t, DIM:], ALU.add).then_inc(u_ready, 1)
                dve.wait_ge(u_ready, TILES)
                link(V.tensor_tensor(dtmp[:, :, :], u[:, :, :], rows(d_skip[:, :]), ALU.mult))
                half = FCH // 2
                for j in range(half):
                    dve.wait_ge(spec_done, j + 1)
                    uc, us = ps[:, 4 + j, 0:DIM], ps[:, 4 + j, DIM:2 * DIM]
                    kc, ks = k_cos[:, j, :], k_sin[:, j, :]
                    kc2 = k_cos0[:, :] if j == 0 else kc
                    p4 = ptmp[:, j % 2]
                    V.tensor_tensor(p4[:, 0, :], uc, kc, ALU.mult)
                    V.tensor_tensor(p4[:, 1, :], us, ks, ALU.mult)
                    V.tensor_tensor(p4[:, 2, :], uc, ks, ALU.mult)
                    link(V.tensor_tensor(p4[:, 3, :], us, kc2, ALU.mult))
                    link(V.tensor_tensor(spec[:, j, :], p4[:, 0, :], p4[:, 1, :], ALU.subtract))
                    V.tensor_tensor(spec[:, half + j, :], p4[:, 2, :], p4[:, 3, :], ALU.add).then_inc(spec_ready, 1)
                for t in range(TILES):
                    dve.wait_ge(y1_done, t + 1)
                    link(V.tensor_tensor(dtmp[:, t, :], dtmp[:, t, :], ps[:, t, 0:DIM], ALU.add))
                    link(V.scalar_tensor_tensor(dtmp[:, t, :], f_out[:, t, 0:DIM], 1.0, dtmp[:, t, :], ALU.add, ALU.mult))
                    link(V.tensor_tensor(dtmp[:, t, :], dtmp[:, t, :], f_out[:, t, DIM:], ALU.add))
                    link(V.tensor_tensor(xt[:, t, :], xt[:, t, :], dtmp[:, t, :], ALU.add))

                layernorm(xn, xt, False)
                link(V.tensor_tensor(xn[:, :, :], xn[:, :, :], rows(norm_g[:, 1, :]), ALU.mult))
                for t in range(TILES):
                    V.tensor_tensor(xn[:, t, :], xn[:, t, :], norm_b[:, 1, :], ALU.add).then_inc(xn_ready, 1)
                for t in range(TILES):
                    dve.wait_ge(f_done, t + 1)
                    link(V.tensor_tensor(xt[:, t, :], xt[:, t, :], ps[:, 4 + t, 0:DIM], ALU.add))
                    link(V.tensor_tensor(xt[:, t, :], xt[:, t, :], b2[:, :], ALU.add))
                dve.wait_ge(xn_ready, 4 * TILES)
                layernorm(xn, xt, False)
                link(V.tensor_tensor(xn[:, :, :], xn[:, :, :], rows(norm_g[:, 2, :]), ALU.mult))
                link(V.tensor_tensor(xn[:, :, :], xn[:, :, :], rows(norm_b[:, 2, :]), ALU.add))
                link(V.tensor_tensor(x[:, :, :], x[:, :, :], xn[:, :, :], ALU.add))

                layernorm(xn, x, True)
                dve.wait_ge(g2_done, 1)
                V.tensor_copy(gate_v, ps[:, 6, :].rearrange("p (n e) -> p n e", e=E2)).then_inc(g2_read, 1)
                V.tensor_copy(gate_o, ps[:, 7, :].rearrange("p (n e) -> p n e", e=E2)).then_inc(g2_read, 1)
                dve.wait_ge(g2_read, 2)
                top2(gate_v, t_m, t_oh1, t_oh2, t_a)
                link(V.tensor_tensor(t_oh1, t_oh1, t_oh2, ALU.add))
                dve.wait_ge(sig_ready, 1)
                V.tensor_tensor(t_b, t_oh1, sig_v, ALU.mult).then_inc(mix_ready, 1)
                dve.wait_ge(mix_ready, 1)
                dve.wait_ge(pv_ready, TILES)
                for t in range(TILES - 1):
                    for e in range(E2):
                        src = proj_v[:, t, e * D2:(e + 1) * D2].unsqueeze(1).to_broadcast([P, H2, D2])
                        mix = t_b[:, t * H2:(t + 1) * H2, e].unsqueeze(2).to_broadcast([P, H2, D2])
                        dst = v2[:, t, :] if e == 0 else v_tmp
                        link(V.tensor_tensor(dst.rearrange("p (h d) -> p h d", d=D2), src, mix, ALU.mult))
                        if e:
                            link(V.tensor_tensor(v2[:, t, :], v2[:, t, :], v_tmp, ALU.add))
                    dve.drain().then_inc(v2_ready, 1)
                top2(gate_o, t_m, t_oh1, t_oh2, t_a)
                link(V.tensor_tensor(t_oh1, t_oh1, t_oh2, ALU.add))

                def turned_p2(n):
                    dve.wait_ge(p2T_done, n + 1)
                    if n >= 2:
                        dve.wait_ge(o2_done, n - 1)
                    V.tensor_copy(pT2[:, n % 2, :], ps[:, 2 + n % 2, :]).then_inc(p2T_dve, 1)

                def head_sum(t):
                    dve.wait_ge(p2_ready, H2 * (t + 1))
                    link(V.reciprocal(rs2[:, t, :], sums2[:, t, :]))
                    g = t_oh1[:, t * H2:(t + 1) * H2, :]
                    link(V.tensor_tensor(g, g, per(rs2[:, t, :], E2), ALU.mult))
                    if t >= 1:
                        dve.wait_ge(zT_done, t)
                    for h in range(H2):
                        dve.wait_ge(o2_done, t * H2 + 8 * (h // 8) + 8)
                        src = ps[:, 4 + h // 8, (h % 8) * D2:(h % 8 + 1) * D2].unsqueeze(1).to_broadcast([P, E2, D2])
                        gate = g[:, h, :].unsqueeze(2).to_broadcast([P, E2, D2])
                        dst = z if h == 0 else z_tmp
                        link(V.tensor_tensor(dst.rearrange("p (e d) -> p e d", d=D2), src, gate, ALU.mult))
                        if h:
                            link(V.tensor_tensor(z, z, z_tmp, ALU.add))
                    dve.drain().then_inc(z_ready, 1)
                    dve.wait_ge(zT_done, t + 1)
                    V.tensor_copy(zT, ps[:, 6, :]).then_inc(zT_ready, 1)
                    dve.wait_ge(r_done, t + 1)
                    V.tensor_tensor(x[:, t, :], x[:, t, :], ps[:, 7, 0:DIM], ALU.add).then_inc(out_ready, 1)

                for n in range(NG + 1):
                    if n < NG:
                        t, h = n // H2, n % H2
                        dve.wait_ge(s2_done, n + 1)
                        link(V.tensor_reduce(nmax2[:, t, h:h + 1], ps[:, n % 2, :], AX.X, ALU.max))
                        V.tensor_scalar(nmax2[:, t, h:h + 1], nmax2[:, t, h:h + 1], -1.0, None, ALU.mult).then_inc(s2_max, 1)
                    if n >= 1 and (n - 1) % 2 == 0:
                        turned_p2(n - 1)
                    if n >= H2 and n % H2 == 0:
                        head_sum(n // H2 - 1)
                end_of_batch(dve, b)


def layout(inp):
    f = np.float32
    g = {k: np.asarray(v) for k, v in inp.items()}
    n = 2 * SEQ
    m = np.arange(SEQ)[:, None].astype(np.float64) * np.arange(SEQ)[None, :]
    cos, sin = np.cos(2 * np.pi * m / n), np.sin(2 * np.pi * m / n)
    sin[:, 0] = np.cos(np.pi * np.arange(SEQ))
    w = np.where(np.arange(SEQ) == 0, 1.0, 2.0)[:, None] / n
    wv0 = np.zeros((DCTX, H0, V0W), f)
    wv0[:, :, :D0] = g["L0_xattn_Wv"].reshape(DCTX, H0, D0)
    bv0 = np.zeros((H0, V0W), f)
    bv0[:, :D0] = g["L0_xattn_bv"].reshape(H0, D0)
    bv0[:, D0] = 1.0
    fold = np.zeros((P, V0W), f)
    fold[np.arange(P), np.arange(P) % V0W] = 1.0
    max_rows = np.zeros((P, P), np.uint16)
    max_rows[NSPLIT:NSPLIT + 3, :] = 0x3F80
    phase = np.zeros((P, 4), f)
    phase[:NSTATE, 0] = phase[NSTATE:, 1] = np.pi / 2
    phase[:NSTATE, 2] = phase[NSTATE:, 3] = 0.25
    ramp = np.concatenate([np.arange(LB), LB * np.arange(LA)]).astype(f)

    def columns(v):
        return np.ascontiguousarray(v.reshape(-1, P).T)

    return {
        "x": g["x"],
        "ctxT": np.ascontiguousarray(g["ctx_768"].transpose(0, 2, 1)),
        "tmask": np.ascontiguousarray(g["mask_BxS_bf1"].view(np.uint8).reshape(NBATCH, TILES, P).transpose(0, 2, 1)),
        "vmask": np.ascontiguousarray(g["mask_BxS2_bf1"]).view(np.uint8),
        "wq0": g["L0_xattn_Wq"], "wk0": g["L0_xattn_Wk"], "wv0": wv0.reshape(DCTX, H0 * V0W), "wo0": g["L0_xattn_Wo"],
        "bq0": columns(g["L0_xattn_bq"]), "bk0": columns(g["L0_xattn_bk"]), "bv0": bv0.reshape(-1), "bo0": g["L0_xattn_bo"],
        "wg": g["L0_ffn_Wg"], "w11": g["L0_ffn_W11"], "w12": g["L0_ffn_W12"], "w2e": g["L0_ffn_W2"],
        "wq1": g["L1_xattn_Wq"], "wk1": g["L1_xattn_Wk"], "wv1": g["L1_xattn_Wv"],
        "film_w": np.stack([g["L1_xattn_W_film_in"], g["L1_xattn_W_film_out"]]),
        "film_b": np.stack([g["L1_xattn_b_film_in"], g["L1_xattn_b_film_out"]]),
        "norm_g": np.stack([g["L1_xattn_g_norm_in"], g["L1_xattn_g_ffn"], g["L1_xattn_g_norm_out"]]),
        "norm_b": np.stack([g["L1_xattn_b_norm_in"], g["L1_xattn_b_ffn"], g["L1_xattn_b_norm_out"]]),
        "wf1": g["L1_xattn_W1"], "b1": columns(g["L1_xattn_b1"]), "wf2": g["L1_xattn_W2"], "b2": g["L1_xattn_b2"],
        "log_dt": g["L1_xattn_log_dt"],
        "s4d": np.stack([np.ascontiguousarray(g["L1_xattn_" + k].T) for k in ("A_re", "A_im", "C_re", "C_im")]),
        "d_skip": g["L1_xattn_D_skip"], "mod_gate": g["L1_xattn_mod_gate"].reshape(1),
        "wq2": np.ascontiguousarray(g["L1_ffn_Wq"].reshape(H2 * D2, DIM).T),
        "wk2": np.ascontiguousarray(g["L1_ffn_Wk"].reshape(H2 * D2, DIM).T),
        "wsd": np.concatenate([g["L1_ffn_Ws"].reshape(H2 * E2, DIM).T, g["L1_ffn_Wd"].reshape(H2 * E2, DIM).T], axis=1),
        "wv2": np.ascontiguousarray(g["L1_ffn_Wv"].reshape(E2 * D2, DIM).T),
        "wo2": np.ascontiguousarray(g["L1_ffn_Wo"].transpose(0, 2, 1).reshape(E2 * D2, DIM)),
        "dft": np.concatenate([cos, sin], axis=1).astype(f),
        "idft": np.concatenate([cos.T * w, sin.T * w], axis=0).astype(f),
        "ident": np.eye(P, dtype=f), "fold": fold, "max_rows": max_rows,
        "prio": np.arange(NEXP, 0, -1).astype(f), "phase": phase, "ramp": ramp,
    }


def kernel(**inputs):
    import concourse.bacc as bacc
    from concourse.bass_utils import run_bass_kernel_spmd

    nc = bacc.Bacc("TRN2", target_bir_lowering=False, num_devices=1)
    arrays = {"in_" + k: np.ascontiguousarray(v) for k, v in layout(inputs).items()}
    aps = {k[3:]: nc.dram_tensor(k, v.shape, mybir.dt.from_np(v.dtype), kind="ExternalInput").ap() for k, v in arrays.items()}
    aps["out"] = nc.dram_tensor("out", (NBATCH, SEQ, DIM), F32, kind="ExternalOutput").ap()
    program(nc, aps)
    r = run_bass_kernel_spmd(nc, [arrays], core_ids=[0])
    return r.results[0]["out"]
```

```python
from contextlib import ExitStack

import numpy as np

import concourse.bass as bass
from concourse import mybir

F32 = mybir.dt.float32
BF16 = mybir.dt.bfloat16
U8 = mybir.dt.uint8
I32 = mybir.dt.int32
ALU = mybir.AluOpType
ACT = mybir.ActivationFunctionType
AX = mybir.AxisListType

P = 128
NBATCH, SEQ, DIM = 4, 512, 256
TILES = SEQ // P
DCH = DIM // P
GKEYS, DCTX = 1601, 192
CTXCH = 2
KCH = (GKEYS + P - 1) // P
KW = [min(P, GKEYS - P * k) for k in range(KCH)]
COLS = [(c, min(512, GKEYS - c)) for c in range(0, GKEYS, 512)]
H0, D0 = 16, 16
V0W = 32
CLAMP = 10000.0
BOUND = 64.0
SPLIT_Q = [0, 0, 1, 0, 2, 1]
SPLIT_K = [0, 1, 0, 2, 0, 1]
NSPLIT = len(SPLIT_Q) * D0
NEXP, INNER = 8, 512
ICH = INNER // P
H1, D1, TOPK = 4, 32, 32
DROPPED = -3.4e38
PART = 60
PARTS = [(c, min(PART, GKEYS - c)) for c in range(0, GKEYS, PART)]
MASKED = 3.0e38
NSTATE = 64
LB, LA = 32, 16
FCH = 2 * SEQ // P
HID = 4 * DIM
HCH = HID // P
H2, D2, E2 = 16, 64, 8
TWO_ONES = float(np.array(0x3F803F80, np.uint32).view(np.float32))
MAGIC = 12582912.0
TWO_PI = 6.283185307179586
LN_EPS = 1e-5
ARENA = 37352
CTX_AT = 27232
AFTER_CTX = CTX_AT + 2 * GKEYS + 2


def program(nc, a, dbg=None):
    ctx = ExitStack()
    with ctx:
        def sb(name, shape, dt=F32):
            return ctx.enter_context(nc.sbuf_tensor("sb_" + name, shape, dt))

        sems = []

        def sem(name):
            s = ctx.enter_context(nc.semaphore(name))
            sems.append(s)
            return s

        x = sb("x", [P, TILES, DIM])
        xt = sb("xt", [P, TILES, DIM])
        xn = sb("xn", [P, TILES, DIM])
        xnT = sb("xnT", [P, DCH, SEQ])
        wq0 = sb("wq0", [P, DCH, DIM])
        wk0 = sb("wk0", [P, CTXCH, DIM])
        wv0 = sb("wv0", [P, CTXCH, DIM])
        wo0 = sb("wo0", [P, DCH, DIM])
        bv0 = sb("bv0", [P, DIM])
        bo0 = sb("bo0", [P, DIM])
        bq0 = sb("bq0", [P, DCH])
        bk0 = sb("bk0", [P, DCH])
        wg = sb("wg", [P, DCH, NEXP])
        wq1 = sb("wq1", [P, DCH, H1 * D1])
        wk1 = sb("wk1", [P, CTXCH, H1 * D1])
        wv1 = sb("wv1", [P, CTXCH, DIM])
        film_w = sb("film_w", [P, 2, DCH, 2 * DIM])
        film_b = sb("film_b", [P, 2, 2 * DIM])
        norm_g = sb("norm_g", [P, 3, DIM])
        norm_b = sb("norm_b", [P, 3, DIM])
        b1 = sb("b1", [P, HCH])
        b2 = sb("b2", [P, DIM])
        d_skip = sb("d_skip", [P, DIM])
        mod_gate = sb("mod_gate", [P, 1])
        k_cos = sb("k_cos", [P, FCH // 2, DIM])
        k_sin = sb("k_sin", [P, FCH // 2, DIM])
        k_cos0 = sb("k_cos0", [P, DIM])
        ident = sb("ident", [P, P])
        fold = sb("fold", [P, V0W])
        max_rows = sb("max_rows", [P, P], BF16)
        prio = sb("prio", [P, NEXP])
        phase = sb("phase", [P, 4])
        eps = sb("eps", [P, 1])
        ln_stats = sb("ln_stats", [P, TILES, 6])
        ln_mv = sb("ln_mv", [P, TILES, 2])
        ln_std = sb("ln_std", [P, TILES])
        ln_rstd = sb("ln_rstd", [P, TILES])
        tmask = sb("tmask", [P, TILES])
        tmask8 = sb("tmask8", [P, TILES], U8)
        small = sb("small", [P, 256])
        ones = sb("ones", [P, 1])
        ones_row = sb("ones_row", [1, P], BF16)
        head_sum_w = sb("head_sum_w", [P, DCH, H0])
        norms = sb("norms", [H0, 4])
        bounded = sb("bounded", [H0, 1])
        general = sb("general", [1, 1], I32)
        flag = sb("flag", [1, 1], I32)

        arena = sb("arena", [P, ARENA])

        def at(off, shape, dt=F32):
            n = int(np.prod(shape))
            words = n if dt == F32 else (n + 1) // 2 if dt == BF16 else (n + 3) // 4
            v = arena[:, off:off + words]
            if dt != F32:
                v = v.bitcast(dt)[:, 0:n]
            if len(shape) == 2:
                v = v.rearrange("p (a b) -> p a b", b=shape[1])
            elif len(shape) == 3:
                v = v.rearrange("p (a b c) -> p a b c", b=shape[1], c=shape[2])
            return v

        ps = ctx.enter_context(nc.psum_tensor("ps", [P, 8, 512], F32))

        def wide(bank, n):
            return ps[:, bank:bank + (n + 511) // 512, :].rearrange("p a b -> p (a b)")[:, 0:n]

        ctxT = at(CTX_AT, [CTXCH, GKEYS])
        KPAD = KCH * P
        o = 0
        k_stack = at(o, [H0, KPAD], BF16); o += H0 * KPAD // 2
        q_stack = at(o, [H0, SEQ], BF16); o += H0 * SEQ // 2
        o_tr = o
        v0 = at(o, [KCH, H0 * V0W]); o += KCH * H0 * V0W
        low = at(o, [2, SEQ]); o += 2 * SEQ
        attn0 = at(o, [TILES, DIM]); o += TILES * DIM
        row_max = at(o, [TILES, H0]); o += TILES * H0
        neg_max = at(o, [TILES, H0]); o += TILES * H0
        assert o <= CTX_AT
        o = AFTER_CTX
        probs0 = at(o, [8, SEQ]); o += 8 * SEQ
        o_part = at(o, [2, SEQ]); o += 2 * SEQ
        nm_f = at(o, [SEQ]); o += SEQ
        nm_r = at(o, [SEQ]); o += SEQ
        nm_p = at(o, [3, SEQ], BF16); o += 3 * SEQ // 2
        assert o <= ARENA
        o = 0
        k_f = at(o, [DCH, GKEYS]); o += DCH * GKEYS
        k_r = at(o, [DCH, GKEYS]); o += DCH * GKEYS
        k_sq = at(o, [DCH, GKEYS]); o += DCH * GKEYS
        k_p = at(o, [3, DCH, KPAD], BF16); o += 3 * DCH * KPAD // 2
        q_f = at(o, [DCH, SEQ]); o += DCH * SEQ
        q_r = at(o, [DCH, SEQ]); o += DCH * SEQ
        q_sq = at(o, [DCH, SEQ]); o += DCH * SEQ
        q_p = at(o, [3, DCH, SEQ], BF16); o += 3 * DCH * SEQ // 2
        assert o <= CTX_AT
        o = 0
        w_exp = [at(o + 3072 * i, [3072]) for i in range(2)]; o += 2 * 3072
        w11 = [w[:, 0:1024].rearrange("p (c i) -> p c i", c=DCH) for w in w_exp]
        w12 = [w[:, 1024:2048].rearrange("p (c i) -> p c i", c=DCH) for w in w_exp]
        w2e = [w[:, 2048:3072].rearrange("p (c d) -> p c d", c=ICH) for w in w_exp]
        silu = at(o, [2, SEQ]); o += 2 * SEQ
        fused = at(o, [2, ICH * SEQ]); o += 2 * ICH * SEQ
        gl = at(o, [TILES, NEXP]); o += 32
        g_tmp = [at(o + 32 * i, [TILES, NEXP]) for i in range(6)]; o += 32 * 6
        g_red = [at(o + 8 * i, [TILES]) for i in range(6)]; o += 48
        g_w = at(o, [TILES, NEXP]); o += 32
        o = 0
        KS = 1602
        s_sb = at(o, [3, KS]); o += 3 * KS
        s_cut = at(o, [KS]); o += KS
        kept01 = at(o, [2, KS]); o += 2 * KS
        probs1 = at(o, [3, KS]); o += 3 * KS
        p_mean = at(o, [2, KS]); o += 2 * KS
        attnT = at(o, [KCH, P]); o += KCH * P
        kT1 = at(o, [GKEYS]); o += KS
        v1 = at(o, [KCH, DIM]); o += KCH * DIM
        q1z = at(o, [H1, SEQ]); o += H1 * SEQ
        assert o <= CTX_AT
        o = AFTER_CTX
        cand = at(o, [8 * len(PARTS)]); o += 8 * len(PARTS)
        top = at(o, [2, TOPK]); o += 2 * TOPK
        top_e = at(o, [2, TOPK]); o += 2 * TOPK
        NEG, SUM, WEIGHT = range(3)
        stat1 = at(o, [3, 3]); o += 9
        kept = at(o, [TILES * H1]); o += TILES * H1
        mask8 = at(o, [GKEYS], U8); o += 402
        mask_row = at(o, [GKEYS], BF16); o += 802
        c_tT = at(ARENA - 1024, [DCH, SEQ])
        assert o <= ARENA - 1024
        o = 0
        dft = at(o, [SEQ // P, 2 * SEQ]); o += SEQ // P * 2 * SEQ
        idft = at(o, [FCH, SEQ]); o += FCH * SEQ
        u = at(o, [TILES, DIM]); o += TILES * DIM
        f_in = at(o, [TILES, 2 * DIM]); f_out = at(o + 2048, [TILES, 2 * DIM]); o += 4096
        spec = at(o, [FCH, DIM]); o += FCH * DIM
        ptmp = at(o, [2, 4, DIM]); o += 8 * DIM
        dtmp = at(o, [TILES, DIM]); o += TILES * DIM
        wf1 = at(o, [DCH, HID]); o += DCH * HID
        wf2 = at(o, [HCH, DIM]); o += HCH * DIM
        assert o <= ARENA - 1024 - 6656
        hid = at(0, [HCH, SEQ])
        o = ARENA - 1024 - 6656
        wq2 = at(o, [DCH, H2 * D2]); o += DCH * H2 * D2
        wk2 = at(o, [DCH, H2 * D2]); o += DCH * H2 * D2
        wsd = at(o, [DCH, 2 * H2 * E2]); o += DCH * 2 * H2 * E2
        wv2 = at(o, [DCH, E2 * D2]); o += DCH * E2 * D2
        wo2 = at(o, [E2 * D2 // P, DIM]); o += E2 * D2 // P * DIM
        z = at(o, [E2 * D2]); o += 512
        z_tmp = at(o, [E2 * D2]); o += 512
        assert o == ARENA
        o = 0
        q2z = at(o, [H2, SEQ]); o += H2 * SEQ
        kT2 = at(o, [H2 // 2, SEQ]); o += H2 // 2 * SEQ
        proj_v = at(o, [TILES, E2 * D2]); o += TILES * E2 * D2
        v2 = at(o, [TILES, H2 * D2]); o += TILES * H2 * D2
        NG = TILES * H2
        gate_v = at(o, [NG, E2]); o += NG * E2
        gate_o = at(o, [NG, E2]); o += NG * E2
        sig_v = at(o, [NG, E2]); o += NG * E2
        t_oh1 = at(o, [NG, E2]); o += NG * E2
        t_oh2 = at(o, [NG, E2]); o += NG * E2
        t_a = at(o, [NG, E2]); o += NG * E2
        t_b = at(o, [NG, E2]); o += NG * E2
        t_m = at(o, [NG]); o += NG
        sums2 = at(o, [TILES, H2]); o += NG
        rs2 = at(o, [TILES, H2]); o += NG
        nmax2 = at(o, [TILES, H2]); o += NG
        p2 = at(o, [2, SEQ]); o += 2 * SEQ
        pT2 = at(o, [2, SEQ]); o += 2 * SEQ
        zT = at(o, [E2 * D2]); o += 512
        v_tmp = at(o, [H2 * D2]); o += H2 * D2
        v_tmp2 = at(o, [H2 * D2]); o += H2 * D2
        assert o <= ARENA - 1024 - 6656, o
        o = 0
        NW, NPW = DIM * LB, DIM * LA
        k_w = at(o, [DIM, LB]); o += NW
        s_n = at(o, [NW]); o += NW
        s_x = at(o, [NPW]); o += NPW
        s_y = at(o, [NPW]); o += NPW
        s_t = [at(o + DIM * i, [DIM]) for i in range(18)]; o += 18 * DIM
        ramp = at(o, [LB + LA]); o += LB + LA
        k_time = at(o, [SEQ // P, DIM]); o += SEQ // P * DIM
        dft_s = at(o, [SEQ // P, 2 * SEQ]); o += SEQ // P * 2 * SEQ
        assert o <= ARENA
        k_spill = nc.dram_tensor("k_spill", [NBATCH, 3, DIM, KPAD], BF16).ap()
        q_spill = nc.dram_tensor("q_spill", [NBATCH, 3, DIM, SEQ], BF16).ap()

        consts = ctx.enter_context(nc.semaphore("consts"))
        setup_v = ctx.enter_context(nc.semaphore("setup_v"))
        setup_a = ctx.enter_context(nc.semaphore("setup_a"))
        setup_p = ctx.enter_context(nc.semaphore("setup_p"))
        setup_done = ctx.enter_context(nc.semaphore("setup_done"))
        engine_ended = ctx.enter_context(nc.semaphore("engine_ended"))
        batch_closed = ctx.enter_context(nc.semaphore("batch_closed"))
        batch_opened = ctx.enter_context(nc.semaphore("batch_opened"))
        def once(name):
            return ctx.enter_context(nc.semaphore(name))

        in_x, in_ctx = once("in_x"), once("in_ctx")
        in_var, in_dev, in_xn, in_step = once("in_var"), once("in_dev"), once("in_xn"), once("in_step")
        in_xT_done, in_xT_ready = once("in_xT_done"), once("in_xT_ready")
        in_k_done, in_k_read, in_k_rest, in_k_mid, in_k_parts = (once("in_k_" + n) for n in ("done", "read", "rest", "mid", "parts"))
        in_q_done, in_q_read, in_q_parts = once("in_q_done"), once("in_q_read"), once("in_q_parts")
        in_squares, in_norms_done, in_norms_read = once("in_squares"), once("in_norms_done"), once("in_norms_read")
        in_spilled_k, in_spilled_q = once("in_spilled_k"), once("in_spilled_q")
        bounds_ready, bounds_done, path_known = once("bounds_ready"), once("bounds_done"), once("path_known")
        loaded = sem("loaded")
        pads_ready = sem("pads_ready")
        v_step = sem("v_step")
        ln_var = sem("ln_var")
        ln_dev = sem("ln_dev")
        xn_ready = sem("xn_ready")
        xT_done = sem("xT_done")
        xT_ready = sem("xT_ready")
        v0_pads = sem("v0_pads")
        stacked = [sem("stacked%d" % i) for i in range(4)]
        pair_scores = sem("pair_scores")
        pair_probs = sem("pair_probs")
        group_values = sem("group_values")
        head_out = sem("head_out")
        head_turned = sem("head_turned")
        head_step = sem("head_step")
        general_step = sem("general_step")
        v0_done = sem("v0_done")
        v0_ready = sem("v0_ready")
        s0_ready = sem("s0_ready")
        s0_read = sem("s0_read")
        nmax_ready = sem("nmax_ready")
        nmaxT_done = sem("nmaxT_done")
        nmax_parts = sem("nmax_parts")
        nmax_stacked = sem("nmax_stacked")
        low_done = sem("low_done")
        low_ready = sem("low_ready")
        t0_ready = sem("t0_ready")
        t0_clipped = sem("t0_clipped")
        p0_ready = sem("p0_ready")
        pv0_done = sem("pv0_done")
        o0_ready = sem("o0_ready")
        o0_turned = sem("o0_turned")
        attn0_ready = sem("attn0_ready")
        y0_done = sem("y0_done")
        x1_ready = sem("x1_ready")
        gl_done = sem("gl_done")
        gl_ready = sem("gl_ready")
        g_exp = sem("g_exp")
        w_loaded = [sem("w_loaded0"), sem("w_loaded1")]
        gv_done = sem("gv_done")
        silu_ready = sem("silu_ready")
        fused_ready = sem("fused_ready")
        down_done = sem("down_done")
        down_read = sem("down_read")
        c_done = sem("c_done")
        c_ready = sem("c_ready")
        q1_clear = sem("q1_clear")
        q1_done = sem("q1_done")
        q1_ready = sem("q1_ready")
        s1_done = sem("s1_done")
        s1_ready = sem("s1_ready")
        top_ready = sem("top_ready")
        e1_ready = sem("e1_ready")
        sum1_ready = sem("sum1_ready")
        p1_ready = sem("p1_ready")
        count_ready = sem("count_ready")
        count_done = sem("count_done")
        flag_ready = sem("flag_ready")
        w1_ready = sem("w1_ready")
        p1_kept = sem("p1_kept")
        p1_scaled = sem("p1_scaled")
        p1_added = sem("p1_added")
        aT_done = sem("aT_done")
        aT_ready = sem("aT_ready")
        ctx_done = sem("ctx_done")
        mask_ready = sem("mask_ready")
        ctx_ready = sem("ctx_ready")
        w_late = sem("w_late")
        film_done = sem("film_done")
        film_read = sem("film_read")
        u_ready = sem("u_ready")
        spec_done = sem("spec_done")
        spec_ready = sem("spec_ready")
        y1_done = sem("y1_done")
        xt2_ready = sem("xt2_ready")
        h_done = sem("h_done")
        h_ready = sem("h_ready")
        f_done = sem("f_done")
        f_read = sem("f_read")
        x3_ready = sem("x3_ready")
        q2_clear = sem("q2_clear")
        qk2_done = sem("qk2_done")
        qk2_ready = sem("qk2_ready")
        g2_done = sem("g2_done")
        g2_read = sem("g2_read")
        sig_ready = sem("sig_ready")
        pv_done = sem("pv_done")
        pv_ready = sem("pv_ready")
        mix_ready = sem("mix_ready")
        v2_ready = sem("v2_ready")
        v2_ready_p = sem("v2_ready_p")
        p_step = sem("p_step")
        s2_done = sem("s2_done")
        s2_max = sem("s2_max")
        p2_ready = sem("p2_ready")
        p2T_done = sem("p2T_done")
        p2T_act = sem("p2T_act")
        p2T_dve = sem("p2T_dve")
        o2_done = sem("o2_done")
        z_ready = sem("z_ready")
        zT_done = sem("zT_done")
        zT_ready = sem("zT_ready")
        r_done = sem("r_done")
        out_ready = sem("out_ready")
        stored = sem("stored")

        NLOADS = []

        block = ctx.enter_context(nc.Block())

        @block.sync
        def _(sp):
            def const(dst, src):
                sp.dma_start(dst, src).then_inc(consts, 16)
                NLOADS.append(1)

            def bcast(dst, src):
                const(dst, src.partition_broadcast(P))

            for i, name in enumerate(["A_re", "A_im", "C_re", "C_im"]):
                for half in range(2):
                    const(s_t[i][half * NSTATE:(half + 1) * NSTATE, :], a["s4d"][i])
            bcast(s_t[4][:, :], a["log_dt"])
            bcast(ramp[:, :], a["ramp"])
            const(phase[:, :], a["phase"])
            const(dft_s[:, :, :], a["dft"].rearrange("(c p) f -> p c f", p=P))
            const(ident[:, :], a["ident"])
            const(fold[:, :], a["fold"])
            const(head_sum_w[:, :, :], a["head_sum_w"].rearrange("(c p) n -> p c n", p=P))
            const(max_rows[:, :].bitcast(mybir.dt.uint16), a["max_rows"])
            bcast(prio[:, :], a["prio"])
            const(wq0[:, :, :], a["wq0"].rearrange("(c p) n -> p c n", p=P))
            const(wk0[:, :, :], a["wk0"].rearrange("(c p) n -> p c n", p=P))
            const(wv0[:, :, :], a["wv0"].rearrange("(c p) n -> p c n", p=P))
            const(wo0[:, :, :], a["wo0"].rearrange("(c p) n -> p c n", p=P))
            bcast(bv0[:, :], a["bv0"])
            bcast(bo0[:, :], a["bo0"])
            const(bq0[:, :], a["bq0"])
            const(bk0[:, :], a["bk0"])
            const(wg[:, :, :], a["wg"].rearrange("(c p) n -> p c n", p=P))
            const(wq1[:, :, :], a["wq1"].rearrange("(c p) n -> p c n", p=P))
            const(wk1[:, :, :], a["wk1"].rearrange("(c p) n -> p c n", p=P))
            const(wv1[:, :, :], a["wv1"].rearrange("(c p) n -> p c n", p=P))
            for i in range(2):
                const(film_w[:, i, :, :], a["film_w"][i].rearrange("(c p) n -> p c n", p=P))
                bcast(film_b[:, i, :], a["film_b"][i])
            for i in range(3):
                bcast(norm_g[:, i, :], a["norm_g"][i])
                bcast(norm_b[:, i, :], a["norm_b"][i])
            const(b1[:, :], a["b1"])
            bcast(b2[:, :], a["b2"])
            bcast(d_skip[:, :], a["d_skip"])
            bcast(mod_gate[:, :], a["mod_gate"])
            sp.wait_ge(setup_done, 1)

            with sp.Fori(0, NBATCH) as b:
                sp.wait_ge(in_xn, TILES * b)
                sp.dma_start(x[:, :, :], a["x"][b].rearrange("(t p) d -> p t d", p=P)).then_inc(in_x, 16)
                sp.wait_ge(in_k_done, DCH * len(COLS) * b)
                sp.dma_start(ctxT[:, :, :], a["ctxT"][b].rearrange("(c p) k -> p c k", p=P)).then_inc(in_ctx, 16)
                sp.wait_ge(in_q_parts, b + 1)
                for i in range(3):
                    sp.dma_start(q_spill[b, i].rearrange("(c p) k -> p c k", p=P), q_p[:, i, :, :]).then_inc(in_spilled_q, 16)
                sp.wait_ge(in_k_parts, DCH * b + DCH)
                for i in range(3):
                    sp.dma_start(k_spill[b, i].rearrange("(c p) k -> p c k", p=P), k_p[:, i, :, :]).then_inc(in_spilled_k, 16)
            sp.wait_ge(in_spilled_q, 48 * NBATCH)
            sp.wait_ge(in_spilled_k, 48 * NBATCH)
            sp.wait_ge(path_known, 1)

            with sp.Fori(0, NBATCH) as b:
                sp.dma_start(ctxT[:, :, :], a["ctxT"][b].rearrange("(c p) k -> p c k", p=P)).then_inc(loaded, 16)
                sp.dma_start(x[:, :, :], a["x"][b].rearrange("(t p) d -> p t d", p=P)).then_inc(loaded, 16)
                sp.dma_start(tmask8[:, :], a["tmask"][b].rearrange("p t -> p t")).then_inc(loaded, 16)
                for g in range(4):
                    hs = slice(4 * g, 4 * g + 4)
                    rows = slice(4 * g * D0, (4 * g + 4) * D0)
                    for i, part in enumerate(SPLIT_K):
                        sp.dma_start(k_stack[i * D0:(i + 1) * D0, hs, :],
                                     k_spill[b, part, rows].rearrange("(h d) k -> d h k", d=D0)).then_inc(stacked[g], 16)
                    for i, part in enumerate(SPLIT_Q):
                        sp.dma_start(q_stack[i * D0:(i + 1) * D0, hs, :],
                                     q_spill[b, part, rows].rearrange("(h d) k -> d h k", d=D0)).then_inc(stacked[g], 16)

                for e in range(NEXP):
                    if e == 0:
                        sp.wait_ge(attn0_ready, H0)
                        sp.dma_start(mask8[0:1, :], a["vmask"][b].unsqueeze(0)).then_inc(loaded, 16)
                    if e >= 2:
                        sp.wait_ge(down_done, TILES * (e - 1))
                    sp.dma_start(w11[e % 2], a["w11"][e].rearrange("(c p) n -> p c n", p=P)).then_inc(w_loaded[e % 2], 16)
                    sp.dma_start(w12[e % 2], a["w12"][e].rearrange("(c p) n -> p c n", p=P)).then_inc(w_loaded[e % 2], 16)
                    sp.dma_start(w2e[e % 2], a["w2e"][e].rearrange("(c p) n -> p c n", p=P)).then_inc(w_loaded[e % 2], 16)

                sp.wait_ge(down_done, TILES * NEXP)
                sp.wait_ge(ctx_done, TILES)
                sp.wait_ge(p1_added, TILES * (H1 - 1))
                sp.wait_ge(w1_ready, TILES * H1)
                sp.dma_start(dft[:, :, :], a["dft"].rearrange("(c p) f -> p c f", p=P)).then_inc(w_late, 16)
                sp.dma_start(idft[:, :, :], a["idft"].rearrange("(c p) f -> p c f", p=P)).then_inc(w_late, 16)
                sp.dma_start(wf1[:, :, :], a["wf1"].rearrange("(c p) f -> p c f", p=P)).then_inc(w_late, 16)
                sp.dma_start(wf2[:, :, :], a["wf2"].rearrange("(c p) f -> p c f", p=P)).then_inc(w_late, 16)
                sp.dma_start(wq2[:, :, :], a["wq2"].rearrange("(c p) f -> p c f", p=P)).then_inc(w_late, 16)
                sp.dma_start(wk2[:, :, :], a["wk2"].rearrange("(c p) f -> p c f", p=P)).then_inc(w_late, 16)
                sp.dma_start(wsd[:, :, :], a["wsd"].rearrange("(c p) f -> p c f", p=P)).then_inc(w_late, 16)
                sp.dma_start(wv2[:, :, :], a["wv2"].rearrange("(c p) f -> p c f", p=P)).then_inc(w_late, 16)
                sp.dma_start(wo2[:, :, :], a["wo2"].rearrange("(c p) f -> p c f", p=P)).then_inc(w_late, 16)

                for t in range(TILES):
                    sp.wait_ge(out_ready, t + 1)
                    sp.dma_start(a["out"][b].rearrange("(t p) d -> p t d", p=P)[:, t, :], x[:, t, :]).then_inc(stored, 16)
                if dbg is not None:
                    pass
                sp.wait_ge(stored, 16 * TILES)

                sp.wait_ge(engine_ended, 4 * b + 4)
                sp.sem_inc(batch_closed, 1)
                for s in sems:
                    sp.sem_clear(s)
                sp.sem_inc(batch_opened, 1)

        def end_of_batch(eng, b):
            eng.drain().then_inc(engine_ended, 1)
            eng.wait_ge(batch_opened, b + 1)

        def as_words(v):
            return v.rearrange("p a b -> p (a b)").bitcast(F32)

        @block.gpsimd
        def _(pool):
            G = nc.gpsimd
            pool.wait_ge(setup_done, 1)
            with pool.Fori(0, NBATCH) as b:
                pool.wait_ge(in_norms_done, 2 * b)
                pool.wait_ge(in_q_read, b + 1)
                G.tensor_tensor(q_sq, q_f, q_f, ALU.mult).then_inc(in_squares, 1)
                pool.wait_ge(in_k_read, DCH * b + DCH)
                G.tensor_tensor(k_sq, k_f, k_f, ALU.mult).then_inc(in_squares, 1)
            pool.wait_ge(path_known, 1)
            pool.wait_ge(in_spilled_q, 48 * NBATCH)
            pool.wait_ge(in_spilled_k, 48 * NBATCH)

            with pool.Fori(0, NBATCH) as b:
                vpad = v0.rearrange("p k (h w) -> p k h w", w=V0W)
                G.memset(v0, 0.0).then_inc(v0_pads, 1)
                pool.wait_ge(v0_pads, 1)
                G.memset(vpad[:, 0:KCH - 1, :, D0:D0 + 1], 1.0).then_inc(v0_pads, 1)
                G.memset(vpad[0:KW[-1], KCH - 1, :, D0:D0 + 1], 1.0).then_inc(v0_pads, 1)
                pool.wait_ge(down_read, TILES * NEXP)
                pool.wait_ge(fused_ready, ICH * NEXP)
                G.memset(q1z[:, :, :], 0.0).then_inc(q1_clear, 1)
                def add_head(n):
                    t, h = n // H1, n % H1
                    if h:
                        mean = p_mean[:, t % 2, 0:GKEYS]
                        pool.wait_ge(p1_scaled, n + 1)
                        if n > 1:
                            pool.wait_ge(p1_added, n - 1 - t)
                        G.tensor_tensor(mean, mean, probs1[:, n % 3, 0:GKEYS], ALU.add).then_inc(p1_added, 1)

                for n in range(TILES * H1):
                    e = probs1[:, n % 3, 0:GKEYS]
                    pool.wait_ge(e1_ready, n + 1)
                    pool.wait_ge(w1_ready, n + 1)
                    G.tensor_tensor(e, e, kept01[:, n % 2, 0:GKEYS], ALU.mult).then_inc(p1_kept, 1)
                    if n >= 1:
                        add_head(n - 1)
                add_head(TILES * H1 - 1)
                pool.wait_ge(f_done, TILES)
                nc.gpsimd.memset(q2z[0:D2, 1:H2:2, :], 0.0).then_inc(q2_clear, 1)
                nc.gpsimd.memset(q2z[D2:P, 0:H2:2, :], 0.0).then_inc(q2_clear, 1)
                pool.wait_ge(mix_ready, 1)
                pool.wait_ge(pv_ready, TILES)
                t = TILES - 1
                k = 0
                for e in range(E2):
                    src = proj_v[:, t, e * D2:(e + 1) * D2].unsqueeze(1).to_broadcast([P, H2, D2])
                    mix = t_b[:, t * H2:(t + 1) * H2, e].unsqueeze(2).to_broadcast([P, H2, D2])
                    dst = v2[:, t, :] if e == 0 else v_tmp2
                    nc.gpsimd.tensor_tensor(dst.rearrange("p (h d) -> p h d", d=D2), src, mix, ALU.mult).then_inc(p_step, 1)
                    k += 1
                    pool.wait_ge(p_step, k)
                    if e:
                        nc.gpsimd.tensor_tensor(v2[:, t, :], v2[:, t, :], v_tmp2, ALU.add).then_inc(p_step, 1)
                        k += 1
                        pool.wait_ge(p_step, k)
                pool.drain().then_inc(v2_ready_p, 1)
                end_of_batch(pool, b)

        def attn_turned(act, A, t):
            if t >= 1:
                act.wait_ge(ctx_done, t)
            for j in range(4):
                act.wait_ge(aT_done, 4 * t + j + 1)
                k0, k1 = 4 * j, min(4 * j + 4, KCH)
                if k1 == KCH and KW[-1] < P:
                    A(attnT[0:KW[-1], KCH - 1, :], ps[0:KW[-1], 4 + j, (KCH - 1 - k0) * P:(KCH - k0) * P],
                      ACT.Copy).then_inc(aT_ready, 1)
                    k1 -= 1
                if k1 > k0:
                    A(attnT[:, k0:k1, :], ps[:, 4 + j, 0:(k1 - k0) * P].rearrange("p (k q) -> p k q", q=P),
                      ACT.Copy).then_inc(aT_ready, 1)

        @block.scalar
        def _(act):
            A = nc.scalar.activation
            act.wait_ge(setup_v, 1)
            A(s_t[5], s_t[4], ACT.Exp).then_inc(setup_a, 1)
            act.wait_ge(setup_v, 2)
            A(s_t[8], s_t[6], ACT.Exp).then_inc(setup_a, 1)
            act.wait_ge(setup_v, 3)
            A(s_t[9], s_t[9], ACT.Sin).then_inc(setup_a, 1)
            A(s_t[10], s_t[10], ACT.Sin).then_inc(setup_a, 1)
            act.wait_ge(setup_v, 4)
            A(k_w.rearrange("p a b -> p (a b)"), k_w.rearrange("p a b -> p (a b)"), ACT.Sin).then_inc(setup_a, 1)
            act.wait_ge(setup_v, 5)
            A(s_n, s_n, ACT.Exp).then_inc(setup_a, 1)
            act.wait_ge(setup_v, 6)
            A(s_x, s_x, ACT.Sin).then_inc(setup_a, 1)
            act.wait_ge(setup_v, 7)
            A(s_y, s_y, ACT.Sin).then_inc(setup_a, 1)
            act.wait_ge(setup_v, 8)
            A(s_n[:, 0:NPW], s_n[:, 0:NPW], ACT.Exp).then_inc(setup_a, 1)
            act.wait_ge(setup_done, 1)

            with act.Fori(0, NBATCH) as b:
                act.wait_ge(in_spilled_k, 48 * b)
                act.wait_ge(in_spilled_q, 48 * b)
                act.wait_ge(in_k_parts, DCH * b)
                act.wait_ge(in_squares, 2 * b)
                n = 0
                for g in range(DCH):
                    for c0, w in COLS:
                        act.wait_ge(in_k_done, DCH * len(COLS) * b + n + 1)
                        A(k_f[:, g, c0:c0 + w], ps[:, n % 4, 0:w], ACT.Identity, bias=bk0[:, g:g + 1])
                        ins = A(k_p[:, 0, g, c0:c0 + w], ps[:, n % 4, 0:w], ACT.Identity, bias=bk0[:, g:g + 1])
                        n += 1
                    ins.then_inc(in_k_read, 1)
                    if g == 0:
                        act.wait_ge(in_var, TILES * b + TILES)
                        A(ln_std[:, :], ln_mv[:, :, 1], ACT.Sqrt, bias=eps[:, 0:1]).then_inc(in_dev, 1)
                for c in range(DCH):
                    act.wait_ge(in_xT_done, DCH * b + c + 1)
                    A(xnT[:, c, :], ps[:, 4 + c, :], ACT.Copy).then_inc(in_xT_ready, 1)
                for g in range(DCH):
                    act.wait_ge(in_k_rest, DCH * b + g + 1)
                    A(k_p[:, 1, g, 0:GKEYS], k_r[:, g, :], ACT.Copy).then_inc(in_k_mid, 1)
                act.wait_ge(in_q_done, b + 1)
                for g in range(DCH):
                    A(q_f[:, g, :], ps[:, 6 + g, :], ACT.Identity, bias=bq0[:, g:g + 1], scale=D0 ** -0.5)
                    ins = A(q_p[:, 0, g, :], ps[:, 6 + g, :], ACT.Identity, bias=bq0[:, g:g + 1], scale=D0 ** -0.5)
                ins.then_inc(in_q_read, 1)
            act.wait_ge(path_known, 1)
            use_general = act.value_load(general[0:1, 0:1], min_val=0, max_val=1)

            def attend_bounded():
                for m in range(H0 * KCH // 2):
                    act.wait_ge(pair_scores, m + 1)
                    if m >= 4:
                        act.wait_ge(group_values, m // 2 - 1)
                    A(probs0[:, 2 * (m % 4):2 * (m % 4) + 2, :], ps[:, 2 * (m % 2):2 * (m % 2) + 2, :], ACT.Exp).then_inc(pair_probs, 1)

            def attend_general():
                act.wait_ge(nmax_parts, 1)
                for i in range(3):
                    act.dma_start(q_stack[NSPLIT + i:NSPLIT + i + 1, :, :], nm_p[0:H0, i, :]).then_inc(nmax_stacked, 16)
                for h in range(H0):
                    for k in range(KCH):
                        n = h * KCH + k
                        act.wait_ge(t0_clipped, n + 1)
                        A(probs0[0:KW[k], n % 4, :], probs0[0:KW[k], n % 4, :], ACT.Exp).then_inc(p0_ready, 1)
                        if h >= 1 and k == 2:
                            act.wait_ge(pv0_done, h * KCH)
                            if h >= 3:
                                act.wait_ge(o0_turned, h - 2)
                            A(o_part[:, (h - 1) % 2, :], ps[:, 4 + (h - 1) % 2, :], ACT.Copy).then_inc(o0_ready, 1)
                act.wait_ge(pv0_done, H0 * KCH)
                act.wait_ge(o0_turned, H0 - 2)
                A(o_part[:, (H0 - 1) % 2, :], ps[:, 4 + (H0 - 1) % 2, :], ACT.Copy).then_inc(o0_ready, 1)

            with act.Fori(0, NBATCH) as b:
                n_ln = [0]
                n_xT = [0]

                def deviation():
                    n_ln[0] += 1
                    act.wait_ge(ln_var, TILES * n_ln[0])
                    A(ln_std[:, :], ln_mv[:, :, 1], ACT.Sqrt, bias=eps[:, 0:1]).then_inc(ln_dev, 1)

                def turned():
                    for c in range(DCH):
                        n_xT[0] += 1
                        act.wait_ge(xT_done, n_xT[0])
                        A(xnT[:, c, :], ps[:, 4 + c, :], ACT.Copy).then_inc(xT_ready, 1)

                with act.If(use_general != 0):
                    attend_general()
                with act.Else():
                    attend_bounded()
                turned()

                deviation()
                turned()
                act.wait_ge(gl_ready, 1)
                A(g_tmp[5], g_tmp[4], ACT.Exp).then_inc(g_exp, 1)
                for n in range(NEXP * ICH):
                    act.wait_ge(gv_done, n + 1)
                    if n >= 2:
                        act.wait_ge(fused_ready, n - 1)
                    A(silu[:, n % 2, :], ps[:, 2 * (n % 2), :], ACT.Silu).then_inc(silu_ready, 1)

                for n, (c0, w) in enumerate(COLS):
                    act.wait_ge(c_done, n + 1)
                    A(kT1[:, c0:c0 + w], ps[:, n % 4, 0:w], ACT.Copy).then_inc(c_ready, 1)
                for k in range(KCH):
                    n = len(COLS) + k
                    act.wait_ge(c_done, n + 1)
                    A(v1[0:KW[k], k, :], ps[0:KW[k], n % 4, 0:DIM], ACT.Copy).then_inc(c_ready, 1)
                deviation()
                turned()
                act.wait_ge(q1_clear, 1)
                act.wait_ge(q1_done, 1)
                for h in range(H1):
                    r = slice(h * D1, (h + 1) * D1)
                    A(q1z[r, h, :], ps[r, 6, :], ACT.Copy, scale=float(np.float32(1) / np.sqrt(np.float32(D1)))).then_inc(q1_ready, 1)
                def score_out(n):
                    act.wait_ge(s1_done, n + 1)
                    if n >= 3:
                        act.wait_ge(w1_ready, n - 2)
                    A(s_sb[:, n % 3, 0:GKEYS], wide(0, GKEYS), ACT.Copy).then_inc(s1_ready, 1)

                def context_out(t):
                    act.wait_ge(ctx_done, t + 1)
                    A(c_tT[:, :, t * P:(t + 1) * P], ps[:, 7, P:P + DCH * P].rearrange("p (c q) -> p c q", q=P), ACT.Copy).then_inc(ctx_ready, 1)

                def probs_used(n):
                    if n % H1:
                        act.wait_ge(p1_added, n - n // H1)
                    else:
                        act.wait_ge(p1_scaled, n + 1)

                def scale_head(n):
                    t = n // H1
                    act.wait_ge(p1_kept, n + 1)
                    act.wait_ge(w1_ready, n + 1)
                    if n % H1 == 0 and t >= 2:
                        act.wait_ge(aT_done, 4 * (t - 1))
                    p = probs1[:, n % 3, 0:GKEYS]
                    A(p if n % H1 else p_mean[:, t % 2, 0:GKEYS], p, ACT.Copy, scale=stat1[:, n % 3, WEIGHT:WEIGHT + 1]).then_inc(p1_scaled, 1)

                score_out(0)
                for n in range(TILES * H1):
                    if n + 1 < TILES * H1:
                        score_out(n + 1)
                    if n % H1 == 2 and n > H1:
                        attn_turned(act, A, n // H1 - 1)
                    if n % H1 == 3 and n > H1:
                        context_out(n // H1 - 1)
                    act.wait_ge(top_ready, n + 1)
                    if n >= 3:
                        probs_used(n - 3)
                    bias = stat1[:, n % 3, NEG:NEG + 1]
                    A(probs1[:, n % 3, 0:GKEYS], s_sb[:, n % 3, 0:GKEYS], ACT.Exp, bias=bias).then_inc(e1_ready, 1)
                    A(top_e[:, n % 2, :], top[:, n % 2, :], ACT.Exp, bias=bias,
                      accum_out=stat1[:, n % 3, SUM:SUM + 1]).then_inc(sum1_ready, 1)
                    if n >= 1:
                        scale_head(n - 1)
                scale_head(TILES * H1 - 1)
                attn_turned(act, A, TILES - 1)
                context_out(TILES - 1)
                deviation()
                deviation()
                turned()
                for i in range(HCH):
                    act.wait_ge(h_done, i + 1)
                    A(hid[:, i, :], ps[:, i % 4, :], ACT.Gelu, bias=b1[:, i:i + 1]).then_inc(h_ready, 1)
                deviation()
                deviation()
                turned()
                act.wait_ge(q2_clear, 2)
                for i in range(H2 // 2):
                    act.wait_ge(qk2_done, 2 * i + 1)
                    for j in range(2):
                        r = slice(j * D2, (j + 1) * D2)
                        ins = A(q2z[r, 2 * i + j, :], ps[r, (2 * i) % 4, :], ACT.Copy, scale=D2 ** -0.5)
                    ins.then_inc(qk2_ready, 1)
                    act.wait_ge(qk2_done, 2 * i + 2)
                    A(kT2[:, i, :], ps[:, (2 * i + 1) % 4, :], ACT.Copy).then_inc(qk2_ready, 1)
                for t in range(TILES):
                    act.wait_ge(pv_done, t + 1)
                    A(proj_v[:, t, :], ps[:, t, :], ACT.Copy).then_inc(pv_ready, 1)
                act.wait_ge(g2_read, 1)
                A(sig_v, gate_v, ACT.Sigmoid).then_inc(sig_ready, 1)
                for n in range(NG + 1):
                    if n < NG:
                        t, h = n // H2, n % H2
                        act.wait_ge(s2_max, n + 1)
                        if n >= 2:
                            act.wait_ge(p2T_done, n - 1)
                        A(p2[:, n % 2, :], ps[:, n % 2, :], ACT.Exp, bias=nmax2[:, t, h:h + 1],
                          accum_out=sums2[:, t, h:h + 1]).then_inc(p2_ready, 1)
                    if n >= 1 and (n - 1) % 2 == 1:
                        m = n - 1
                        act.wait_ge(p2T_done, m + 1)
                        if m >= 2:
                            act.wait_ge(o2_done, m - 1)
                        A(pT2[:, m % 2, :], ps[:, 2 + m % 2, :], ACT.Copy).then_inc(p2T_act, 1)
                end_of_batch(act, b)

        @block.tensor
        def _(pe):
            mm, tr = nc.tensor.matmul, nc.tensor.transpose
            pe.wait_ge(setup_v, 9)
            kw_p = s_x.rearrange("p (d a) -> p d a", a=LA)
            for d in range(DIM):
                for j in range(4):
                    ins = mm(ps[32 * j:32 * j + 32, d // P, 4 * (d % P):4 * (d % P) + 4], k_w[:, d, :], kw_p[:, d, j::4],
                             start=True, stop=True)
            ins.then_inc(setup_p, 1)
            pe.wait_ge(setup_v, 10)
            for j in range(FCH):
                for c in range(SEQ // P):
                    ins = mm(ps[:, 2 + j // 2, (j % 2) * DIM:(j % 2 + 1) * DIM], dft_s[:, c, j * P:(j + 1) * P], k_time[:, c, :],
                             start=(c == 0), stop=(c == SEQ // P - 1))
            ins.then_inc(setup_p, 1)
            pe.wait_ge(setup_done, 1)

            with pe.Fori(0, NBATCH) as b:
                pe.wait_ge(in_ctx, 16 * b + 16)
                pe.wait_ge(in_norms_read, 2 * b)
                n = 0
                for g in range(DCH):
                    if g:
                        pe.wait_ge(in_k_read, DCH * b + g)
                    for c0, w in COLS:
                        for c in range(CTXCH):
                            ins = mm(ps[:, n % 4, 0:w], wk0[:, c, g * P:(g + 1) * P], ctxT[:, c, c0:c0 + w],
                                     start=(c == 0), stop=(c == CTXCH - 1))
                        ins.then_inc(in_k_done, 1)
                        n += 1
                pe.wait_ge(in_xn, TILES * b + TILES)
                for c in range(DCH):
                    for t in range(TILES):
                        ins = tr(ps[:, 4 + c, t * P:(t + 1) * P], xn[:, t, c * P:(c + 1) * P], ident[:, :])
                    ins.then_inc(in_xT_done, 1)
                pe.wait_ge(in_xT_ready, DCH * b + DCH)
                for g in range(DCH):
                    for c in range(DCH):
                        ins = mm(ps[:, 6 + g, :], wq0[:, c, g * P:(g + 1) * P], xnT[:, c, :], start=(c == 0), stop=(c == DCH - 1))
                ins.then_inc(in_q_done, 1)
                pe.wait_ge(in_squares, 2 * b + 1)
                for g in range(DCH):
                    ins = mm(ps[0:H0, 4, :], head_sum_w[:, g, :], q_sq[:, g, :], start=(g == 0), stop=(g == DCH - 1))
                ins.then_inc(in_norms_done, 1)
                pe.wait_ge(in_squares, 2 * b + 2)
                pe.wait_ge(in_k_read, DCH * b + DCH)
                for j, (c0, w) in enumerate(COLS):
                    for g in range(DCH):
                        ins = mm(ps[0:H0, j, 0:w], head_sum_w[:, g, :], k_sq[:, g, c0:c0 + w], start=(g == 0), stop=(g == DCH - 1))
                ins.then_inc(in_norms_done, 1)
            pe.wait_ge(bounds_ready, 1)
            mm(ps[0:1, 4, 0:1], bounded[:, :], ones[0:H0, :], start=True, stop=True).then_inc(bounds_done, 1)
            pe.wait_ge(path_known, 1)
            use_general = pe.value_load(general[0:1, 0:1], min_val=0, max_val=1)

            def attend_bounded():
                NCK = H0 * KCH

                def pair(m):
                    if m >= 2:
                        pe.wait_ge(pair_probs, m - 1)
                    for i in range(2):
                        n = 2 * m + i
                        h, k = n // KCH, n % KCH
                        if k == 0 and h % 4 == 0:
                            pe.wait_ge(stacked[h // 4], 32 * NSPLIT // D0)
                        ins = mm(ps[:, 2 * (m % 2) + i, :], k_stack[0:NSPLIT, h, k * P:(k + 1) * P], q_stack[0:NSPLIT, h, :],
                                 start=True, stop=True)
                    ins.then_inc(pair_scores, 1)

                def group(g):
                    pe.wait_ge(pair_probs, 2 * g + 2)
                    for n in range(4 * g, 4 * g + 4):
                        h, k = n // KCH, n % KCH
                        j = n % 4
                        if k == 0 and h >= 2:
                            pe.wait_ge(head_out, h - 1)
                        ins = mm(ps[32 * j:32 * j + 32, 4 + h % 2, :], v0[:, k, h * V0W:(h + 1) * V0W], probs0[:, n % 8, :],
                                 start=(k < 4), stop=(k >= KCH - 4))
                    ins.then_inc(group_values, 1)

                def turn(h):
                    pe.wait_ge(head_out, h + 1)
                    if h >= 2:
                        pe.wait_ge(attn0_ready, h - 1)
                    for t in range(TILES):
                        ins = mm(ps[:, 6 + h % 2, t * V0W:(t + 1) * V0W], o_part[:, h % 2, t * P:(t + 1) * P],
                                 fold[:, :], start=True, stop=True)
                    ins.then_inc(head_turned, 1)

                pair(0)
                pair(1)
                turned = 0
                for g in range(NCK // 4):
                    if g + 1 < NCK // 4:
                        pair(2 * g + 2)
                        pair(2 * g + 3)
                    group(g)
                    if 4 * (g - 1) >= KCH * (turned + 1):
                        turn(turned)
                        turned += 1
                for h in range(turned, H0):
                    turn(h)

            def attend_general():
                for g in range(4):
                    pe.wait_ge(stacked[g], 32 * NSPLIT // D0)
                for n in range(H0 * TILES):
                    h, t = n // TILES, n % TILES
                    if n >= 2:
                        pe.wait_ge(s0_read, n - 1)
                    for j, (c0, w) in enumerate(COLS):
                        ins = mm(ps[:, 4 * (n % 2) + j, 0:w], q_stack[0:NSPLIT, h, t * P:(t + 1) * P],
                                 k_stack[0:NSPLIT, h, c0:c0 + w], start=True, stop=True)
                    ins.then_inc(s0_ready, 1)
                pe.wait_ge(nmax_ready, 1)
                for t in range(TILES):
                    ins = tr(ps[0:H0, 0, t * P:(t + 1) * P], neg_max[:, t, :], ident[:, :])
                ins.then_inc(nmaxT_done, 1)
                pe.wait_ge(nmax_stacked, 48)
                pe.wait_ge(pads_ready, 3)

                def value_product(n):
                    h, k = n // KCH, n % KCH
                    j = k % 4
                    pe.wait_ge(p0_ready, n + 1)
                    if k == 0 and h >= 2:
                        pe.wait_ge(o0_ready, h - 1)
                    mm(ps[32 * j:32 * j + 32, 4 + h % 2, :], v0[0:KW[k], k, h * V0W:(h + 1) * V0W], probs0[0:KW[k], n % 4, :],
                       start=(k < 4), stop=(k >= KCH - 4)).then_inc(pv0_done, 1)

                def turn_head(h):
                    pe.wait_ge(o0_ready, h + 1)
                    if h >= 4:
                        pe.wait_ge(attn0_ready, h - 3)
                    for t in range(TILES):
                        ins = mm(ps[:, 7, (h % 4) * P + t * V0W:(h % 4) * P + (t + 1) * V0W], o_part[:, h % 2, t * P:(t + 1) * P],
                                 fold[:, :], start=True, stop=True)
                    ins.then_inc(o0_turned, 1)

                LAG = 3
                NCK = H0 * KCH
                for n in range(NCK + LAG):
                    if n < NCK:
                        h, k = n // KCH, n % KCH
                        if k == 0:
                            if h >= 1:
                                pe.wait_ge(low_ready, h)
                            mm(ps[:, 6, :], max_rows[:, :], q_stack[:, h, :], start=True, stop=True).then_inc(low_done, 1)
                        if n >= 4:
                            pe.wait_ge(t0_clipped, n - 3)
                        mm(ps[0:KW[k], n % 4, :], k_stack[:, h, k * P:k * P + KW[k]], q_stack[:, h, :],
                           start=True, stop=True).then_inc(t0_ready, 1)
                        if h >= 1 and k == 7:
                            turn_head(h - 1)
                    if n >= LAG:
                        value_product(n - LAG)
                turn_head(H0 - 1)
            with pe.Fori(0, NBATCH) as b:
                n_xT = [0]
                n_src = [0]

                def turn(src):
                    for c in range(DCH):
                        for t in range(TILES):
                            ins = tr(ps[:, 4 + c, t * P:(t + 1) * P], src[:, t, c * P:(c + 1) * P], ident[:, :])
                        ins.then_inc(xT_done, 1)
                    n_xT[0] += DCH

                pe.wait_ge(loaded, 48)
                for k in range(KCH):
                    if k >= 4:
                        pe.wait_ge(v0_ready, k - 3)
                    for c in range(CTXCH):
                        ins = mm(ps[0:KW[k], k % 4, 0:DIM], ctxT[:, c, k * P:k * P + KW[k]], wv0[:, c, :],
                                 start=(c == 0), stop=(c == CTXCH - 1))
                    ins.then_inc(v0_done, 1)
                pe.wait_ge(v0_ready, KCH)
                with pe.If(use_general != 0):
                    attend_general()
                with pe.Else():
                    attend_bounded()
                pe.wait_ge(attn0_ready, H0)
                turn(attn0)
                pe.wait_ge(xT_ready, n_xT[0])
                for t in range(TILES):
                    for c in range(DCH):
                        ins = mm(ps[:, t, 0:DIM], xnT[:, c, t * P:(t + 1) * P], wo0[:, c, :], start=(c == 0), stop=(c == DCH - 1))
                    ins.then_inc(y0_done, 1)

                pe.wait_ge(xn_ready, 1 * TILES)
                turn(xn)
                pe.wait_ge(xT_ready, n_xT[0])
                for t in range(TILES):
                    for c in range(DCH):
                        ins = mm(ps[:, 6, t * NEXP:(t + 1) * NEXP], xnT[:, c, t * P:(t + 1) * P], wg[:, c, :],
                                 start=(c == 0), stop=(c == DCH - 1))
                ins.then_inc(gl_done, 1)
                pe.wait_ge(x1_ready, TILES)

                def expert_down(e):
                    for t in range(TILES):
                        pe.wait_ge(fused_ready, ICH * (e + 1))
                        m = e * TILES + t
                        if m >= 4:
                            pe.wait_ge(down_read, m - 3)
                        for i in range(ICH):
                            ins = mm(ps[:, 4 + m % 4, 0:DIM], fused[:, e % 2, i * SEQ + t * P:i * SEQ + (t + 1) * P], w2e[e % 2][:, i, :],
                                     start=(i == 0), stop=(i == ICH - 1))
                        ins.then_inc(down_done, 1)

                pe.wait_ge(gl_ready, 1)
                for e in range(NEXP):
                    pe.wait_ge(w_loaded[e % 2], 48 * (e // 2 + 1))
                    for i in range(ICH):
                        n = e * ICH + i
                        if n >= 2:
                            pe.wait_ge(fused_ready, n - 1)
                        for j, w in enumerate((w11, w12)):
                            for c in range(DCH):
                                ins = mm(ps[:, 2 * (n % 2) + j, :], w[e % 2][:, c, i * P:(i + 1) * P], xnT[:, c, :],
                                         start=(c == 0), stop=(c == DCH - 1))
                        ins.then_inc(gv_done, 1)
                        if i == 1 and e >= 1:
                            expert_down(e - 1)
                expert_down(NEXP - 1)

                pe.wait_ge(fused_ready, NEXP * ICH)
                for n in range(len(COLS) + KCH):
                    if n >= 4:
                        pe.wait_ge(c_ready, n - 3)
                    for c in range(CTXCH):
                        if n < len(COLS):
                            c0, w = COLS[n]
                            ins = mm(ps[:, n % 4, 0:w], wk1[:, c, :], ctxT[:, c, c0:c0 + w], start=(c == 0), stop=(c == CTXCH - 1))
                        else:
                            k = n - len(COLS)
                            ins = mm(ps[0:KW[k], n % 4, 0:DIM], ctxT[:, c, k * P:k * P + KW[k]], wv1[:, c, :],
                                     start=(c == 0), stop=(c == CTXCH - 1))
                    ins.then_inc(c_done, 1)
                pe.wait_ge(down_read, NEXP * TILES)
                pe.wait_ge(xn_ready, 2 * TILES)
                turn(xt)
                pe.wait_ge(xT_ready, n_xT[0])
                for c in range(DCH):
                    ins = mm(ps[:, 6, :], wq1[:, c, :], xnT[:, c, :], start=(c == 0), stop=(c == DCH - 1))
                ins.then_inc(q1_done, 1)
                pe.wait_ge(c_ready, len(COLS) + KCH)
                pe.wait_ge(q1_ready, H1)

                def scores(n):
                    if n >= 1:
                        pe.wait_ge(s1_ready, n)
                    t, h = n // H1, n % H1
                    for j, (c0, w) in enumerate(COLS):
                        mm(ps[:, j, 0:w], q1z[:, h, t * P:(t + 1) * P], kT1[:, c0:c0 + w], start=True, stop=False)
                        ins = mm(ps[:, j, 0:w], ones_row[:, :], mask_row[0:1, c0:c0 + w], start=False, stop=True)
                    ins.then_inc(s1_done, 1)

                def count(n):
                    pe.wait_ge(count_ready, n + 1)
                    if n >= 1:
                        pe.wait_ge(flag_ready, n)
                    mm(ps[0:1, 7, 448:449], kept[:, n:n + 1], ones[:, :], start=True, stop=True).then_inc(count_done, 1)

                def turn_probs(t, flags):
                    pe.wait_ge(p1_added, (H1 - 1) * (t + 1))
                    if t >= 1:
                        pe.wait_ge(aT_ready, 4 * t)
                        pe.wait_ge(ctx_ready, t)
                    pe.wait_ge(flag_ready, flags)
                    for k in range(KCH):
                        ins = tr(ps[0:KW[k], 4 + k // 4, (k % 4) * P:(k % 4 + 1) * P], p_mean[:, t % 2, k * P:k * P + KW[k]], ident[:, :])
                        if k % 4 == 3 or k == KCH - 1:
                            ins.then_inc(aT_done, 1)

                def context(t):
                    pe.wait_ge(aT_ready, 4 * t + 4)
                    for c in range(DCH):
                        for k in range(KCH):
                            ins = mm(ps[:, 7, P + c * P:P + (c + 1) * P], v1[0:KW[k], k, c * P:(c + 1) * P], attnT[0:KW[k], k, :],
                                     start=(k == 0), stop=(k == KCH - 1))
                    ins.then_inc(ctx_done, 1)

                pe.wait_ge(mask_ready, 1)
                scores(0)
                for n in range(TILES * H1):
                    if n + 1 < TILES * H1:
                        scores(n + 1)
                    if n % H1 == 2 and n > H1:
                        turn_probs(n // H1 - 1, n)
                        pe.wait_ge(aT_ready, 4 * (n // H1))
                    if n % H1 == 3 and n > H1:
                        pe.wait_ge(flag_ready, n)
                        context(n // H1 - 1)
                        pe.wait_ge(ctx_ready, n // H1)
                    count(n)
                turn_probs(TILES - 1, TILES * H1)
                context(TILES - 1)

                pe.wait_ge(ctx_ready, TILES)
                for i in range(2):
                    for t in range(TILES):
                        n = i * TILES + t
                        if n >= 4:
                            pe.wait_ge(film_read, n - 3)
                        for c in range(DCH):
                            ins = mm(ps[:, n % 4, :], c_tT[:, c, t * P:(t + 1) * P], film_w[:, i, c, :], start=(c == 0), stop=(c == DCH - 1))
                        ins.then_inc(film_done, 1)
                pe.wait_ge(u_ready, TILES)
                pe.wait_ge(w_late, 16 * 9)
                for j in range(FCH // 2):
                    for half in range(2):
                        for c in range(SEQ // P):
                            ins = mm(ps[:, 4 + j, half * DIM:(half + 1) * DIM], dft[:, c, (half * (FCH // 2) + j) * P:(half * (FCH // 2) + j + 1) * P],
                                     u[:, c, :], start=(c == 0), stop=(c == SEQ // P - 1))
                    ins.then_inc(spec_done, 1)
                pe.wait_ge(spec_ready, FCH // 2)
                pe.wait_ge(film_read, 2 * TILES)
                for t in range(TILES):
                    for j in range(FCH):
                        ins = mm(ps[:, t, 0:DIM], idft[:, j, t * P:(t + 1) * P], spec[:, j, :], start=(j == 0), stop=(j == FCH - 1))
                    ins.then_inc(y1_done, 1)

                pe.wait_ge(xn_ready, 3 * TILES)
                turn(xn)
                pe.wait_ge(xT_ready, n_xT[0])
                for i in range(HCH):
                    if i >= 4:
                        pe.wait_ge(h_ready, i - 3)
                    for c in range(DCH):
                        ins = mm(ps[:, i % 4, :], wf1[:, c, i * P:(i + 1) * P], xnT[:, c, :], start=(c == 0), stop=(c == DCH - 1))
                    ins.then_inc(h_done, 1)
                pe.wait_ge(h_ready, HCH)
                for t in range(TILES):
                    for i in range(HCH):
                        ins = mm(ps[:, 4 + t, 0:DIM], hid[:, i, t * P:(t + 1) * P], wf2[:, i, :], start=(i == 0), stop=(i == HCH - 1))
                    ins.then_inc(f_done, 1)

                pe.wait_ge(xn_ready, 4 * TILES)
                turn(xn)
                pe.wait_ge(xT_ready, n_xT[0])
                for i in range(H2):
                    w = wk2 if i % 2 else wq2
                    if i >= 4:
                        pe.wait_ge(qk2_ready, i - 3)
                    for c in range(DCH):
                        ins = mm(ps[:, i % 4, :], w[:, c, (i // 2) * P:(i // 2 + 1) * P], xnT[:, c, :], start=(c == 0), stop=(c == DCH - 1))
                    ins.then_inc(qk2_done, 1)
                for t in range(TILES):
                    for j in range(2):
                        for c in range(DCH):
                            ins = mm(ps[:, 6 + j, t * P:(t + 1) * P], xnT[:, c, t * P:(t + 1) * P], wsd[:, c, j * P:(j + 1) * P],
                                     start=(c == 0), stop=(c == DCH - 1))
                ins.then_inc(g2_done, 1)
                pe.wait_ge(qk2_ready, H2)
                for t in range(TILES):
                    for c in range(DCH):
                        ins = mm(ps[:, t, :], xnT[:, c, t * P:(t + 1) * P], wv2[:, c, :], start=(c == 0), stop=(c == DCH - 1))
                    ins.then_inc(pv_done, 1)
                pe.wait_ge(pv_ready, TILES)
                pe.wait_ge(g2_read, 2)

                def turn_p2(n):
                    pe.wait_ge(p2_ready, n + 1)
                    if n >= 2:
                        if n % 2:
                            pe.wait_ge(p2T_act, n // 2)
                        else:
                            pe.wait_ge(p2T_dve, n // 2)
                    for j in range(TILES):
                        ins = tr(ps[:, 2 + n % 2, j * P:(j + 1) * P], p2[:, n % 2, j * P:(j + 1) * P], ident[:, :])
                    ins.then_inc(p2T_done, 1)

                def value2(n):
                    t, h = n // H2, n % H2
                    if n == 0:
                        pe.wait_ge(v2_ready, TILES - 1)
                        pe.wait_ge(v2_ready_p, 1)
                    if n % 2:
                        pe.wait_ge(p2T_act, n // 2 + 1)
                    else:
                        pe.wait_ge(p2T_dve, n // 2 + 1)
                    if h == 0 and t >= 1:
                        pe.wait_ge(z_ready, t)
                    for j in range(TILES):
                        ins = mm(ps[:, 4 + h // 8, (h % 8) * D2:(h % 8 + 1) * D2], pT2[:, n % 2, j * P:(j + 1) * P],
                                 v2[:, j, h * D2:(h + 1) * D2], start=(j == 0), stop=(j == TILES - 1))
                    ins.then_inc(o2_done, 1)

                def result(t):
                    pe.wait_ge(z_ready, t + 1)
                    if t >= 1:
                        pe.wait_ge(out_ready, t)
                    for c in range(TILES):
                        ins = tr(ps[:, 6, c * P:(c + 1) * P], z[:, c * P:(c + 1) * P], ident[:, :])
                    ins.then_inc(zT_done, 1)
                    pe.wait_ge(zT_ready, t + 1)
                    for c in range(TILES):
                        ins = mm(ps[:, 7, 0:DIM], zT[:, c * P:(c + 1) * P], wo2[:, c, :], start=(c == 0), stop=(c == TILES - 1))
                    ins.then_inc(r_done, 1)

                for n in range(NG + 2):
                    if n < NG:
                        h, t = n % H2, n // H2
                        if n >= 2:
                            pe.wait_ge(p2_ready, n - 1)
                        mm(ps[:, n % 2, :], q2z[:, h, t * P:(t + 1) * P], kT2[:, h // 2, :], start=True, stop=True).then_inc(s2_done, 1)
                    if 1 <= n <= NG:
                        turn_p2(n - 1)
                    if n >= 2:
                        value2(n - 2)
                        if (n - 2) % H2 == H2 - 1:
                            result((n - 2) // H2)
                end_of_batch(pe, b)

        @block.vector
        def _(dve):
            V = nc.vector
            steps = [0]
            step_sem = [setup_v]

            def setup_program():
                count = [0]
                own = [0]
                chain = ctx.enter_context(nc.semaphore("setup_step"))

                def link(ins):
                    own[0] += 1
                    ins.then_inc(chain, 1)
                    dve.wait_ge(chain, own[0])

                def done(n):
                    count[0] += 1
                    assert count[0] == n
                    dve.drain().then_inc(setup_v, 1)

                link(V.memset(eps[:, :], LN_EPS))
                link(V.memset(ones[:, :], 1.0))
                link(V.memset(ones_row[:, :], 1.0))
                link(V.memset(bounded[:, :], 1.0))
                dve.wait_ge(consts, 16 * len(NLOADS))
                link(V.tensor_scalar(bq0[:, :], bq0[:, :], D0 ** -0.5, None, ALU.mult))
                done(1)
                ar, ai, dt = s_t[6], s_t[7], s_t[5]
                dve.wait_ge(setup_a, 1)
                link(V.tensor_tensor(ar, s_t[0], dt, ALU.mult))
                link(V.tensor_tensor(ai, s_t[1], dt, ALU.mult))
                done(2)
                C1 = 6.28125
                C2 = TWO_PI - C1

                def reduce_angle(out, n, theta, turns, col):
                    link(V.tensor_scalar(n, theta, 1.0 / TWO_PI, turns, ALU.mult, ALU.add))
                    link(V.tensor_scalar(n, n, MAGIC, MAGIC, ALU.add, ALU.subtract))
                    link(V.scalar_tensor_tensor(theta, n, -C1, theta, ALU.mult, ALU.add))
                    link(V.scalar_tensor_tensor(theta, n, -C2, theta, ALU.mult, ALU.add))
                    link(V.tensor_scalar(out, theta, col, 3.14159, ALU.add, ALU.min))
                    link(V.tensor_scalar(out, out, -3.14159, None, ALU.max))

                link(V.tensor_copy(s_t[11], ai))
                reduce_angle(s_t[9], s_t[12], s_t[11], 0.25, float(TWO_PI / 4))
                link(V.tensor_copy(s_t[11], ai))
                reduce_angle(s_t[10], s_t[12], s_t[11], 0.0, 0.0)
                done(3)
                dve.wait_ge(setup_a, 4)
                er, ei, den, br, bi, t0, t1 = s_t[9], s_t[10], s_t[11], s_t[12], s_t[13], s_t[14], s_t[15]
                link(V.tensor_tensor(er, er, s_t[8], ALU.mult))
                link(V.tensor_scalar(er, er, -1.0, None, ALU.add))
                link(V.tensor_tensor(ei, ei, s_t[8], ALU.mult))
                link(V.tensor_tensor(den, s_t[0], s_t[0], ALU.mult))
                link(V.tensor_tensor(t0, s_t[1], s_t[1], ALU.mult))
                link(V.tensor_tensor(den, den, t0, ALU.add))
                link(V.reciprocal(den, den))

                def cmul(out, p, q, r, s, sign):
                    link(V.tensor_tensor(t0, p, q, ALU.mult))
                    link(V.tensor_tensor(t1, r, s, ALU.mult))
                    link(V.tensor_tensor(out, t0, t1, ALU.add if sign > 0 else ALU.subtract))

                cmul(br, er, s_t[0], ei, s_t[1], 1)
                cmul(bi, ei, s_t[0], er, s_t[1], -1)
                link(V.tensor_tensor(br, br, den, ALU.mult))
                link(V.tensor_tensor(bi, bi, den, ALU.mult))
                g1, g2 = s_t[16], s_t[17]
                cmul(g1, s_t[2], br, s_t[3], bi, -1)
                cmul(g2, s_t[2], bi, s_t[3], br, 1)
                link(V.tensor_scalar(g1[0:NSTATE, :], g1[0:NSTATE, :], 2.0, None, ALU.mult))
                link(V.tensor_scalar(g1[NSTATE:P, :], g1[NSTATE:P, :], -2.0, None, ALU.mult))
                link(V.tensor_scalar(g2, g2, -2.0, None, ALU.mult))
                kb = ramp[:, 0:LB].unsqueeze(1).to_broadcast([P, DIM, LB])
                ka = ramp[:, LB:LB + LA].unsqueeze(1).to_broadcast([P, DIM, LA])
                kw = k_w.rearrange("p a b -> p (a b)")
                link(V.tensor_tensor(k_w, ai.unsqueeze(2).to_broadcast([P, DIM, LB]), kb, ALU.mult))
                reduce_angle(kw, s_n, kw, phase[:, 2:3], phase[:, 0:1])
                done(4)
                link(V.tensor_tensor(s_n.rearrange("p (a b) -> p a b", b=LB), ar.unsqueeze(2).to_broadcast([P, DIM, LB]), kb, ALU.mult))
                done(5)
                dve.wait_ge(setup_a, 6)
                link(V.tensor_tensor(kw, kw, s_n, ALU.mult))
                sx3, sy3 = (v.rearrange("p (d a) -> p d a", a=LA) for v in (s_x, s_y))
                ai3 = ai.unsqueeze(2).to_broadcast([P, DIM, LA])
                link(V.tensor_tensor(sx3, ai3, ka, ALU.mult))
                reduce_angle(s_x, s_n[:, 0:NPW], s_x, phase[:, 2:3], phase[:, 0:1])
                done(6)
                link(V.tensor_tensor(sy3, ai3, ka, ALU.mult))
                reduce_angle(s_y, s_n[:, 0:NPW], s_y, phase[:, 3:4], phase[:, 1:2])
                done(7)
                link(V.tensor_tensor(s_n[:, 0:NPW].rearrange("p (d a) -> p d a", a=LA), ar.unsqueeze(2).to_broadcast([P, DIM, LA]), ka, ALU.mult))
                done(8)
                dve.wait_ge(setup_a, 9)
                link(V.tensor_tensor(sx3, sx3, g1.unsqueeze(2).to_broadcast([P, DIM, LA]), ALU.mult))
                link(V.tensor_tensor(sy3, sy3, g2.unsqueeze(2).to_broadcast([P, DIM, LA]), ALU.mult))
                link(V.tensor_tensor(s_x, s_x, s_y, ALU.add))
                link(V.tensor_tensor(s_x, s_x, s_n[:, 0:NPW], ALU.mult))
                done(9)
                dve.wait_ge(setup_p, 1)
                for bank in range(2):
                    link(V.tensor_copy(k_time[:, :, bank * P:(bank + 1) * P], ps[:, bank, :].rearrange("p (d a) -> p a d", a=4)))
                done(10)
                dve.wait_ge(setup_p, 2)
                half = FCH // 2
                spec_k = ps[:, 2:6, :].rearrange("p b (j d) -> p (b j) d", d=DIM)
                link(V.tensor_copy(k_cos[:, :, :], spec_k[:, 0:half, :]))
                link(V.tensor_copy(k_sin[:, :, :], spec_k[:, half:FCH, :]))
                link(V.tensor_copy(k_cos0[:, :], k_cos[:, 0, :]))
                link(V.tensor_copy(k_cos0[0:1, :], k_sin[0:1, 0, :]))
                link(V.memset(k_sin[0:1, 0, :], 0.0))
                dve.drain().then_inc(setup_done, 1)

            setup_program()

            IN_STEPS = 6
            link_of = {}

            def prepare(b):
                steps = [0]

                def link(ins):
                    steps[0] += 1
                    ins.then_inc(in_step, 1)
                    dve.wait_ge(in_step, IN_STEPS * b + steps[0])

                dve.wait_ge(in_x, 16 * b + 16)
                dve.wait_ge(in_xT_done, DCH * b)
                for t in range(TILES):
                    V.bn_stats(ln_stats[:, t, :], x[:, t, :])
                dve.drain()
                for t in range(TILES):
                    V.bn_aggr(ln_mv[:, t, :], ln_stats[:, t, :]).then_inc(in_var, 1)
                dve.wait_ge(in_dev, b + 1)
                link(V.reciprocal(ln_rstd[:, :], ln_std[:, :]))
                for t in range(TILES):
                    V.tensor_scalar(xn[:, t, :], x[:, t, :], ln_mv[:, t, 0:1], ln_rstd[:, t:t + 1], ALU.subtract, ALU.mult).then_inc(in_xn, 1)
                dve.wait_ge(in_spilled_k, 48 * b)
                dve.wait_ge(in_spilled_q, 48 * b)
                for g in range(DCH):
                    dve.wait_ge(in_k_read, DCH * b + g + 1)
                    V.tensor_tensor(k_r[:, g, :], k_f[:, g, :], k_p[:, 0, g, 0:GKEYS], ALU.subtract).then_inc(in_k_rest, 1)
                dve.wait_ge(in_q_read, b + 1)
                link(V.tensor_tensor(q_r, q_f, q_p[:, 0], ALU.subtract))
                link(V.tensor_copy(q_p[:, 1], q_r))
                V.tensor_tensor(q_p[:, 2], q_r, q_p[:, 1], ALU.subtract).then_inc(in_q_parts, 1)
                for g in range(DCH):
                    dve.wait_ge(in_k_mid, DCH * b + g + 1)
                    V.tensor_tensor(k_p[:, 2, g, 0:GKEYS], k_r[:, g, :], k_p[:, 1, g, 0:GKEYS], ALU.subtract).then_inc(in_k_parts, 1)
                dve.wait_ge(in_norms_done, 2 * b + 1)
                V.tensor_reduce(norms[:, 0:1], ps[0:H0, 4, :], AX.X, ALU.max).then_inc(in_norms_read, 1)
                dve.wait_ge(in_norms_done, 2 * b + 2)
                V.tensor_reduce(norms[:, 1:2], ps[0:H0, 0:4, :].rearrange("p a b -> p (a b)")[:, 0:GKEYS], AX.X, ALU.max).then_inc(in_norms_read, 1)
                dve.wait_ge(in_norms_read, 2 * b + 2)
                link(V.tensor_tensor(norms[:, 2:3], norms[:, 0:1], norms[:, 1:2], ALU.mult))
                link(V.tensor_scalar(norms[:, 3:4], norms[:, 2:3], BOUND * BOUND, None, ALU.is_le))
                link(V.tensor_tensor(bounded[:, :], bounded[:, :], norms[:, 3:4], ALU.mult))
                assert steps[0] == IN_STEPS

            V.memset(k_p[:, :, :, GKEYS:KPAD], 0.0)
            with dve.Fori(0, NBATCH) as b:
                prepare(b)
            dve.drain().then_inc(bounds_ready, 1)
            dve.wait_ge(bounds_done, 1)
            V.tensor_scalar(general[0:1, 0:1], ps[0:1, 4, 0:1], H0 - 0.5, None, ALU.is_lt)
            dve.drain().then_inc(path_known, 1)
            dve.wait_ge(path_known, 1)
            use_general = dve.value_load(general[0:1, 0:1], min_val=0, max_val=1)

            def per(v, n):
                return v.unsqueeze(2).to_broadcast([P, v.shape[1], n])

            def head_rows(h, out, turned, link):
                dve.wait_ge(turned, h + 1)
                o4 = out.rearrange("p (t d) -> p t d", d=V0W)
                r = small[:, TILES * h:TILES * (h + 1)]
                link(V.reciprocal(r, o4[:, :, D0]))
                V.tensor_tensor(attn0[:, :, h * D0:(h + 1) * D0], o4[:, :, 0:D0], per(r, D0), ALU.mult).then_inc(attn0_ready, 1)

            def attend_bounded():
                steps = [0]

                def link(ins):
                    steps[0] += 1
                    ins.then_inc(head_step, 1)
                    dve.wait_ge(head_step, steps[0])

                for h in range(H0):
                    dve.wait_ge(group_values, (KCH * h + KCH - 1) // 4 + 1)
                    if h >= 2:
                        dve.wait_ge(head_turned, h - 1)
                    V.tensor_copy(o_part[:, h % 2, :], ps[:, 4 + h % 2, :]).then_inc(head_out, 1)
                    if h >= 1:
                        head_rows(h - 1, ps[:, 6 + (h - 1) % 2, 0:TILES * V0W], head_turned, link)
                head_rows(H0 - 1, ps[:, 6 + (H0 - 1) % 2, 0:TILES * V0W], head_turned, link)

            def attend_general():
                steps = [0]

                def link(ins):
                    steps[0] += 1
                    ins.then_inc(general_step, 1)
                    dve.wait_ge(general_step, steps[0])

                link(V.memset(as_words(q_stack[NSPLIT:P, :, :]), 0.0))
                link(V.memset(as_words(k_stack[NSPLIT:P, :, :]), 0.0))
                V.memset(as_words(k_stack[NSPLIT:NSPLIT + 3, :, :]), TWO_ONES)
                dve.drain().then_inc(pads_ready, 3)
                for n in range(H0 * TILES):
                    h, t = n // TILES, n % TILES
                    dve.wait_ge(s0_ready, n + 1)
                    V.tensor_reduce(row_max[:, t, h:h + 1], wide(4 * (n % 2), GKEYS), AX.X, ALU.max).then_inc(s0_read, 1)
                dve.wait_ge(s0_read, H0 * TILES)
                link(V.tensor_scalar(neg_max, row_max, -CLAMP, CLAMP, ALU.max, ALU.min))
                V.tensor_scalar(neg_max, neg_max, -1.0, None, ALU.mult).then_inc(nmax_ready, 1)
                dve.wait_ge(nmaxT_done, 1)
                link(V.tensor_copy(nm_f[0:H0, :], ps[0:H0, 0, :]))
                link(V.tensor_copy(nm_p[0:H0, 0, :], nm_f[0:H0, :]))
                link(V.tensor_tensor(nm_r[0:H0, :], nm_f[0:H0, :], nm_p[0:H0, 0, :], ALU.subtract))
                link(V.tensor_copy(nm_p[0:H0, 1, :], nm_r[0:H0, :]))
                V.tensor_tensor(nm_p[0:H0, 2, :], nm_r[0:H0, :], nm_p[0:H0, 1, :], ALU.subtract).then_inc(nmax_parts, 1)

                for h in range(H0):
                    dve.wait_ge(low_done, h + 1)
                    V.tensor_scalar(low[:, h % 2, :], ps[:, 6, :], -CLAMP, None, ALU.add).then_inc(low_ready, 1)
                    dve.wait_ge(low_ready, h + 1)
                    for k in range(KCH):
                        n = h * KCH + k
                        dve.wait_ge(t0_ready, n + 1)
                        if n >= 4:
                            dve.wait_ge(pv0_done, n - 3)
                        w = KW[k]
                        V.scalar_tensor_tensor(probs0[0:w, n % 4, :], ps[0:w, n % 4, :], 0.0, low[0:w, h % 2, :],
                                               ALU.min, ALU.max).then_inc(t0_clipped, 1)
                        if h >= 1 and k == 11:
                            head_rows(h - 1, ps[:, 7, (h - 1) % 4 * P:((h - 1) % 4 + 1) * P], o0_turned, link)
                head_rows(H0 - 1, ps[:, 7, (H0 - 1) % 4 * P:((H0 - 1) % 4 + 1) * P], o0_turned, link)
            with dve.Fori(0, NBATCH) as b:
                steps = [0]
                n_ln = [0]

                def link(ins):
                    steps[0] += 1
                    ins.then_inc(v_step, 1)
                    dve.wait_ge(v_step, steps[0])

                def layernorm(dst, src, event):
                    n_ln[0] += 1
                    for t in range(TILES):
                        link(V.bn_stats(ln_stats[:, t, :], src[:, t, :]))
                    for t in range(TILES):
                        V.bn_aggr(ln_mv[:, t, :], ln_stats[:, t, :]).then_inc(ln_var, 1)
                    dve.wait_ge(ln_dev, n_ln[0])
                    link(V.reciprocal(ln_rstd[:, :], ln_std[:, :]))
                    for t in range(TILES):
                        ins = V.tensor_scalar(dst[:, t, :], src[:, t, :], ln_mv[:, t, 0:1], ln_rstd[:, t:t + 1], ALU.subtract, ALU.mult)
                        if event:
                            ins.then_inc(xn_ready, 1)
                        else:
                            link(ins)

                def rows(v):
                    return v.unsqueeze(1).to_broadcast([P, TILES, DIM])

                def top2(vals, m, oh1, oh2, tmp):
                    n = vals.shape[1]
                    first = prio[:, :].unsqueeze(1).to_broadcast([P, n, NEXP])
                    for k, oh in enumerate((oh1, oh2)):
                        src = vals if k == 0 else tmp
                        link(V.tensor_reduce(m, src, AX.X, ALU.max))
                        link(V.tensor_tensor(oh, src, per(m, NEXP), ALU.is_equal))
                        link(V.tensor_tensor(oh, oh, first, ALU.mult))
                        link(V.tensor_reduce(m, oh, AX.X, ALU.max))
                        link(V.tensor_tensor(oh, oh, per(m, NEXP), ALU.is_equal))
                        if k == 0:
                            link(V.scalar_tensor_tensor(tmp, oh, DROPPED, vals, ALU.mult, ALU.add))

                dve.wait_ge(v0_pads, 3)
                for k in range(KCH):
                    dve.wait_ge(v0_done, k + 1)
                    w = KW[k]
                    V.tensor_tensor(v0[0:w, k, :].rearrange("p (h w) -> p h w", w=V0W)[:, :, 0:D0],
                                    ps[0:w, k % 4, 0:DIM].rearrange("p (h d) -> p h d", d=D0),
                                    bv0[0:w, :].rearrange("p (h d) -> p h d", d=D0), ALU.add).then_inc(v0_ready, 1)
                dve.wait_ge(loaded, 48)
                link(V.tensor_copy(tmask[:, :], tmask8[:, :]))
                with dve.If(use_general != 0):
                    attend_general()
                with dve.Else():
                    attend_bounded()
                dve.wait_ge(attn0_ready, H0)
                for t in range(TILES):
                    dve.wait_ge(y0_done, t + 1)
                    link(V.tensor_tensor(x[:, t, :], x[:, t, :], ps[:, t, 0:DIM], ALU.add))
                    V.tensor_tensor(x[:, t, :], x[:, t, :], bo0[:, :], ALU.add).then_inc(x1_ready, 1)
                dve.wait_ge(x1_ready, TILES)

                layernorm(xn, x, True)
                dve.wait_ge(gl_done, 1)
                link(V.tensor_copy(gl, ps[:, 6, 0:TILES * NEXP].rearrange("p (t e) -> p t e", e=NEXP)))
                link(V.tensor_reduce(g_red[0], gl, AX.X, ALU.max))
                V.tensor_tensor(g_tmp[4], gl, per(g_red[0], NEXP), ALU.subtract).then_inc(gl_ready, 1)
                top2(gl, g_red[1], g_tmp[0], g_tmp[1], g_tmp[2])
                dve.wait_ge(g_exp, 1)
                link(V.tensor_reduce(g_red[2], g_tmp[5], AX.X, ALU.add))
                link(V.reciprocal(g_red[2], g_red[2]))
                link(V.tensor_tensor(g_tmp[5], g_tmp[5], per(g_red[2], NEXP), ALU.mult))
                link(V.tensor_tensor(g_tmp[0], g_tmp[0], g_tmp[1], ALU.add))
                link(V.tensor_tensor(g_w, g_tmp[0], g_tmp[5], ALU.mult))
                link(V.tensor_reduce(g_red[3], g_w, AX.X, ALU.add))
                link(V.tensor_scalar(g_red[3], g_red[3], 1e-8, None, ALU.add))
                link(V.reciprocal(g_red[3], g_red[3]))
                link(V.tensor_tensor(g_w, g_w, per(g_red[3], NEXP), ALU.mult))

                def expert_sum(e):
                    for t in range(TILES):
                        m = e * TILES + t
                        dve.wait_ge(down_done, m + 1)
                        if e:
                            dve.wait_ge(down_read, m - TILES + 1)
                        V.scalar_tensor_tensor(x[:, t, :], ps[:, 4 + m % 4, 0:DIM], g_w[:, t, e:e + 1], x[:, t, :],
                                               ALU.mult, ALU.add).then_inc(down_read, 1)

                for e in range(NEXP):
                    for i in range(ICH):
                        n = e * ICH + i
                        dve.wait_ge(silu_ready, n + 1)
                        if e >= 2 and i == 0:
                            dve.wait_ge(down_done, TILES * (e - 1))
                        V.tensor_tensor(fused[:, e % 2, i * SEQ:(i + 1) * SEQ], silu[:, n % 2, :], ps[:, 2 * (n % 2) + 1, :],
                                        ALU.mult).then_inc(fused_ready, 1)
                        if e >= 1 and i == 3:
                            expert_sum(e - 1)
                expert_sum(NEXP - 1)
                dve.wait_ge(down_read, TILES * NEXP)

                layernorm(xt, x, True)
                def settle(n):
                    s, cut = s_sb[:, n % 3, 0:GKEYS], s_cut[:, 0:GKEYS]
                    st = stat1[:, n % 3]
                    dve.wait_ge(count_done, n + 1)
                    V.tensor_scalar(flag[0:1, 0:1], ps[0:1, 7, 448:449], float(P * TOPK), None, ALU.is_gt).then_inc(flag_ready, 1)
                    dve.wait_ge(flag_ready, n + 1)
                    undecided = dve.value_load(flag[0:1, 0:1], min_val=0, max_val=1)
                    with dve.If(undecided != 0):
                        dve.wait_ge(e1_ready, n + 1)
                        dve.wait_ge(sum1_ready, n + 1)
                        for r in range(TOPK // 8):
                            eight = top[:, n % 2, 8 * r:8 * r + 8]
                            src = s if r == 0 else cut
                            V.max(eight, src)
                            dve.drain()
                            V.match_replace(cut, eight, src, DROPPED)
                            dve.drain()
                        V.tensor_scalar(kept01[:, n % 2, 0:GKEYS], cut, DROPPED, None, ALU.is_le)
                        dve.drain()
                        V.scalar_tensor_tensor(cut, kept01[:, n % 2, 0:GKEYS], 0.5, probs1[:, n % 3, 0:GKEYS], ALU.is_ge, ALU.mult, accum_out=st[:, SUM:SUM + 1])
                        dve.drain()

                def weight(n):
                    st = stat1[:, n % 3]
                    dve.wait_ge(sum1_ready, n + 1)
                    link(V.reciprocal(st[:, WEIGHT:WEIGHT + 1], st[:, SUM:SUM + 1]))
                    t = n // H1
                    V.tensor_scalar(st[:, WEIGHT:WEIGHT + 1], st[:, WEIGHT:WEIGHT + 1], tmask[:, t:t + 1], 1.0 / H1, ALU.mult, ALU.mult).then_inc(w1_ready, 1)

                dve.wait_ge(loaded, 64)
                V.tensor_scalar(mask_row[0:1, :], mask8[0:1, :], MASKED, MASKED, ALU.mult, ALU.subtract).then_inc(mask_ready, 1)
                for n in range(TILES * H1):
                    s, st = s_sb[:, n % 3, 0:GKEYS], stat1[:, n % 3]
                    eights = top[:, n % 2, :]
                    dve.wait_ge(s1_ready, n + 1)
                    for j, (c0, w) in enumerate(PARTS):
                        ins = V.max(cand[:, 8 * j:8 * j + 8], s[:, c0:c0 + w])
                    link(ins)
                    if n >= 1:
                        settle(n - 1)
                        weight(n - 1)
                    if n >= 2:
                        dve.wait_ge(sum1_ready, n - 1)
                    for r in range(TOPK // 8):
                        link(V.max(eights[:, 8 * r:8 * r + 8], cand))
                        if r < TOPK // 8 - 1:
                            link(V.match_replace(cand, eights[:, 8 * r:8 * r + 8], cand, DROPPED))
                    if n >= 3:
                        dve.wait_ge(p1_scaled, n - 2)
                    V.tensor_scalar(st[:, NEG:NEG + 1], eights[:, 0:1], -1.0, None, ALU.mult).then_inc(top_ready, 1)
                    if n >= 2:
                        dve.wait_ge(p1_kept, n - 1)
                    V.tensor_scalar(kept01[:, n % 2, 0:GKEYS], s, eights[:, TOPK - 1:TOPK], None, ALU.is_ge, ALU.add,
                                    accum_out=kept[:, n:n + 1]).then_inc(count_ready, 1)
                    dve.wait_ge(count_ready, n + 1)
                settle(TILES * H1 - 1)
                weight(TILES * H1 - 1)

                layernorm(xn, xt, False)
                link(V.tensor_tensor(xn[:, :, :], xn[:, :, :], rows(norm_g[:, 0, :]), ALU.mult))
                link(V.tensor_tensor(xn[:, :, :], xn[:, :, :], rows(norm_b[:, 0, :]), ALU.add))
                dve.wait_ge(ctx_done, TILES)
                dve.wait_ge(aT_ready, 4 * TILES)
                for i, f in enumerate((f_in, f_out)):
                    for t in range(TILES):
                        n = i * TILES + t
                        dve.wait_ge(film_done, n + 1)
                        V.tensor_tensor(f[:, t, :], ps[:, n % 4, :], film_b[:, i, :], ALU.add).then_inc(film_read, 1)
                        dve.wait_ge(film_read, n + 1)
                        link(V.tensor_scalar(f[:, t, :], f[:, t, :], mod_gate[:, 0:1], None, ALU.mult))
                        if i == 0:
                            link(V.scalar_tensor_tensor(u[:, t, :], f[:, t, 0:DIM], 1.0, xn[:, t, :], ALU.add, ALU.mult))
                            V.tensor_tensor(u[:, t, :], u[:, t, :], f[:, t, DIM:], ALU.add).then_inc(u_ready, 1)
                dve.wait_ge(u_ready, TILES)
                link(V.tensor_tensor(dtmp[:, :, :], u[:, :, :], rows(d_skip[:, :]), ALU.mult))
                half = FCH // 2
                for j in range(half):
                    dve.wait_ge(spec_done, j + 1)
                    uc, us = ps[:, 4 + j, 0:DIM], ps[:, 4 + j, DIM:2 * DIM]
                    kc, ks = k_cos[:, j, :], k_sin[:, j, :]
                    kc2 = k_cos0[:, :] if j == 0 else kc
                    p4 = ptmp[:, j % 2]
                    V.tensor_tensor(p4[:, 0, :], uc, kc, ALU.mult)
                    V.tensor_tensor(p4[:, 1, :], us, ks, ALU.mult)
                    V.tensor_tensor(p4[:, 2, :], uc, ks, ALU.mult)
                    link(V.tensor_tensor(p4[:, 3, :], us, kc2, ALU.mult))
                    link(V.tensor_tensor(spec[:, j, :], p4[:, 0, :], p4[:, 1, :], ALU.subtract))
                    V.tensor_tensor(spec[:, half + j, :], p4[:, 2, :], p4[:, 3, :], ALU.add).then_inc(spec_ready, 1)
                for t in range(TILES):
                    dve.wait_ge(y1_done, t + 1)
                    link(V.tensor_tensor(dtmp[:, t, :], dtmp[:, t, :], ps[:, t, 0:DIM], ALU.add))
                    link(V.scalar_tensor_tensor(dtmp[:, t, :], f_out[:, t, 0:DIM], 1.0, dtmp[:, t, :], ALU.add, ALU.mult))
                    link(V.tensor_tensor(dtmp[:, t, :], dtmp[:, t, :], f_out[:, t, DIM:], ALU.add))
                    link(V.tensor_tensor(xt[:, t, :], xt[:, t, :], dtmp[:, t, :], ALU.add))

                layernorm(xn, xt, False)
                link(V.tensor_tensor(xn[:, :, :], xn[:, :, :], rows(norm_g[:, 1, :]), ALU.mult))
                for t in range(TILES):
                    V.tensor_tensor(xn[:, t, :], xn[:, t, :], norm_b[:, 1, :], ALU.add).then_inc(xn_ready, 1)
                for t in range(TILES):
                    dve.wait_ge(f_done, t + 1)
                    link(V.tensor_tensor(xt[:, t, :], xt[:, t, :], ps[:, 4 + t, 0:DIM], ALU.add))
                    link(V.tensor_tensor(xt[:, t, :], xt[:, t, :], b2[:, :], ALU.add))
                dve.wait_ge(xn_ready, 3 * TILES)
                layernorm(xn, xt, False)
                link(V.tensor_tensor(xn[:, :, :], xn[:, :, :], rows(norm_g[:, 2, :]), ALU.mult))
                link(V.tensor_tensor(xn[:, :, :], xn[:, :, :], rows(norm_b[:, 2, :]), ALU.add))
                link(V.tensor_tensor(x[:, :, :], x[:, :, :], xn[:, :, :], ALU.add))

                layernorm(xn, x, True)
                dve.wait_ge(g2_done, 1)
                V.tensor_copy(gate_v, ps[:, 6, :].rearrange("p (n e) -> p n e", e=E2)).then_inc(g2_read, 1)
                V.tensor_copy(gate_o, ps[:, 7, :].rearrange("p (n e) -> p n e", e=E2)).then_inc(g2_read, 1)
                dve.wait_ge(g2_read, 2)
                top2(gate_v, t_m, t_oh1, t_oh2, t_a)
                link(V.tensor_tensor(t_oh1, t_oh1, t_oh2, ALU.add))
                dve.wait_ge(sig_ready, 1)
                V.tensor_tensor(t_b, t_oh1, sig_v, ALU.mult).then_inc(mix_ready, 1)
                dve.wait_ge(mix_ready, 1)
                dve.wait_ge(pv_ready, TILES)
                for t in range(TILES - 1):
                    for e in range(E2):
                        src = proj_v[:, t, e * D2:(e + 1) * D2].unsqueeze(1).to_broadcast([P, H2, D2])
                        mix = t_b[:, t * H2:(t + 1) * H2, e].unsqueeze(2).to_broadcast([P, H2, D2])
                        dst = v2[:, t, :] if e == 0 else v_tmp
                        link(V.tensor_tensor(dst.rearrange("p (h d) -> p h d", d=D2), src, mix, ALU.mult))
                        if e:
                            link(V.tensor_tensor(v2[:, t, :], v2[:, t, :], v_tmp, ALU.add))
                    dve.drain().then_inc(v2_ready, 1)
                top2(gate_o, t_m, t_oh1, t_oh2, t_a)
                link(V.tensor_tensor(t_oh1, t_oh1, t_oh2, ALU.add))

                def turned_p2(n):
                    dve.wait_ge(p2T_done, n + 1)
                    if n >= 2:
                        dve.wait_ge(o2_done, n - 1)
                    V.tensor_copy(pT2[:, n % 2, :], ps[:, 2 + n % 2, :]).then_inc(p2T_dve, 1)

                def head_sum(t):
                    dve.wait_ge(p2_ready, H2 * (t + 1))
                    link(V.reciprocal(rs2[:, t, :], sums2[:, t, :]))
                    g = t_oh1[:, t * H2:(t + 1) * H2, :]
                    link(V.tensor_tensor(g, g, per(rs2[:, t, :], E2), ALU.mult))
                    if t >= 1:
                        dve.wait_ge(zT_done, t)
                    for h in range(H2):
                        dve.wait_ge(o2_done, t * H2 + 8 * (h // 8) + 8)
                        src = ps[:, 4 + h // 8, (h % 8) * D2:(h % 8 + 1) * D2].unsqueeze(1).to_broadcast([P, E2, D2])
                        gate = g[:, h, :].unsqueeze(2).to_broadcast([P, E2, D2])
                        dst = z if h == 0 else z_tmp
                        link(V.tensor_tensor(dst.rearrange("p (e d) -> p e d", d=D2), src, gate, ALU.mult))
                        if h:
                            link(V.tensor_tensor(z, z, z_tmp, ALU.add))
                    dve.drain().then_inc(z_ready, 1)
                    dve.wait_ge(zT_done, t + 1)
                    V.tensor_copy(zT, ps[:, 6, :]).then_inc(zT_ready, 1)
                    dve.wait_ge(r_done, t + 1)
                    V.tensor_tensor(x[:, t, :], x[:, t, :], ps[:, 7, 0:DIM], ALU.add).then_inc(out_ready, 1)

                for n in range(NG + 1):
                    if n < NG:
                        t, h = n // H2, n % H2
                        dve.wait_ge(s2_done, n + 1)
                        link(V.tensor_reduce(nmax2[:, t, h:h + 1], ps[:, n % 2, :], AX.X, ALU.max))
                        V.tensor_scalar(nmax2[:, t, h:h + 1], nmax2[:, t, h:h + 1], -1.0, None, ALU.mult).then_inc(s2_max, 1)
                    if n >= 1 and (n - 1) % 2 == 0:
                        turned_p2(n - 1)
                    if n >= H2 and n % H2 == 0:
                        head_sum(n // H2 - 1)
                end_of_batch(dve, b)


def layout(inp):
    f = np.float32
    g = {k: np.asarray(v) for k, v in inp.items()}
    n = 2 * SEQ
    m = np.arange(SEQ)[:, None].astype(np.float64) * np.arange(SEQ)[None, :]
    cos, sin = np.cos(2 * np.pi * m / n), np.sin(2 * np.pi * m / n)
    sin[:, 0] = np.cos(np.pi * np.arange(SEQ))
    w = np.where(np.arange(SEQ) == 0, 1.0, 2.0)[:, None] / n
    head_sum_w = np.zeros((DIM, H0), f)
    head_sum_w[np.arange(DIM), np.arange(DIM) // D0] = 1.0

    def rows(w):
        return np.concatenate([w, np.zeros((CTXCH * P - DCTX,) + w.shape[1:], f)])

    fold = np.zeros((P, V0W), f)
    fold[np.arange(P), np.arange(P) % V0W] = 1.0
    max_rows = np.zeros((P, P), np.uint16)
    max_rows[NSPLIT:NSPLIT + 3, :] = 0x3F80
    phase = np.zeros((P, 4), f)
    phase[:NSTATE, 0] = phase[NSTATE:, 1] = np.pi / 2
    phase[:NSTATE, 2] = phase[NSTATE:, 3] = 0.25
    ramp = np.concatenate([np.arange(LB), LB * np.arange(LA)]).astype(f)

    def columns(v):
        return np.ascontiguousarray(v.reshape(-1, P).T)

    return {
        "x": g["x"],
        "ctxT": np.stack([rows(c.T) for c in g["ctx_768"]]),
        "tmask": np.ascontiguousarray(g["mask_BxS_bf1"].view(np.uint8).reshape(NBATCH, TILES, P).transpose(0, 2, 1)),
        "vmask": np.ascontiguousarray(g["mask_BxS2_bf1"]).view(np.uint8),
        "wq0": g["L0_xattn_Wq"], "wk0": rows(g["L0_xattn_Wk"]), "wv0": rows(g["L0_xattn_Wv"]), "wo0": g["L0_xattn_Wo"],
        "bq0": columns(g["L0_xattn_bq"]), "bk0": columns(g["L0_xattn_bk"]), "bv0": g["L0_xattn_bv"], "bo0": g["L0_xattn_bo"],
        "wg": g["L0_ffn_Wg"], "w11": g["L0_ffn_W11"], "w12": g["L0_ffn_W12"], "w2e": g["L0_ffn_W2"],
        "wq1": g["L1_xattn_Wq"], "wk1": rows(g["L1_xattn_Wk"]), "wv1": rows(g["L1_xattn_Wv"]),
        "film_w": np.stack([g["L1_xattn_W_film_in"], g["L1_xattn_W_film_out"]]),
        "film_b": np.stack([g["L1_xattn_b_film_in"], g["L1_xattn_b_film_out"]]),
        "norm_g": np.stack([g["L1_xattn_g_norm_in"], g["L1_xattn_g_ffn"], g["L1_xattn_g_norm_out"]]),
        "norm_b": np.stack([g["L1_xattn_b_norm_in"], g["L1_xattn_b_ffn"], g["L1_xattn_b_norm_out"]]),
        "wf1": g["L1_xattn_W1"], "b1": columns(g["L1_xattn_b1"]), "wf2": g["L1_xattn_W2"], "b2": g["L1_xattn_b2"],
        "log_dt": g["L1_xattn_log_dt"],
        "s4d": np.stack([np.ascontiguousarray(g["L1_xattn_" + k].T) for k in ("A_re", "A_im", "C_re", "C_im")]),
        "d_skip": g["L1_xattn_D_skip"], "mod_gate": g["L1_xattn_mod_gate"].reshape(1),
        "wq2": np.ascontiguousarray(g["L1_ffn_Wq"].reshape(H2 * D2, DIM).T),
        "wk2": np.ascontiguousarray(g["L1_ffn_Wk"].reshape(H2 * D2, DIM).T),
        "wsd": np.concatenate([g["L1_ffn_Ws"].reshape(H2 * E2, DIM).T, g["L1_ffn_Wd"].reshape(H2 * E2, DIM).T], axis=1),
        "wv2": np.ascontiguousarray(g["L1_ffn_Wv"].reshape(E2 * D2, DIM).T),
        "wo2": np.ascontiguousarray(g["L1_ffn_Wo"].transpose(0, 2, 1).reshape(E2 * D2, DIM)),
        "dft": np.concatenate([cos, sin], axis=1).astype(f),
        "idft": np.concatenate([cos.T * w, sin.T * w], axis=0).astype(f),
        "ident": np.eye(P, dtype=f), "fold": fold, "head_sum_w": head_sum_w, "max_rows": max_rows,
        "prio": np.arange(NEXP, 0, -1).astype(f), "phase": phase, "ramp": ramp,
    }


def kernel(**inputs):
    import concourse.bacc as bacc
    from concourse.bass_utils import run_bass_kernel_spmd

    nc = bacc.Bacc("TRN2", target_bir_lowering=False, num_devices=1)
    arrays = {"in_" + k: np.ascontiguousarray(v) for k, v in layout(inputs).items()}
    aps = {k[3:]: nc.dram_tensor(k, v.shape, mybir.dt.from_np(v.dtype), kind="ExternalInput").ap() for k, v in arrays.items()}
    aps["out"] = nc.dram_tensor("out", (NBATCH, SEQ, DIM), F32, kind="ExternalOutput").ap()
    program(nc, aps)
    r = run_bass_kernel_spmd(nc, [arrays], core_ids=[0])
    return r.results[0]["out"]
```

```python
from contextlib import ExitStack

import numpy as np

import concourse.bass as bass
from concourse import mybir

F32 = mybir.dt.float32
BF16 = mybir.dt.bfloat16
U8 = mybir.dt.uint8
I32 = mybir.dt.int32
ALU = mybir.AluOpType
ACT = mybir.ActivationFunctionType
AX = mybir.AxisListType

P = 128
NBATCH, SEQ, DIM = 4, 512, 256
QUARTER = 32
TILES = SEQ // P
DCH = DIM // P
GKEYS, DCTX = 1601, 192
CTXCH = 2
KCH = (GKEYS + P - 1) // P
KW = [min(P, GKEYS - P * k) for k in range(KCH)]
COLS = [(c, min(512, GKEYS - c)) for c in range(0, GKEYS, 512)]
H0, D0 = 16, 16
V0W = 32
CLAMP = 10000.0
BOUND = 64.0
SPLIT_Q = [0, 0, 1, 0, 2, 1]
SPLIT_K = [0, 1, 0, 2, 0, 1]
NSPLIT = len(SPLIT_Q) * D0
NEXP, INNER = 8, 512
ICH = INNER // P
H1, D1, TOPK = 4, 32, 32
ALL_DECIDED = int(np.float32(P * TOPK).view(np.int32))
DROPPED = -3.4e38
PART = 60
PARTS = [(c, min(PART, GKEYS - c)) for c in range(0, GKEYS, PART)]
MASKED = 3.0e38
NSTATE = 64
LB, LA = 32, 16
FCH = 2 * SEQ // P
HID = 4 * DIM
HCH = HID // P
H2, D2, E2 = 16, 64, 8
TWO_ONES = float(np.array(0x3F803F80, np.uint32).view(np.float32))
MAGIC = 12582912.0
TWO_PI = 6.283185307179586
LN_EPS = 1e-5
ARENA = 37352
CTX_AT = 27232
AFTER_CTX = CTX_AT + 2 * GKEYS + 2


def program(nc, a, dbg=None):
    ctx = ExitStack()
    with ctx:
        def sb(name, shape, dt=F32):
            return ctx.enter_context(nc.sbuf_tensor("sb_" + name, shape, dt))

        sems = []

        def sem(name):
            s = ctx.enter_context(nc.semaphore(name))
            sems.append(s)
            return s

        x = sb("x", [P, TILES, DIM])
        xt = sb("xt", [P, TILES, DIM])
        xn = sb("xn", [P, TILES, DIM])
        xnT = sb("xnT", [P, DCH, SEQ])
        wq0 = sb("wq0", [P, DCH, DIM])
        wk0 = sb("wk0", [P, CTXCH, DIM])
        wv0 = sb("wv0", [P, CTXCH, DIM])
        wo0 = sb("wo0", [P, DCH, DIM])
        bv0 = sb("bv0", [P, DIM])
        bo0 = sb("bo0", [P, DIM])
        bq0 = sb("bq0", [P, DCH])
        bk0 = sb("bk0", [P, DCH])
        wg = sb("wg", [P, DCH, NEXP])
        wq1 = sb("wq1", [P, DCH, H1 * D1])
        wk1 = sb("wk1", [P, CTXCH, H1 * D1])
        wv1 = sb("wv1", [P, CTXCH, DIM])
        film_w = sb("film_w", [P, 2, DCH, 2 * DIM])
        film_b = sb("film_b", [P, 2, 2 * DIM])
        norm_g = sb("norm_g", [P, 3, DIM])
        norm_b = sb("norm_b", [P, 3, DIM])
        b1 = sb("b1", [P, HCH])
        b2 = sb("b2", [P, DIM])
        d_skip = sb("d_skip", [P, DIM])
        mod_gate = sb("mod_gate", [P, 1])
        k_cos = sb("k_cos", [P, FCH // 2, DIM])
        k_sin = sb("k_sin", [P, FCH // 2, DIM])
        k_cos0 = sb("k_cos0", [P, DIM])
        ident = sb("ident", [P, P])
        fold = sb("fold", [P, V0W])
        max_rows = sb("max_rows", [P, P], BF16)
        prio = sb("prio", [P, NEXP])
        phase = sb("phase", [P, 4])
        eps = sb("eps", [P, 1])
        quarter = sb("quarter", [P, 1])
        ln_stats = sb("ln_stats", [P, TILES, 6])
        ln_mv = sb("ln_mv", [P, TILES, 2])
        ln_std = sb("ln_std", [P, TILES])
        ln_rstd = sb("ln_rstd", [P, TILES])
        tmask = sb("tmask", [P, TILES])
        tmask8 = sb("tmask8", [P, TILES], U8)
        small = sb("small", [P, TILES * H0])
        ones = sb("ones", [P, 1])
        ones_row = sb("ones_row", [1, P], BF16)
        ones_col = sb("ones_col", [P, 1], BF16)
        head_sum_w = sb("head_sum_w", [P, DCH, QUARTER])
        norms = sb("norms", [P, 4])
        bounded = sb("bounded", [P, 1])
        general = sb("general", [1, 1], I32)

        arena = sb("arena", [P, ARENA])

        def at(off, shape, dt=F32):
            n = int(np.prod(shape))
            words = n if dt == F32 else (n + 1) // 2 if dt == BF16 else (n + 3) // 4
            v = arena[:, off:off + words]
            if dt != F32:
                v = v.bitcast(dt)[:, 0:n]
            if len(shape) == 2:
                v = v.rearrange("p (a b) -> p a b", b=shape[1])
            elif len(shape) == 3:
                v = v.rearrange("p (a b c) -> p a b c", b=shape[1], c=shape[2])
            return v

        ps = ctx.enter_context(nc.psum_tensor("ps", [P, 8, 512], F32))

        def wide(bank, n):
            return ps[:, bank:bank + (n + 511) // 512, :].rearrange("p a b -> p (a b)")[:, 0:n]

        ctxT = at(CTX_AT, [CTXCH, GKEYS])
        KPAD = KCH * P
        o = 0
        k_stack = at(o, [H0, KPAD], BF16); o += H0 * KPAD // 2
        q_stack = at(o, [H0, SEQ], BF16); o += H0 * SEQ // 2
        o_tr = o
        v0 = at(o, [KCH, H0 * V0W]); o += KCH * H0 * V0W
        low = at(o, [2, SEQ]); o += 2 * SEQ
        attn0 = at(o, [TILES, DIM]); o += TILES * DIM
        row_max = at(o, [TILES, H0]); o += TILES * H0
        neg_max = at(o, [TILES, H0]); o += TILES * H0
        assert o <= CTX_AT
        o = AFTER_CTX
        probs0 = at(o, [8, SEQ]); o += 8 * SEQ
        o_part = at(o, [2, SEQ]); o += 2 * SEQ
        nm_f = at(o, [SEQ]); o += SEQ
        nm_r = at(o, [SEQ]); o += SEQ
        nm_p = at(o, [3, SEQ], BF16); o += 3 * SEQ // 2
        assert o <= ARENA
        o = 0
        k_f = at(o, [DCH, GKEYS]); o += DCH * GKEYS
        k_r = at(o, [DCH, GKEYS]); o += DCH * GKEYS
        k_sq = at(o, [DCH, GKEYS]); o += DCH * GKEYS
        k_p = at(o, [3, DCH, KPAD], BF16); o += 3 * DCH * KPAD // 2
        q_f = at(o, [DCH, SEQ]); o += DCH * SEQ
        q_r = at(o, [DCH, SEQ]); o += DCH * SEQ
        q_sq = at(o, [DCH, SEQ]); o += DCH * SEQ
        q_p = at(o, [3, DCH, SEQ], BF16); o += 3 * DCH * SEQ // 2
        assert o <= CTX_AT
        o = 0
        w_exp = [at(o + 3072 * i, [3072]) for i in range(2)]; o += 2 * 3072
        w11 = [w[:, 0:1024].rearrange("p (c i) -> p c i", c=DCH) for w in w_exp]
        w12 = [w[:, 1024:2048].rearrange("p (c i) -> p c i", c=DCH) for w in w_exp]
        w2e = [w[:, 2048:3072].rearrange("p (c d) -> p c d", c=ICH) for w in w_exp]
        silu = at(o, [2, SEQ]); o += 2 * SEQ
        fused = at(o, [2, ICH * SEQ]); o += 2 * ICH * SEQ
        gl = at(o, [TILES, NEXP]); o += 32
        g_tmp = [at(o + 32 * i, [TILES, NEXP]) for i in range(6)]; o += 32 * 6
        g_red = [at(o + 8 * i, [TILES]) for i in range(6)]; o += 48
        g_w = at(o, [TILES, NEXP]); o += 32
        o = 0
        KS = 1602
        s_sb = [at(o + KS * i, [KS]) for i in range(3)] + [at(CTX_AT, [KS])]; o += 3 * KS
        s_cut = at(o, [KS]); o += KS
        kept01 = at(o, [2, KS], BF16); o += KS
        kept_by_col = at(o, [P]); o += P
        probs1 = at(o, [3, KS]); o += 3 * KS
        p_mean = at(o, [2, KS]); o += 2 * KS
        attnT = at(o, [KCH, P]); o += KCH * P
        kT1 = at(o, [GKEYS]); o += KS
        v1 = at(o, [KCH, DIM]); o += KCH * DIM
        q1z = at(o, [H1, SEQ]); o += H1 * SEQ
        assert o <= CTX_AT
        o = AFTER_CTX
        cand = at(o, [2, 8 * len(PARTS)]); o += 2 * 8 * len(PARTS)
        top = at(o, [2, TOPK]); o += 2 * TOPK
        top_e = at(o, [2, TOPK]); o += 2 * TOPK
        NEG, SUM, WEIGHT = range(3)
        stat1 = at(o, [3, 3]); o += 9
        kept = at(o, [TILES * H1]); o += TILES * H1
        mask8 = at(o, [GKEYS], U8); o += 402
        mask_row = at(o, [GKEYS], BF16); o += 802
        c_tT = at(ARENA - 1024, [DCH, SEQ])
        assert o <= ARENA - 1024 - SEQ // P * 2 * SEQ
        o = 0
        dft = at(ARENA - 1024 - SEQ // P * 2 * SEQ, [SEQ // P, 2 * SEQ])
        idft = at(o, [FCH, SEQ]); o += FCH * SEQ
        u = at(o, [TILES, DIM]); o += TILES * DIM
        f_in = at(o, [TILES, 2 * DIM]); f_out = at(o + 2048, [TILES, 2 * DIM]); o += 4096
        spec = at(o, [FCH, DIM]); o += FCH * DIM
        ptmp = at(o, [2, 4, DIM]); o += 8 * DIM
        dtmp = at(o, [TILES, DIM]); o += TILES * DIM
        wf1 = at(o, [DCH, HID]); o += DCH * HID
        wf2 = at(o, [HCH, DIM]); o += HCH * DIM
        assert o <= ARENA - 1024 - 6656
        hid_end = HCH * SEQ
        hid = at(0, [HCH, SEQ])
        o = ARENA - 1024 - 6656
        wq2 = at(o, [DCH, H2 * D2]); o += DCH * H2 * D2
        wk2 = at(o, [DCH, H2 * D2]); o += DCH * H2 * D2
        wsd = at(o, [DCH, 2 * H2 * E2]); o += DCH * 2 * H2 * E2
        wv2 = at(o, [DCH, E2 * D2]); o += DCH * E2 * D2
        wo2 = at(o, [E2 * D2 // P, DIM]); o += E2 * D2 // P * DIM
        o += 1024
        assert o == ARENA
        o = 0
        q2z = at(o, [H2, SEQ]); o += H2 * SEQ
        kT2 = at(o, [H2 // 2, SEQ]); o += H2 // 2 * SEQ
        proj_v = at(o, [TILES, E2 * D2]); o += TILES * E2 * D2
        v2 = at(o, [TILES, H2 * D2]); o += TILES * H2 * D2
        NG = TILES * H2
        gate_v = at(o, [NG, E2]); o += NG * E2
        gate_o = at(o, [NG, E2]); o += NG * E2
        t_oh1 = at(o, [NG, E2]); o += NG * E2
        t_oh2 = at(o, [NG, E2]); o += NG * E2
        t_a = at(o, [NG, E2]); o += NG * E2
        t_b = at(o, [NG, E2]); o += NG * E2
        t_m = at(o, [NG]); o += NG
        sums2 = at(o, [TILES, H2]); o += NG
        rs2 = at(o, [TILES, H2]); o += NG
        nmax2 = at(o, [TILES, H2]); o += NG
        p2 = at(o, [4, SEQ]); o += 4 * SEQ
        pT2 = at(o, [2, SEQ]); o += 2 * SEQ
        S2_BANKS = (0, 1, 6, 7)
        v_tmp = at(o, [TILES, 4 * D2])
        zT = at(o, [2, E2 * D2]); o += 2 * E2 * D2
        v_tmp2 = at(o, [TILES, 4 * D2]); o += TILES * 4 * D2
        assert o <= CTX_AT, o
        o = ARENA - 1024 - 6656
        assert o <= AFTER_CTX
        o = AFTER_CTX
        z = at(o, [TILES, E2 * D2]); o += TILES * E2 * D2
        z_tmp = at(o, [TILES, E2 * D2]); o += TILES * E2 * D2
        sig_v = at(o, [NG, E2]); o += NG * E2
        assert o <= ARENA - 1024 - 1024
        o = 0
        NW, NPW = DIM * LB, DIM * LA
        k_w = at(o, [DIM, LB]); o += NW
        s_n = at(o, [NW])
        s_n3 = at(o, [DIM, LB]); o += NW
        s_x = at(o, [NPW]); o += NPW
        s_y = at(o, [NPW]); o += NPW
        s_t = [at(o + DIM * i, [DIM]) for i in range(16)]; o += 16 * DIM
        ramp = at(o, [LB + LA]); o += LB + LA
        dft_s = at(o, [SEQ // P, 2 * SEQ]); o += SEQ // P * 2 * SEQ
        s_e = at(o, [NPW])
        k_time = at(o, [SEQ // P, DIM]); o += NPW
        assert o <= ARENA
        k_spill = nc.dram_tensor("k_spill", [NBATCH, 3, DIM, KPAD], BF16).ap()
        q_spill = nc.dram_tensor("q_spill", [NBATCH, 3, DIM, SEQ], BF16).ap()

        s4d_loaded = ctx.enter_context(nc.semaphore("s4d_loaded"))
        setup_g = ctx.enter_context(nc.semaphore("setup_g"))
        consts = ctx.enter_context(nc.semaphore("consts"))
        setup_v = ctx.enter_context(nc.semaphore("setup_v"))
        setup_a = ctx.enter_context(nc.semaphore("setup_a"))
        setup_p = ctx.enter_context(nc.semaphore("setup_p"))
        setup_done = ctx.enter_context(nc.semaphore("setup_done"))
        engine_ended = ctx.enter_context(nc.semaphore("engine_ended"))
        batch_closed = ctx.enter_context(nc.semaphore("batch_closed"))
        batch_opened = ctx.enter_context(nc.semaphore("batch_opened"))
        def once(name):
            return ctx.enter_context(nc.semaphore(name))

        in_x, in_ctx = once("in_x"), once("in_ctx")
        in_var, in_dev, in_xn, in_step = once("in_var"), once("in_dev"), once("in_xn"), once("in_step")
        in_xT_done, in_xT_ready = once("in_xT_done"), once("in_xT_ready")
        in_k_done, in_k_read, in_k_rest, in_k_mid, in_k_parts = (once("in_k_" + n) for n in ("done", "read", "rest", "mid", "parts"))
        in_q_done, in_q_read, in_q_parts = once("in_q_done"), once("in_q_read"), once("in_q_parts")
        in_squares, in_norms_done, in_norms_read = once("in_squares"), once("in_norms_done"), once("in_norms_read")
        in_spilled_k, in_spilled_q = once("in_spilled_k"), once("in_spilled_q")
        stored = once("stored")
        ctx_loaded = once("ctx_loaded")
        bounds_ready, bounds_done, path_known = once("bounds_ready"), once("bounds_done"), once("path_known")
        loaded = sem("loaded")
        pads_ready = sem("pads_ready")
        v_step = sem("v_step")
        ln_var = sem("ln_var")
        ln_dev = sem("ln_dev")
        xn_ready = sem("xn_ready")
        xT_done = sem("xT_done")
        xT_ready = sem("xT_ready")
        v0_pads = sem("v0_pads")
        stacked = [sem("stacked%d" % i) for i in range(4)]
        pair_scores = sem("pair_scores")
        pair_probs = sem("pair_probs")
        group_values = sem("group_values")
        head_out = sem("head_out")
        head_turned = sem("head_turned")
        head_step = sem("head_step")
        general_step = sem("general_step")
        v0_done = sem("v0_done")
        v0_ready = sem("v0_ready")
        s0_ready = sem("s0_ready")
        s0_read = sem("s0_read")
        nmax_ready = sem("nmax_ready")
        nmaxT_done = sem("nmaxT_done")
        nmax_parts = sem("nmax_parts")
        nmax_stacked = sem("nmax_stacked")
        low_done = sem("low_done")
        low_ready = sem("low_ready")
        t0_ready = sem("t0_ready")
        t0_clipped = sem("t0_clipped")
        p0_ready = sem("p0_ready")
        pv0_done = sem("pv0_done")
        o0_ready = sem("o0_ready")
        o0_turned = sem("o0_turned")
        attn0_ready = sem("attn0_ready")
        y0_done = sem("y0_done")
        x1_ready = sem("x1_ready")
        gl_done = sem("gl_done")
        gl_ready = sem("gl_ready")
        g_exp = sem("g_exp")
        w_loaded = [sem("w_loaded0"), sem("w_loaded1")]
        gv_done = sem("gv_done")
        silu_ready = sem("silu_ready")
        fused_ready = sem("fused_ready")
        down_done = sem("down_done")
        down_read = sem("down_read")
        c_done = sem("c_done")
        c_ready = sem("c_ready")
        q1_clear = sem("q1_clear")
        in_normal = sem("in_normal")
        in_ready = sem("in_ready")
        q1_done = sem("q1_done")
        q1_ready = sem("q1_ready")
        s1_done = sem("s1_done")
        s1_ready = sem("s1_ready")
        top_ready = sem("top_ready")
        e1_ready = sem("e1_ready")
        sum1_ready = sem("sum1_ready")
        p1_ready = sem("p1_ready")
        choice_ready = sem("choice_ready")
        count_ready = sem("count_ready")
        count_done = sem("count_done")
        w1_ready = sem("w1_ready")
        cand_ready = sem("cand_ready")
        cand_step = sem("cand_step")
        p1_kept = sem("p1_kept")
        p1_scaled = sem("p1_scaled")
        p1_added = sem("p1_added")
        aT_done = sem("aT_done")
        aT_ready = sem("aT_ready")
        ctx_half = sem("ctx_half")
        mask_ready = sem("mask_ready")
        ctx_ready = sem("ctx_ready")
        dft_loaded = sem("dft_loaded")
        idft_loaded = sem("idft_loaded")
        ff_loaded = sem("ff_loaded")
        w2_loaded = sem("w2_loaded")
        film_done = sem("film_done")
        film_read = sem("film_read")
        u_ready = sem("u_ready")
        spec_done = sem("spec_done")
        spec_ready = sem("spec_ready")
        y1_done = sem("y1_done")
        xt2_ready = sem("xt2_ready")
        h_done = sem("h_done")
        h_ready = sem("h_ready")
        f_done = sem("f_done")
        f_read = sem("f_read")
        x3_ready = sem("x3_ready")
        q2_clear = sem("q2_clear")
        qk2_done = sem("qk2_done")
        qk2_ready = sem("qk2_ready")
        g2_done = sem("g2_done")
        g2_read = sem("g2_read")
        sig_ready = sem("sig_ready")
        pv_done = sem("pv_done")
        pv_ready = sem("pv_ready")
        mix_ready = sem("mix_ready")
        v2_first = sem("v2_first")
        v2_rest = sem("v2_rest")
        p2T_ready = sem("p2T_ready")
        gated = sem("gated")
        z_added = sem("z_added")
        p_step = sem("p_step")
        s2_done = sem("s2_done")
        s2_max = sem("s2_max")
        p2_ready = sem("p2_ready")
        p2T_done = sem("p2T_done")
        o2_done = sem("o2_done")
        z_ready = sem("z_ready")
        zT_done = sem("zT_done")
        zT_ready = sem("zT_ready")
        r_done = sem("r_done")
        out_ready = sem("out_ready")
        assert [s.num for s in sems] == list(range(sems[0].num, sems[-1].num + 1))

        NLOADS = []

        block = ctx.enter_context(nc.Block())

        @block.sync
        def _(sp):
            def const(dst, src):
                sp.dma_start(dst, src).then_inc(consts, 16)
                NLOADS.append(1)

            def bcast(dst, src):
                const(dst, src.partition_broadcast(P))

            for i, name in enumerate(["A_re", "A_im", "C_re", "C_im"]):
                for half in range(2):
                    sp.dma_start(s_t[i][half * NSTATE:(half + 1) * NSTATE, :], a["s4d"][i]).then_inc(s4d_loaded, 16)
            sp.dma_start(s_t[4][:, :], a["log_dt"].partition_broadcast(P)).then_inc(s4d_loaded, 16)
            sp.dma_start(ramp[:, :], a["ramp"].partition_broadcast(P)).then_inc(s4d_loaded, 16)
            sp.dma_start(phase[:, :], a["phase"]).then_inc(s4d_loaded, 16)
            const(dft_s[:, :, :], a["dft"].rearrange("(c p) f -> p c f", p=P))
            const(ident[:, :], a["ident"])
            const(fold[:, :], a["fold"])
            const(head_sum_w[:, :, :], a["head_sum_w"].rearrange("(c p) n -> p c n", p=P))
            const(max_rows[:, :].bitcast(mybir.dt.uint16), a["max_rows"])
            bcast(prio[:, :], a["prio"])
            const(wq0[:, :, :], a["wq0"].rearrange("(c p) n -> p c n", p=P))
            const(wk0[:, :, :], a["wk0"].rearrange("(c p) n -> p c n", p=P))
            const(wv0[:, :, :], a["wv0"].rearrange("(c p) n -> p c n", p=P))
            const(wo0[:, :, :], a["wo0"].rearrange("(c p) n -> p c n", p=P))
            bcast(bv0[:, :], a["bv0"])
            bcast(bo0[:, :], a["bo0"])
            const(bq0[:, :], a["bq0"])
            const(bk0[:, :], a["bk0"])
            const(wg[:, :, :], a["wg"].rearrange("(c p) n -> p c n", p=P))
            const(wq1[:, :, :], a["wq1"].rearrange("(c p) n -> p c n", p=P))
            const(wk1[:, :, :], a["wk1"].rearrange("(c p) n -> p c n", p=P))
            const(wv1[:, :, :], a["wv1"].rearrange("(c p) n -> p c n", p=P))
            for i in range(2):
                const(film_w[:, i, :, :], a["film_w"][i].rearrange("(c p) n -> p c n", p=P))
                bcast(film_b[:, i, :], a["film_b"][i])
            for i in range(3):
                bcast(norm_g[:, i, :], a["norm_g"][i])
                bcast(norm_b[:, i, :], a["norm_b"][i])
            const(b1[:, :], a["b1"])
            bcast(b2[:, :], a["b2"])
            bcast(d_skip[:, :], a["d_skip"])
            bcast(mod_gate[:, :], a["mod_gate"])
            sp.wait_ge(setup_done, 1)

            sp.sem_inc(in_spilled_k, 1)
            sp.sem_inc(in_spilled_q, 1)
            sp.dma_start(x[:, :, :], a["x"][0].rearrange("(t p) d -> p t d", p=P)).then_inc(in_x, 16)
            sp.dma_start(ctxT[:, :, :], a["ctxT"][0].rearrange("(c p) k -> p c k", p=P)).then_inc(in_ctx, 16)
            with sp.Fori(0, NBATCH) as b:
                sp.wait_ge(in_xn, TILES * b + TILES + 1)
                sp.dma_start(x[:, :, :], a["x"][b + 1].rearrange("(t p) d -> p t d", p=P)).then_inc(in_x, 16)
                sp.wait_ge(in_k_done, DCH * len(COLS) * (b + 1) + 1)
                sp.dma_start(ctxT[:, :, :], a["ctxT"][b + 1].rearrange("(c p) k -> p c k", p=P)).then_inc(in_ctx, 16)
                sp.wait_ge(in_q_parts, b + 1)
                for i in range(3):
                    sp.dma_start(q_spill[b, i].rearrange("(c p) k -> p c k", p=P), q_p[:, i, :, :]).then_inc(in_spilled_q, 16)
                sp.wait_ge(in_k_parts, DCH * b + DCH + 1)
                for i in range(3):
                    sp.dma_start(k_spill[b, i].rearrange("(c p) k -> p c k", p=P), k_p[:, i, :, :]).then_inc(in_spilled_k, 16)
            sp.wait_ge(in_spilled_q, 48 * NBATCH + 1)
            sp.wait_ge(in_spilled_k, 48 * NBATCH + 1)
            sp.wait_ge(path_known, 1)
            sp.wait_ge(in_ctx, 16 * NBATCH + 16)

            sp.dma_start(ctxT[:, :, :], a["ctxT"][0].rearrange("(c p) k -> p c k", p=P)).then_inc(ctx_loaded, 16)
            sp.sem_inc(stored, 1)
            with sp.Fori(0, NBATCH) as b:
                sp.wait_ge(stored, 16 * TILES * b + 1)
                sp.dma_start(x[:, :, :], a["x"][b].rearrange("(t p) d -> p t d", p=P)).then_inc(loaded, 16)
                sp.dma_start(tmask8[:, :], a["tmask"][b].rearrange("p t -> p t")).then_inc(loaded, 16)
                for g in range(4):
                    hs = slice(4 * g, 4 * g + 4)
                    rows = slice(4 * g * D0, (4 * g + 4) * D0)
                    for i, part in enumerate(SPLIT_K):
                        sp.dma_start(k_stack[i * D0:(i + 1) * D0, hs, :],
                                     k_spill[b, part, rows].rearrange("(h d) k -> d h k", d=D0)).then_inc(stacked[g], 16)
                    for i, part in enumerate(SPLIT_Q):
                        sp.dma_start(q_stack[i * D0:(i + 1) * D0, hs, :],
                                     q_spill[b, part, rows].rearrange("(h d) k -> d h k", d=D0)).then_inc(stacked[g], 16)

                for e in range(NEXP):
                    if e == 0:
                        sp.wait_ge(attn0_ready, H0)
                        sp.dma_start(mask8[0:1, :], a["vmask"][b].unsqueeze(0)).then_inc(loaded, 16)
                        sp.dma_start(dft[:, :, :], a["dft"].rearrange("(c p) f -> p c f", p=P)).then_inc(dft_loaded, 16)
                    if e >= 2:
                        sp.wait_ge(down_done, TILES * (e - 1))
                    sp.dma_start(w11[e % 2], a["w11"][e].rearrange("(c p) n -> p c n", p=P)).then_inc(w_loaded[e % 2], 16)
                    sp.dma_start(w12[e % 2], a["w12"][e].rearrange("(c p) n -> p c n", p=P)).then_inc(w_loaded[e % 2], 16)
                    sp.dma_start(w2e[e % 2], a["w2e"][e].rearrange("(c p) n -> p c n", p=P)).then_inc(w_loaded[e % 2], 16)

                sp.wait_ge(down_done, TILES * NEXP)
                sp.wait_ge(ctx_half, DCH * TILES)
                sp.wait_ge(p1_added, TILES * (H1 - 1))
                sp.wait_ge(w1_ready, TILES * H1)
                sp.dma_start(idft[:, :, :], a["idft"].rearrange("(c p) f -> p c f", p=P)).then_inc(idft_loaded, 16)
                sp.dma_start(wf1[:, :, :], a["wf1"].rearrange("(c p) f -> p c f", p=P)).then_inc(ff_loaded, 16)
                sp.dma_start(wf2[:, :, :], a["wf2"].rearrange("(c p) f -> p c f", p=P)).then_inc(ff_loaded, 16)
                sp.wait_ge(spec_done, FCH // 2)
                for w, name in ((wsd, "wsd"), (wv2, "wv2"), (wq2, "wq2"), (wk2, "wk2"), (wo2, "wo2")):
                    sp.dma_start(w[:, :, :], a[name].rearrange("(c p) f -> p c f", p=P)).then_inc(w2_loaded, 16)

                sp.wait_ge(qk2_done, H2)
                sp.wait_ge(pv_done, TILES)
                sp.wait_ge(g2_done, 1)
                sp.dma_start(ctxT[:, :, :], a["ctxT"][b + 1].rearrange("(c p) k -> p c k", p=P)).then_inc(ctx_loaded, 16)

                for t in range(TILES):
                    sp.wait_ge(out_ready, t + 1)
                    sp.dma_start(a["out"][b].rearrange("(t p) d -> p t d", p=P)[:, t, :], x[:, t, :]).then_inc(stored, 16)
                if dbg is not None:
                    pass
                sp.wait_ge(ctx_loaded, 16 * b + 32)

                sp.wait_ge(engine_ended, 4 * b + 4)
                sp.sem_inc(batch_closed, 1)
                sp.sem_clear(range(sems[0].num, sems[-1].num + 1))
                sp.sem_inc(batch_opened, 1)
            sp.wait_ge(stored, 16 * TILES * NBATCH + 1)

        def end_of_batch(eng, b):
            eng.drain().then_inc(engine_ended, 1)
            eng.wait_ge(batch_opened, b + 1)

        def mix_values(eng, g, tmp, link):
            hs = slice(4 * g * D2, (4 * g + 4) * D2)
            shape = [P, TILES, 4, D2]

            def heads(v):
                return v.rearrange("p t (h d) -> p t h d", d=D2)

            for e in range(E2):
                src = proj_v[:, :, e * D2:(e + 1) * D2].unsqueeze(2).to_broadcast(shape)
                mix = t_b.rearrange("p (t h) e -> p t h e", h=H2)[:, :, 4 * g:4 * g + 4, e].unsqueeze(3).to_broadcast(shape)
                link(eng.tensor_tensor(heads(tmp if e else v2[:, :, hs]), src, mix, ALU.mult))
                if e:
                    link(eng.tensor_tensor(v2[:, :, hs], v2[:, :, hs], tmp, ALU.add))

        def as_words(v):
            return v.rearrange("p a b -> p (a b)").bitcast(F32)

        @block.gpsimd
        def _(pool):
            G = nc.gpsimd
            ar = s_t[6]
            kb = ramp[:, 0:LB].unsqueeze(1).to_broadcast([P, DIM, LB])
            ka = ramp[:, LB:LB + LA].unsqueeze(1).to_broadcast([P, DIM, LA])
            pool.wait_ge(setup_v, 2)
            G.tensor_tensor(s_e.rearrange("p (d a) -> p d a", a=LA), ar.unsqueeze(2).to_broadcast([P, DIM, LA]), ka, ALU.mult).then_inc(setup_g, 1)
            pool.wait_ge(setup_v, 5)
            G.tensor_tensor(s_n3[:, 0:DIM // 2, :], ar[:, 0:DIM // 2].unsqueeze(2).to_broadcast([P, DIM // 2, LB]), kb[:, 0:DIM // 2, :],
                            ALU.mult).then_inc(setup_g, 1)
            pool.wait_ge(setup_done, 1)
            pool.sem_inc(in_squares, 1)
            with pool.Fori(0, NBATCH) as b:
                pool.wait_ge(in_norms_done, 2 * b + 1)
                pool.wait_ge(in_q_read, b + 1)
                G.tensor_tensor(q_sq, q_f, q_f, ALU.mult).then_inc(in_squares, 1)
                pool.wait_ge(in_k_read, DCH * b + DCH)
                G.tensor_tensor(k_sq, k_f, k_f, ALU.mult).then_inc(in_squares, 1)
            pool.wait_ge(path_known, 1)
            pool.wait_ge(in_spilled_q, 48 * NBATCH + 1)
            pool.wait_ge(in_spilled_k, 48 * NBATCH + 1)

            with pool.Fori(0, NBATCH) as b:
                vpad = v0.rearrange("p k (h w) -> p k h w", w=V0W)
                G.memset(v0[P // 2:P, KCH - 1, :], 0.0).then_inc(v0_pads, 1)
                pool.wait_ge(v0_pads, 1)
                G.memset(vpad[:, 0:KCH - 1, :, D0 + 1:V0W], 0.0).then_inc(v0_pads, 1)
                G.memset(vpad[:, 0:KCH - 1, :, D0:D0 + 1], 1.0).then_inc(v0_pads, 1)
                pool.wait_ge(v0_pads, 3)
                G.memset(vpad[0:KW[-1], KCH - 1, :, D0 + 1:V0W], 0.0).then_inc(v0_pads, 1)
                G.memset(vpad[0:KW[-1], KCH - 1, :, D0:D0 + 1], 1.0).then_inc(v0_pads, 1)
                pool.wait_ge(v0_pads, 5)
                pool.wait_ge(x1_ready, TILES)
                G.memset(q1z[:, :, :], 0.0).then_inc(q1_clear, 1)
                def over_tiles(v):
                    return v.unsqueeze(1).to_broadcast([P, TILES, DIM])

                pool.wait_ge(in_normal, TILES)
                G.tensor_tensor(xn[:, :, :], xn[:, :, :], over_tiles(norm_g[:, 0, :]), ALU.mult).then_inc(in_ready, 1)
                pool.wait_ge(in_ready, 1)
                G.tensor_tensor(xn[:, :, :], xn[:, :, :], over_tiles(norm_b[:, 0, :]), ALU.add).then_inc(in_ready, 1)
                def add_head(n):
                    t, h = n // H1, n % H1
                    if h:
                        mean = p_mean[:, t % 2, 0:GKEYS]
                        pool.wait_ge(p1_scaled, n + 1)
                        if n > 1:
                            pool.wait_ge(p1_added, n - 1 - t)
                        G.tensor_tensor(mean, mean, probs1[:, n % 3, 0:GKEYS], ALU.add).then_inc(p1_added, 1)

                for n in range(TILES * H1 - 2):
                    e = probs1[:, n % 3, 0:GKEYS]
                    pool.wait_ge(e1_ready, n + 1)
                    pool.wait_ge(w1_ready, n + 1)
                    G.tensor_tensor(e, e, kept01[:, n % 2, 0:GKEYS], ALU.mult).then_inc(p1_kept, 1)
                    if n >= 1:
                        add_head(n - 1)
                add_head(TILES * H1 - 3)
                pool.wait_ge(f_done, TILES)
                nc.gpsimd.memset(q2z[0:D2, 1:H2:2, :], 0.0).then_inc(q2_clear, 1)
                nc.gpsimd.memset(q2z[D2:P, 0:H2:2, :], 0.0).then_inc(q2_clear, 1)
                pool.wait_ge(q2_clear, 2)
                pool.wait_ge(mix_ready, 1)
                pool.wait_ge(pv_ready, TILES)
                steps = [0]

                def link(ins):
                    steps[0] += 1
                    ins.then_inc(p_step, 1)
                    pool.wait_ge(p_step, steps[0])

                for g in range(1, H2 // 4):
                    mix_values(G, g, v_tmp2, link)
                    pool.drain().then_inc(v2_rest, 1)
                end_of_batch(pool, b)

        def attn_turned(act, A, t):
            if t >= 1:
                act.wait_ge(ctx_half, DCH * t)
            for j in range(4):
                act.wait_ge(aT_done, 4 * t + j + 1)
                k0, k1 = 4 * j, min(4 * j + 4, KCH)
                if k1 == KCH and KW[-1] < P:
                    A(attnT[0:KW[-1], KCH - 1, :], ps[0:KW[-1], 4 + j, (KCH - 1 - k0) * P:(KCH - k0) * P],
                      ACT.Copy).then_inc(aT_ready, 1)
                    k1 -= 1
                if k1 > k0:
                    A(attnT[:, k0:k1, :], ps[:, 4 + j, 0:(k1 - k0) * P].rearrange("p (k q) -> p k q", q=P),
                      ACT.Copy).then_inc(aT_ready, 1)

        @block.scalar
        def _(act):
            A = nc.scalar.activation
            RAD = -6.2831845
            act.wait_ge(setup_v, 1)
            A(s_t[5], s_t[4], ACT.Exp).then_inc(setup_a, 1)
            act.wait_ge(setup_v, 2)
            A(s_t[8], s_t[6], ACT.Exp).then_inc(setup_a, 1)
            act.wait_ge(setup_v, 3)
            A(s_t[9], s_t[9], ACT.Sin, scale=RAD, bias=quarter[:, 0:1]).then_inc(setup_a, 1)
            A(s_t[10], s_t[10], ACT.Sin, scale=RAD).then_inc(setup_a, 1)
            act.wait_ge(setup_v, 4)
            A(s_y, s_y, ACT.Sin, scale=RAD, bias=phase[:, 1:2]).then_inc(setup_a, 1)
            A(s_x, s_x, ACT.Sin, scale=RAD, bias=phase[:, 0:1]).then_inc(setup_a, 1)
            act.wait_ge(setup_v, 5)
            kw = k_w.rearrange("p a b -> p (a b)")
            A(kw, kw, ACT.Sin, scale=RAD, bias=phase[:, 0:1]).then_inc(setup_a, 1)
            act.wait_ge(setup_g, 1)
            A(s_e, s_e, ACT.Exp).then_inc(setup_a, 1)
            act.wait_ge(setup_v, 6)
            A(s_n[:, NW // 2:NW], s_n[:, NW // 2:NW], ACT.Exp).then_inc(setup_a, 1)
            act.wait_ge(setup_g, 2)
            A(s_n[:, 0:NW // 2], s_n[:, 0:NW // 2], ACT.Exp).then_inc(setup_a, 1)
            act.wait_ge(setup_done, 1)

            def in_deviation(n):
                act.wait_ge(in_var, TILES * n)
                A(ln_std[:, :], ln_mv[:, :, 1], ACT.Sqrt, bias=eps[:, 0:1]).then_inc(in_dev, 1)

            in_deviation(1)
            with act.Fori(0, NBATCH) as b:
                for c in range(DCH):
                    act.wait_ge(in_xT_done, DCH * b + c + 1 + 1)
                    A(xnT[:, c, :], ps[:, 4 + c, :], ACT.Copy).then_inc(in_xT_ready, 1)
                act.wait_ge(in_spilled_k, 48 * b + 1)
                act.wait_ge(in_spilled_q, 48 * b + 1)
                act.wait_ge(in_k_parts, DCH * b + 1)
                act.wait_ge(in_squares, 2 * b + 1)
                act.wait_ge(in_q_done, b + 1)
                for g in range(DCH):
                    A(q_f[:, g, :], ps[:, 6 + g, :], ACT.Identity, bias=bq0[:, g:g + 1], scale=D0 ** -0.5)
                    ins = A(q_p[:, 0, g, :], ps[:, 6 + g, :], ACT.Identity, bias=bq0[:, g:g + 1], scale=D0 ** -0.5)
                ins.then_inc(in_q_read, 1)
                n = 0
                for g in range(DCH):
                    for c0, w in COLS:
                        act.wait_ge(in_k_done, DCH * len(COLS) * b + n + 2)
                        A(k_f[:, g, c0:c0 + w], ps[:, n % 4, 0:w], ACT.Identity, bias=bk0[:, g:g + 1])
                        ins = A(k_p[:, 0, g, c0:c0 + w], ps[:, n % 4, 0:w], ACT.Identity, bias=bk0[:, g:g + 1])
                        n += 1
                    ins.then_inc(in_k_read, 1)
                    act.wait_ge(in_k_rest, DCH * b + g + 1)
                    A(k_p[:, 1, g, 0:GKEYS], k_r[:, g, :], ACT.Copy).then_inc(in_k_mid, 1)
                    if g == 0:
                        in_deviation(b + 2)
            act.wait_ge(path_known, 1)
            use_general = act.value_load(general[0:1, 0:1], min_val=0, max_val=1)

            def attend_bounded():
                for m in range(H0 * KCH // 2):
                    act.wait_ge(pair_scores, m + 1)
                    if m >= 4:
                        act.wait_ge(group_values, m // 2 - 1)
                    A(probs0[:, 2 * (m % 4):2 * (m % 4) + 2, :], ps[:, 2 * (m % 2):2 * (m % 2) + 2, :], ACT.Exp).then_inc(pair_probs, 1)

            def attend_general():
                act.wait_ge(nmax_parts, 1)
                for i in range(3):
                    act.dma_start(q_stack[NSPLIT + i:NSPLIT + i + 1, :, :], nm_p[0:H0, i, :]).then_inc(nmax_stacked, 16)
                for h in range(H0):
                    for k in range(KCH):
                        n = h * KCH + k
                        act.wait_ge(t0_clipped, n + 1)
                        A(probs0[0:KW[k], n % 4, :], probs0[0:KW[k], n % 4, :], ACT.Exp).then_inc(p0_ready, 1)
                        if h >= 1 and k == 2:
                            act.wait_ge(pv0_done, h * KCH)
                            if h >= 3:
                                act.wait_ge(o0_turned, h - 2)
                            A(o_part[:, (h - 1) % 2, :], ps[:, 4 + (h - 1) % 2, :], ACT.Copy).then_inc(o0_ready, 1)
                act.wait_ge(pv0_done, H0 * KCH)
                act.wait_ge(o0_turned, H0 - 2)
                A(o_part[:, (H0 - 1) % 2, :], ps[:, 4 + (H0 - 1) % 2, :], ACT.Copy).then_inc(o0_ready, 1)

            with act.Fori(0, NBATCH) as b:
                n_ln = [0]
                n_xT = [0]

                def deviation_of(t):
                    n_ln[0] += 1
                    act.wait_ge(ln_var, n_ln[0])
                    A(ln_std[:, t:t + 1], ln_mv[:, t, 1:2], ACT.Sqrt, bias=eps[:, 0:1]).then_inc(ln_dev, 1)

                def deviation():
                    n_ln[0] += TILES
                    act.wait_ge(ln_var, n_ln[0])
                    A(ln_std[:, :], ln_mv[:, :, 1], ACT.Sqrt, bias=eps[:, 0:1]).then_inc(ln_dev, 1)

                def turned():
                    for c in range(DCH):
                        n_xT[0] += 1
                        act.wait_ge(xT_done, n_xT[0])
                        A(xnT[:, c, :], ps[:, 4 + c, :], ACT.Copy).then_inc(xT_ready, 1)

                with act.If(use_general != 0):
                    attend_general()
                with act.Else():
                    attend_bounded()
                turned()

                for n, (c0, w) in enumerate(COLS):
                    act.wait_ge(c_done, n + 1)
                    A(kT1[:, c0:c0 + w], ps[:, 6 + n % 2, 0:w], ACT.Copy).then_inc(c_ready, 1)
                    if n == 2:
                        deviation()
                turned()
                for k in range(KCH):
                    n = len(COLS) + k
                    act.wait_ge(c_done, n + 1)
                    A(v1[0:KW[k], k, :], ps[0:KW[k], 6 + n % 2, 0:DIM], ACT.Copy).then_inc(c_ready, 1)
                act.wait_ge(gl_ready, 1)
                A(g_tmp[5], g_tmp[4], ACT.Exp).then_inc(g_exp, 1)
                for n in range(NEXP * ICH):
                    act.wait_ge(gv_done, n + 1)
                    if n >= 2:
                        act.wait_ge(fused_ready, n - 1)
                    A(silu[:, n % 2, :], ps[:, 2 * (n % 2), :], ACT.Silu).then_inc(silu_ready, 1)

                def turned1(bank, tokens):
                    n_xT[0] += 1
                    act.wait_ge(xT_done, n_xT[0])
                    A(xnT[:, :, tokens], bank, ACT.Copy).then_inc(xT_ready, 1)

                def queries1(n, bank, tokens):
                    act.wait_ge(q1_done, n + 1)
                    for h in range(H1):
                        r = slice(h * D1, (h + 1) * D1)
                        A(q1z[r, h, tokens], ps[r, bank, tokens], ACT.Copy,
                          scale=float(np.float32(1) / np.sqrt(np.float32(D1)))).then_inc(q1_ready, 1)

                first, rest = slice(0, P), slice(P, SEQ)
                deviation_of(0)
                turned1(ps[:, 0, 0:DCH * P].rearrange("p (c q) -> p c q", q=P), first)
                deviation_of(1)
                act.wait_ge(q1_clear, 1)
                queries1(0, 1, first)
                deviation_of(2)
                deviation_of(3)
                deviation()
                def score_out(n):
                    act.wait_ge(s1_done, n + 1)
                    if n >= 4:
                        act.wait_ge(w1_ready, n - 3)
                    if n == 3:
                        act.wait_ge(c_done, len(COLS) + KCH)
                    A(s_sb[n % 4][:, 0:GKEYS], wide(0, GKEYS), ACT.Copy).then_inc(s1_ready, 1)

                def context_out(t):
                    act.wait_ge(ctx_half, DCH * (t + 1))
                    A(c_tT[:, :, t * P:(t + 1) * P], ps[:, 4, 0:DCH * P].rearrange("p (c q) -> p c q", q=P), ACT.Copy).then_inc(ctx_ready, 1)

                def probs_used(n):
                    if n % H1:
                        act.wait_ge(p1_added, n - n // H1)
                    else:
                        act.wait_ge(p1_scaled, n + 1)

                def scale_head(n):
                    t = n // H1
                    act.wait_ge(p1_kept, n + 1)
                    act.wait_ge(w1_ready, n + 1)
                    if n % H1 == 0 and t >= 2:
                        act.wait_ge(aT_done, 4 * (t - 1))
                    p = probs1[:, n % 3, 0:GKEYS]
                    A(p if n % H1 else p_mean[:, t % 2, 0:GKEYS], p, ACT.Copy, scale=stat1[:, n % 3, WEIGHT:WEIGHT + 1]).then_inc(p1_scaled, 1)

                score_out(0)
                score_out(1)
                turned1(ps[:, 4:4 + DCH, rest], rest)
                queries1(1, 6, rest)
                for n in range(TILES * H1):
                    if n + 2 < TILES * H1:
                        score_out(n + 2)
                    act.wait_ge(top_ready, n + 1)
                    if n >= 3:
                        probs_used(n - 3)
                    bias = stat1[:, n % 3, NEG:NEG + 1]
                    A(probs1[:, n % 3, 0:GKEYS], s_sb[n % 4][:, 0:GKEYS], ACT.Exp, bias=bias).then_inc(e1_ready, 1)
                    act.wait_ge(count_done, n + 1)
                    A(kept_by_col[0:1, :], ps[0:1, 7, 3 * P:4 * P], ACT.Copy, accum_out=kept[0:1, n:n + 1]).then_inc(count_ready, 1)
                    A(top_e[:, n % 2, :], top[:, n % 2, :], ACT.Exp, bias=bias,
                      accum_out=stat1[:, n % 3, SUM:SUM + 1]).then_inc(sum1_ready, 1)
                    if 1 <= n < TILES * H1 - 1:
                        scale_head(n - 1)
                    if n % H1 == 2 and n > H1:
                        attn_turned(act, A, n // H1 - 1)
                    if n % H1 == 0 and n > H1:
                        context_out(n // H1 - 2)
                context_out(TILES - 2)
                attn_turned(act, A, TILES - 1)
                context_out(TILES - 1)
                for t in range(TILES):
                    deviation_of(t)
                turned()
                for i in range(HCH):
                    act.wait_ge(h_done, i + 1)
                    A(hid[:, i, :], ps[:, i % 4, :], ACT.Gelu, bias=b1[:, i:i + 1]).then_inc(h_ready, 1)
                for t in range(TILES):
                    deviation_of(t)
                    deviation_of(t)
                turned()
                for t in range(TILES):
                    act.wait_ge(pv_done, t + 1)
                    A(proj_v[:, t, :], ps[:, t, :], ACT.Copy).then_inc(pv_ready, 1)
                act.wait_ge(g2_read, 1)
                A(sig_v, gate_v, ACT.Sigmoid).then_inc(sig_ready, 1)
                act.wait_ge(q2_clear, 2)
                for i in range(H2 // 2):
                    act.wait_ge(qk2_done, 2 * i + 1)
                    for j in range(2):
                        r = slice(j * D2, (j + 1) * D2)
                        ins = A(q2z[r, 2 * i + j, :], ps[r, (2 * i) % 4, :], ACT.Copy, scale=D2 ** -0.5)
                    ins.then_inc(qk2_ready, 1)
                    act.wait_ge(qk2_done, 2 * i + 2)
                    A(kT2[:, i, :], ps[:, (2 * i + 1) % 4, :], ACT.Copy).then_inc(qk2_ready, 1)
                for n in range(NG + 2):
                    if n >= 2:
                        m = n - 2
                        act.wait_ge(p2T_done, m + 1)
                        if m >= 2:
                            act.wait_ge(o2_done, m - 1)
                        A(pT2[:, m % 2, :], ps[:, 2 + m % 2, :], ACT.Copy).then_inc(p2T_ready, 1)
                    if n < NG:
                        h, t = n // TILES, n % TILES
                        act.wait_ge(s2_max, n + 1)
                        if n >= 4:
                            act.wait_ge(p2T_done, n - 3)
                        A(p2[:, n % 4, :], ps[:, S2_BANKS[n % 4], :], ACT.Exp, bias=nmax2[:, t, h:h + 1],
                          accum_out=sums2[:, t, h:h + 1]).then_inc(p2_ready, 1)
                for t in range(TILES):
                    act.wait_ge(zT_done, t + 1)
                    if t >= 2:
                        act.wait_ge(r_done, t - 1)
                    A(zT[:, t % 2, :], ps[:, t % 2, :], ACT.Copy).then_inc(zT_ready, 1)
                end_of_batch(act, b)

        @block.tensor
        def _(pe):
            mm, tr = nc.tensor.matmul, nc.tensor.transpose
            pe.wait_ge(setup_v, 7)
            for g in range(DIM // 4):
                ins = mm(ps[:, g // 8, (g % 8) * 4 * LA:(g % 8 + 1) * 4 * LA], k_w[:, 4 * g:4 * g + 4, :].rearrange("p d b -> p (d b)"),
                         s_x[:, 4 * g * LA:4 * (g + 1) * LA], start=True, stop=True)
            ins.then_inc(setup_p, 1)
            pe.wait_ge(setup_v, 8)
            for j in range(FCH):
                for c in range(SEQ // P):
                    ins = mm(ps[:, 2 + j // 2, (j % 2) * DIM:(j % 2 + 1) * DIM], dft_s[:, c, j * P:(j + 1) * P], k_time[:, c, :],
                             start=(c == 0), stop=(c == SEQ // P - 1))
            ins.then_inc(setup_p, 1)
            pe.wait_ge(setup_done, 1)

            pe.sem_inc(in_k_done, 1)
            pe.sem_inc(in_xT_done, 1)
            pe.sem_inc(in_norms_done, 1)
            def in_turn(n):
                pe.wait_ge(in_xn, TILES * n + 1)
                for c in range(DCH):
                    for t in range(TILES):
                        ins = tr(ps[:, 4 + c, t * P:(t + 1) * P], xn[:, t, c * P:(c + 1) * P], ident[:, :])
                    ins.then_inc(in_xT_done, 1)

            in_turn(1)
            with pe.Fori(0, NBATCH) as b:
                pe.wait_ge(in_xT_ready, DCH * b + DCH)
                for g in range(DCH):
                    for c in range(DCH):
                        ins = mm(ps[:, 6 + g, :], wq0[:, c, g * P:(g + 1) * P], xnT[:, c, :], start=(c == 0), stop=(c == DCH - 1))
                ins.then_inc(in_q_done, 1)
                pe.wait_ge(in_ctx, 16 * b + 16)
                n = 0
                for g in range(DCH):
                    if g:
                        pe.wait_ge(in_k_read, DCH * b + g)
                    for c0, w in COLS:
                        for c in range(CTXCH):
                            ins = mm(ps[:, n % 4, 0:w], wk0[:, c, g * P:(g + 1) * P], ctxT[:, c, c0:c0 + w],
                                     start=(c == 0), stop=(c == CTXCH - 1))
                        ins.then_inc(in_k_done, 1)
                        n += 1
                pe.wait_ge(in_squares, 2 * b + 1 + 1)
                pe.wait_ge(in_q_read, b + 1)
                for g in range(DCH):
                    for j in range(P // QUARTER):
                        ins = mm(ps[QUARTER * j:QUARTER * (j + 1), 6, :], head_sum_w[:, g, :], q_sq[:, g, :], start=(g == 0), stop=(g == DCH - 1))
                ins.then_inc(in_norms_done, 1)
                pe.wait_ge(in_squares, 2 * b + 2 + 1)
                for g in range(DCH):
                    for j, (c0, w) in enumerate(COLS):
                        ins = mm(ps[QUARTER * j:QUARTER * (j + 1), 7, 0:w], head_sum_w[:, g, :], k_sq[:, g, c0:c0 + w],
                                 start=(g == 0), stop=(g == DCH - 1))
                ins.then_inc(in_norms_done, 1)
                in_turn(b + 2)
                pe.wait_ge(in_norms_read, 2 * b + 2 + 1)
                pe.wait_ge(in_k_read, DCH * b + DCH)
            pe.wait_ge(bounds_ready, 1)
            mm(ps[0:1, 7, 0:1], bounded[:, :], ones[:, :], start=True, stop=True).then_inc(bounds_done, 1)
            pe.wait_ge(path_known, 1)
            use_general = pe.value_load(general[0:1, 0:1], min_val=0, max_val=1)

            def attend_bounded():
                NCK = H0 * KCH

                def pair(m):
                    if m >= 2:
                        pe.wait_ge(pair_probs, m - 1)
                    for i in range(2):
                        n = 2 * m + i
                        h, k = n // KCH, n % KCH
                        if k == 0 and h % 4 == 0:
                            pe.wait_ge(stacked[h // 4], 32 * NSPLIT // D0)
                        ins = mm(ps[:, 2 * (m % 2) + i, :], k_stack[0:NSPLIT, h, k * P:(k + 1) * P], q_stack[0:NSPLIT, h, :],
                                 start=True, stop=True)
                    ins.then_inc(pair_scores, 1)

                def group(g):
                    pe.wait_ge(pair_probs, 2 * g + 2)
                    for n in range(4 * g, 4 * g + 4):
                        h, k = n // KCH, n % KCH
                        j = n % 4
                        if k == 0 and h >= 2:
                            pe.wait_ge(head_out, h - 1)
                        ins = mm(ps[32 * j:32 * j + 32, 4 + h % 2, :], v0[:, k, h * V0W:(h + 1) * V0W], probs0[:, n % 8, :],
                                 start=(k < 4), stop=(k >= KCH - 4))
                    ins.then_inc(group_values, 1)

                def turn(h):
                    pe.wait_ge(head_out, h + 1)
                    if h >= 2:
                        pe.wait_ge(attn0_ready, h - 1)
                    for t in range(TILES):
                        ins = mm(ps[:, 6 + h % 2, t * V0W:(t + 1) * V0W], o_part[:, h % 2, t * P:(t + 1) * P],
                                 fold[:, :], start=True, stop=True)
                    ins.then_inc(head_turned, 1)

                pair(0)
                pair(1)
                turned = 0
                for g in range(NCK // 4):
                    if g + 1 < NCK // 4:
                        pair(2 * g + 2)
                        pair(2 * g + 3)
                    group(g)
                    if 4 * (g - 1) >= KCH * (turned + 1):
                        turn(turned)
                        turned += 1
                for h in range(turned, H0):
                    turn(h)

            def attend_general():
                for g in range(4):
                    pe.wait_ge(stacked[g], 32 * NSPLIT // D0)
                for n in range(H0 * TILES):
                    h, t = n // TILES, n % TILES
                    if n >= 2:
                        pe.wait_ge(s0_read, n - 1)
                    for j, (c0, w) in enumerate(COLS):
                        ins = mm(ps[:, 4 * (n % 2) + j, 0:w], q_stack[0:NSPLIT, h, t * P:(t + 1) * P],
                                 k_stack[0:NSPLIT, h, c0:c0 + w], start=True, stop=True)
                    ins.then_inc(s0_ready, 1)
                pe.wait_ge(nmax_ready, 1)
                for t in range(TILES):
                    ins = tr(ps[0:H0, 0, t * P:(t + 1) * P], neg_max[:, t, :], ident[:, :])
                ins.then_inc(nmaxT_done, 1)
                pe.wait_ge(nmax_stacked, 48)
                pe.wait_ge(pads_ready, 3)

                def value_product(n):
                    h, k = n // KCH, n % KCH
                    j = k % 4
                    pe.wait_ge(p0_ready, n + 1)
                    if k == 0 and h >= 2:
                        pe.wait_ge(o0_ready, h - 1)
                    mm(ps[32 * j:32 * j + 32, 4 + h % 2, :], v0[0:KW[k], k, h * V0W:(h + 1) * V0W], probs0[0:KW[k], n % 4, :],
                       start=(k < 4), stop=(k >= KCH - 4)).then_inc(pv0_done, 1)

                def turn_head(h):
                    pe.wait_ge(o0_ready, h + 1)
                    if h >= 4:
                        pe.wait_ge(attn0_ready, h - 3)
                    for t in range(TILES):
                        ins = mm(ps[:, 7, (h % 4) * P + t * V0W:(h % 4) * P + (t + 1) * V0W], o_part[:, h % 2, t * P:(t + 1) * P],
                                 fold[:, :], start=True, stop=True)
                    ins.then_inc(o0_turned, 1)

                LAG = 3
                NCK = H0 * KCH
                for n in range(NCK + LAG):
                    if n < NCK:
                        h, k = n // KCH, n % KCH
                        if k == 0:
                            if h >= 1:
                                pe.wait_ge(low_ready, h)
                            mm(ps[:, 6, :], max_rows[:, :], q_stack[:, h, :], start=True, stop=True).then_inc(low_done, 1)
                        if n >= 4:
                            pe.wait_ge(t0_clipped, n - 3)
                        mm(ps[0:KW[k], n % 4, :], k_stack[:, h, k * P:k * P + KW[k]], q_stack[:, h, :],
                           start=True, stop=True).then_inc(t0_ready, 1)
                        if h >= 1 and k == 7:
                            turn_head(h - 1)
                    if n >= LAG:
                        value_product(n - LAG)
                turn_head(H0 - 1)
            with pe.Fori(0, NBATCH) as b:
                n_xT = [0]
                n_src = [0]

                def turn(src, ready=None):
                    for t in range(TILES):
                        if ready is not None:
                            pe.wait_ge(xn_ready, ready * TILES + t + 1)
                        for c in range(DCH):
                            ins = tr(ps[:, 4 + c, t * P:(t + 1) * P], src[:, t, c * P:(c + 1) * P], ident[:, :])
                            if t == TILES - 1:
                                ins.then_inc(xT_done, 1)
                    n_xT[0] += DCH

                pe.wait_ge(ctx_loaded, 16 * b + 16)
                for k in range(KCH):
                    if k >= 4:
                        pe.wait_ge(v0_ready, k - 3)
                    for c in range(CTXCH):
                        ins = mm(ps[0:KW[k], k % 4, 0:DIM], ctxT[:, c, k * P:k * P + KW[k]], wv0[:, c, :],
                                 start=(c == 0), stop=(c == CTXCH - 1))
                    ins.then_inc(v0_done, 1)
                pe.wait_ge(v0_ready, KCH)
                with pe.If(use_general != 0):
                    attend_general()
                with pe.Else():
                    attend_bounded()
                def context_item(n):
                    if n >= 2:
                        pe.wait_ge(c_ready, n - 1)
                    for c in range(CTXCH):
                        if n < len(COLS):
                            c0, w = COLS[n]
                            ins = mm(ps[:, 6 + n % 2, 0:w], wk1[:, c, :], ctxT[:, c, c0:c0 + w], start=(c == 0), stop=(c == CTXCH - 1))
                        else:
                            k = n - len(COLS)
                            ins = mm(ps[0:KW[k], 6 + n % 2, 0:DIM], ctxT[:, c, k * P:k * P + KW[k]], wv1[:, c, :],
                                     start=(c == 0), stop=(c == CTXCH - 1))
                    ins.then_inc(c_done, 1)

                pe.wait_ge(attn0_ready, H0 - 1)
                context_item(0)
                pe.wait_ge(attn0_ready, H0)
                turn(attn0)
                context_item(1)
                pe.wait_ge(xT_ready, n_xT[0])
                for t in range(TILES):
                    for c in range(DCH):
                        ins = mm(ps[:, t, 0:DIM], xnT[:, c, t * P:(t + 1) * P], wo0[:, c, :], start=(c == 0), stop=(c == DCH - 1))
                    ins.then_inc(y0_done, 1)

                for n in range(2, len(COLS) + KCH):
                    context_item(n)
                    if n == len(COLS) - 1:
                        turn(xn, 0)
                    if n == len(COLS) + 2:
                        pe.wait_ge(xT_ready, n_xT[0])
                        for t in range(TILES):
                            for c in range(DCH):
                                ins = mm(ps[:, 4, t * NEXP:(t + 1) * NEXP], xnT[:, c, t * P:(t + 1) * P], wg[:, c, :],
                                         start=(c == 0), stop=(c == DCH - 1))
                        ins.then_inc(gl_done, 1)

                pe.wait_ge(x1_ready, TILES)

                def expert_down(e, tiles=range(TILES)):
                    for t in tiles:
                        pe.wait_ge(fused_ready, ICH * (e + 1))
                        m = e * TILES + t
                        if m >= 4:
                            pe.wait_ge(down_read, m - 3)
                        for i in range(ICH):
                            ins = mm(ps[:, 4 + m % 4, 0:DIM], fused[:, e % 2, i * SEQ + t * P:i * SEQ + (t + 1) * P], w2e[e % 2][:, i, :],
                                     start=(i == 0), stop=(i == ICH - 1))
                        ins.then_inc(down_done, 1)

                for e in range(NEXP):
                    pe.wait_ge(w_loaded[e % 2], 48 * (e // 2 + 1))
                    for i in range(ICH):
                        n = e * ICH + i
                        if n >= 2:
                            pe.wait_ge(fused_ready, n - 1)
                        for j, w in enumerate((w11, w12)):
                            for c in range(DCH):
                                ins = mm(ps[:, 2 * (n % 2) + j, :], w[e % 2][:, c, i * P:(i + 1) * P], xnT[:, c, :],
                                         start=(c == 0), stop=(c == DCH - 1))
                        ins.then_inc(gv_done, 1)
                        if i == 1 and e >= 1:
                            expert_down(e - 1)
                def turn1(t, banks, col, last):
                    pe.wait_ge(xn_ready, TILES + t + 1)
                    for c in range(DCH):
                        ins = tr(ps[:, banks[c], col[c]:col[c] + P], xt[:, t, c * P:(c + 1) * P], ident[:, :])
                    if last:
                        ins.then_inc(xT_done, 1)
                        n_xT[0] += 1

                def queries1(bank, r):
                    pe.wait_ge(xT_ready, n_xT[0])
                    for c in range(DCH):
                        ins = mm(ps[:, bank, r], wq1[:, c, :], xnT[:, c, r], start=(c == 0), stop=(c == DCH - 1))
                    ins.then_inc(q1_done, 1)

                first, rest = slice(0, P), slice(P, SEQ)
                expert_down(NEXP - 1, [0, 1])
                turn1(0, [0] * DCH, [c * P for c in range(DCH)], True)
                expert_down(NEXP - 1, [2])
                queries1(1, first)
                expert_down(NEXP - 1, [3])
                pe.wait_ge(c_ready, len(COLS) + KCH)
                pe.wait_ge(q1_ready, H1)

                def scores(n):
                    if n >= 1:
                        pe.wait_ge(s1_ready, n)
                    t, h = n // H1, n % H1
                    if t == 1 and h == 0:
                        pe.wait_ge(q1_ready, 2 * H1)
                    for j, (c0, w) in enumerate(COLS):
                        mm(ps[:, j, 0:w], q1z[:, h, t * P:(t + 1) * P], kT1[:, c0:c0 + w], start=True, stop=False)
                        ins = mm(ps[:, j, 0:w], ones_row[:, :], mask_row[0:1, c0:c0 + w], start=False, stop=True)
                    ins.then_inc(s1_done, 1)

                def count(n):
                    pe.wait_ge(choice_ready, n + 1)
                    if n >= 1:
                        pe.wait_ge(count_ready, n)
                    for i in range(KCH):
                        k = -i % KCH
                        ins = mm(ps[0:1, 7, 3 * P:3 * P + KW[k]], ones_col[:, :], kept01[:, n % 2, k * P:k * P + KW[k]],
                                 start=(i == 0), stop=(i == KCH - 1))
                    ins.then_inc(count_done, 1)

                def turn_probs(t, chunks):
                    pe.wait_ge(p1_added, (H1 - 1) * (t + 1))
                    if t >= 1:
                        pe.wait_ge(aT_ready, 4 * t)
                        pe.wait_ge(ctx_ready, t)
                    for k in chunks:
                        ins = tr(ps[0:KW[k], 4 + k // 4, (k % 4) * P:(k % 4 + 1) * P], p_mean[:, t % 2, k * P:k * P + KW[k]], ident[:, :])
                        if k % 4 == 3 or k == KCH - 1:
                            ins.then_inc(aT_done, 1)

                def context(t, c):
                    pe.wait_ge(aT_ready, 4 * t + 4)
                    for k in range(KCH):
                        ins = mm(ps[:, 4, c * P:(c + 1) * P], v1[0:KW[k], k, c * P:(c + 1) * P], attnT[0:KW[k], k, :],
                                 start=(k == 0), stop=(k == KCH - 1))
                    ins.then_inc(ctx_half, 1)

                pe.wait_ge(mask_ready, 1)
                scores(0)
                scores(1)
                pe.wait_ge(down_read, NEXP * TILES)
                for t in range(1, TILES):
                    turn1(t, [4 + c for c in range(DCH)], [t * P] * DCH, t == TILES - 1)
                queries1(6, rest)
                for n in range(TILES * H1):
                    if n + 2 < TILES * H1:
                        scores(n + 2)
                    if n % H1 == 2 and n > H1:
                        turn_probs(n // H1 - 1, range(KCH - 1))
                    if n % H1 == 0 and n > H1:
                        context(n // H1 - 2, 1)
                    if n % H1 == 3 and n > H1:
                        pe.wait_ge(aT_ready, 4 * (n // H1))
                    count(n)
                    if n % H1 == 3 and n > H1:
                        context(n // H1 - 1, 0)
                    if n % H1 == 2 and n > H1:
                        pe.wait_ge(count_ready, n + 1)
                        turn_probs(n // H1 - 1, [KCH - 1])
                context(TILES - 2, 1)
                pe.wait_ge(count_ready, TILES * H1)
                turn_probs(TILES - 1, range(KCH))
                for c in range(DCH):
                    context(TILES - 1, c)

                pe.wait_ge(ctx_ready, TILES)
                def film(i):
                    for t in range(TILES):
                        n = i * TILES + t
                        if n >= 4:
                            pe.wait_ge(film_read, n - 3)
                        for c in range(DCH):
                            ins = mm(ps[:, n % 4, :], c_tT[:, c, t * P:(t + 1) * P], film_w[:, i, c, :], start=(c == 0), stop=(c == DCH - 1))
                        ins.then_inc(film_done, 1)

                film(0)
                pe.wait_ge(u_ready, TILES)
                pe.wait_ge(dft_loaded, 16)
                for j in range(FCH // 2):
                    for half in range(2):
                        for c in range(SEQ // P):
                            ins = mm(ps[:, 4 + j, half * DIM:(half + 1) * DIM], dft[:, c, (half * (FCH // 2) + j) * P:(half * (FCH // 2) + j + 1) * P],
                                     u[:, c, :], start=(c == 0), stop=(c == SEQ // P - 1))
                    ins.then_inc(spec_done, 1)
                film(1)
                pe.wait_ge(spec_ready, FCH // 2)
                pe.wait_ge(idft_loaded, 16)
                pe.wait_ge(film_read, 2 * TILES)
                for t in range(TILES):
                    for j in range(FCH):
                        ins = mm(ps[:, t, 0:DIM], idft[:, j, t * P:(t + 1) * P], spec[:, j, :], start=(j == 0), stop=(j == FCH - 1))
                    ins.then_inc(y1_done, 1)

                turn(xn, 2)
                pe.wait_ge(xT_ready, n_xT[0])
                pe.wait_ge(ff_loaded, 32)
                for i in range(HCH):
                    if i >= 4:
                        pe.wait_ge(h_ready, i - 3)
                    for c in range(DCH):
                        ins = mm(ps[:, i % 4, :], wf1[:, c, i * P:(i + 1) * P], xnT[:, c, :], start=(c == 0), stop=(c == DCH - 1))
                    ins.then_inc(h_done, 1)
                pe.wait_ge(h_ready, HCH)
                for t in range(TILES):
                    for i in range(HCH):
                        ins = mm(ps[:, t, 0:DIM], hid[:, i, t * P:(t + 1) * P], wf2[:, i, :], start=(i == 0), stop=(i == HCH - 1))
                    ins.then_inc(f_done, 1)

                turn(xn, 3)
                pe.wait_ge(xT_ready, n_xT[0])
                pe.wait_ge(w2_loaded, 16 * 5)
                for t in range(TILES):
                    for j in range(2):
                        for c in range(DCH):
                            ins = mm(ps[:, 6 + j, t * P:(t + 1) * P], xnT[:, c, t * P:(t + 1) * P], wsd[:, c, j * P:(j + 1) * P],
                                     start=(c == 0), stop=(c == DCH - 1))
                ins.then_inc(g2_done, 1)
                for t in range(TILES):
                    for c in range(DCH):
                        ins = mm(ps[:, t, :], xnT[:, c, t * P:(t + 1) * P], wv2[:, c, :], start=(c == 0), stop=(c == DCH - 1))
                    ins.then_inc(pv_done, 1)
                pe.wait_ge(pv_ready, TILES)
                for i in range(H2):
                    w = wk2 if i % 2 else wq2
                    if i >= 4:
                        pe.wait_ge(qk2_ready, i - 3)
                    for c in range(DCH):
                        ins = mm(ps[:, i % 4, :], w[:, c, (i // 2) * P:(i // 2 + 1) * P], xnT[:, c, :], start=(c == 0), stop=(c == DCH - 1))
                    ins.then_inc(qk2_done, 1)
                pe.wait_ge(qk2_ready, H2)
                pe.wait_ge(g2_read, 2)

                def turn_p2(n):
                    pe.wait_ge(p2_ready, n + 1)
                    if n >= 2:
                        pe.wait_ge(p2T_ready, n - 1)
                    for j in range(TILES):
                        ins = tr(ps[:, 2 + n % 2, j * P:(j + 1) * P], p2[:, n % 4, j * P:(j + 1) * P], ident[:, :])
                    ins.then_inc(p2T_done, 1)

                def value2(n):
                    h, t = n // TILES, n % TILES
                    if n == 0:
                        pe.wait_ge(v2_first, 1)
                    if t == 0 and h % 4 == 0 and h:
                        pe.wait_ge(v2_rest, h // 4)
                    pe.wait_ge(p2T_ready, n + 1)
                    if t == 0 and h >= 2:
                        pe.wait_ge(gated, h - 1)
                    for j in range(TILES):
                        ins = mm(ps[:, 4 + h % 2, t * D2:(t + 1) * D2], pT2[:, n % 2, j * P:(j + 1) * P],
                                 v2[:, j, h * D2:(h + 1) * D2], start=(j == 0), stop=(j == TILES - 1))
                    ins.then_inc(o2_done, 1)

                for n in range(NG + 3):
                    if n < NG:
                        h, t = n // TILES, n % TILES
                        if n >= 4:
                            pe.wait_ge(p2_ready, n - 3)
                        mm(ps[:, S2_BANKS[n % 4], :], q2z[:, h, t * P:(t + 1) * P], kT2[:, h // 2, :], start=True, stop=True).then_inc(s2_done, 1)
                    if 2 <= n < NG + 2:
                        turn_p2(n - 2)
                    if n >= 3:
                        value2(n - 3)
                for t in range(TILES + 1):
                    if t < TILES:
                        pe.wait_ge(z_ready, t + 1)
                        if t >= 2:
                            pe.wait_ge(zT_ready, t - 1)
                        for c in range(TILES):
                            ins = tr(ps[:, t % 2, c * P:(c + 1) * P], z[:, t, c * P:(c + 1) * P], ident[:, :])
                        ins.then_inc(zT_done, 1)
                    if t >= 1:
                        m = t - 1
                        pe.wait_ge(zT_ready, m + 1)
                        if m >= 2:
                            pe.wait_ge(out_ready, m - 1)
                        for c in range(TILES):
                            ins = mm(ps[:, 6 + m % 2, 0:DIM], zT[:, m % 2, c * P:(c + 1) * P], wo2[:, c, :], start=(c == 0), stop=(c == TILES - 1))
                        ins.then_inc(r_done, 1)
                end_of_batch(pe, b)

        @block.vector
        def _(dve):
            V = nc.vector
            steps = [0]
            step_sem = [setup_v]

            def setup_program():
                count = [0]
                own = [0]
                chain = ctx.enter_context(nc.semaphore("setup_step"))

                def link(ins):
                    own[0] += 1
                    ins.then_inc(chain, 1)
                    dve.wait_ge(chain, own[0])

                def done(n):
                    count[0] += 1
                    assert count[0] == n
                    dve.drain().then_inc(setup_v, 1)

                link(V.memset(eps[:, :], LN_EPS))
                link(V.memset(ones[:, :], 1.0))
                link(V.memset(ones_row[:, :], 1.0))
                link(V.memset(ones_col[:, :], 1.0))
                link(V.memset(bounded[:, :], 1.0))
                link(V.memset(quarter[:, :], float(np.float32(TWO_PI / 4))))
                dve.wait_ge(s4d_loaded, 16 * 11)
                done(1)
                ar, ai, dt, turns = s_t[6], s_t[7], s_t[5], s_t[11]
                dve.wait_ge(setup_a, 1)
                link(V.tensor_tensor(ar, s_t[0], dt, ALU.mult))
                done(2)
                link(V.tensor_tensor(ai, s_t[1], dt, ALU.mult))
                link(V.tensor_scalar(turns, ai, 1.0 / TWO_PI, None, ALU.mult))

                def whole_turns(out, u, ahead):
                    return V.tensor_scalar(out, u, ahead, MAGIC, ALU.add, ALU.add)

                def back(out, whole, u):
                    return V.scalar_tensor_tensor(out, whole, MAGIC, u, ALU.subtract, ALU.subtract)

                whole_turns(s_t[9], turns, 0.25)
                link(whole_turns(s_t[10], turns, 0.0))
                back(s_t[9], s_t[9], turns)
                link(back(s_t[10], s_t[10], turns))
                done(3)
                kb = ramp[:, 0:LB].unsqueeze(1).to_broadcast([P, DIM, LB])
                ka = ramp[:, LB:LB + LA].unsqueeze(1).to_broadcast([P, DIM, LA])
                kw = k_w.rearrange("p a b -> p (a b)")
                sx3, sy3 = (v.rearrange("p (d a) -> p d a", a=LA) for v in (s_x, s_y))
                link(V.tensor_tensor(sx3, turns.unsqueeze(2).to_broadcast([P, DIM, LA]), ka, ALU.mult))
                whole_turns(s_n[:, 0:NPW], s_x, phase[:, 2:3])
                link(whole_turns(s_n[:, NPW:NW], s_x, phase[:, 3:4]))
                link(back(s_y, s_n[:, NPW:NW], s_x))
                link(back(s_x, s_n[:, 0:NPW], s_x))
                done(4)
                link(V.tensor_tensor(k_w, turns.unsqueeze(2).to_broadcast([P, DIM, LB]), kb, ALU.mult))
                link(whole_turns(s_n, kw, phase[:, 2:3]))
                link(back(kw, s_n, kw))
                done(5)
                link(V.tensor_tensor(s_n3[:, DIM // 2:DIM, :], ar[:, DIM // 2:DIM].unsqueeze(2).to_broadcast([P, DIM // 2, LB]),
                                     kb[:, DIM // 2:DIM, :], ALU.mult))
                done(6)
                dve.wait_ge(setup_a, 4)
                er, ei, den, br, bi, t0, t1 = s_t[9], s_t[10], s_t[11], s_t[12], s_t[13], s_t[14], s_t[15]
                link(V.tensor_tensor(er, er, s_t[8], ALU.mult))
                link(V.tensor_scalar(er, er, -1.0, None, ALU.add))
                link(V.tensor_tensor(ei, ei, s_t[8], ALU.mult))
                link(V.tensor_tensor(den, s_t[0], s_t[0], ALU.mult))
                link(V.tensor_tensor(t0, s_t[1], s_t[1], ALU.mult))
                link(V.tensor_tensor(den, den, t0, ALU.add))
                link(V.reciprocal(den, den))

                def cmul(out, p, q, r, s, sign):
                    V.tensor_tensor(t0, p, q, ALU.mult)
                    link(V.tensor_tensor(t1, r, s, ALU.mult))
                    link(V.tensor_tensor(out, t0, t1, ALU.add if sign > 0 else ALU.subtract))

                cmul(br, er, s_t[0], ei, s_t[1], 1)
                cmul(bi, ei, s_t[0], er, s_t[1], -1)
                link(V.tensor_tensor(br, br, den, ALU.mult))
                link(V.tensor_tensor(bi, bi, den, ALU.mult))
                g1, g2 = s_t[4], s_t[5]
                cmul(g1, s_t[2], br, s_t[3], bi, -1)
                cmul(g2, s_t[2], bi, s_t[3], br, 1)
                V.tensor_scalar(g1[0:NSTATE, :], g1[0:NSTATE, :], 2.0, None, ALU.mult)
                V.tensor_scalar(g1[NSTATE:P, :], g1[NSTATE:P, :], -2.0, None, ALU.mult)
                link(V.tensor_scalar(g2, g2, -2.0, None, ALU.mult))
                dve.wait_ge(setup_a, 6)
                V.tensor_tensor(sx3, sx3, g1.unsqueeze(2).to_broadcast([P, DIM, LA]), ALU.mult)
                link(V.tensor_tensor(sy3, sy3, g2.unsqueeze(2).to_broadcast([P, DIM, LA]), ALU.mult))
                link(V.tensor_tensor(s_x, s_x, s_y, ALU.add))
                dve.wait_ge(setup_a, 8)
                V.tensor_tensor(s_x, s_x, s_e, ALU.mult)
                dve.wait_ge(setup_a, 9)
                V.tensor_tensor(kw[:, NW // 2:NW], kw[:, NW // 2:NW], s_n[:, NW // 2:NW], ALU.mult)
                dve.wait_ge(setup_a, 10)
                link(V.tensor_tensor(kw[:, 0:NW // 2], kw[:, 0:NW // 2], s_n[:, 0:NW // 2], ALU.mult))
                dve.wait_ge(consts, 16 * len(NLOADS))
                link(V.tensor_scalar(bq0[:, :], bq0[:, :], D0 ** -0.5, None, ALU.mult))
                V.tensor_scalar(film_w[:, :, :, :], film_w[:, :, :, :], mod_gate[:, 0:1], None, ALU.mult)
                link(V.tensor_scalar(film_b[:, :, :], film_b[:, :, :], mod_gate[:, 0:1], None, ALU.mult))
                done(7)
                dve.wait_ge(setup_p, 1)
                blocks = ps[:, :, :].rearrange("p k (g d a) -> p (k g) d a", d=4, a=LA)
                for d in range(4):
                    for j in range(4):
                        ins = V.tensor_copy(k_time[LB * j:LB * (j + 1), :, d::4].rearrange("p c g -> p g c"),
                                            blocks[LB * d:LB * (d + 1), :, d, j::4])
                link(ins)
                done(8)
                dve.wait_ge(setup_p, 2)
                half = FCH // 2
                spec_k = ps[:, 2:6, :].rearrange("p b (j d) -> p (b j) d", d=DIM)
                link(V.tensor_copy(k_cos[:, :, :], spec_k[:, 0:half, :]))
                link(V.tensor_copy(k_sin[:, :, :], spec_k[:, half:FCH, :]))
                link(V.tensor_copy(k_cos0[:, :], k_cos[:, 0, :]))
                link(V.tensor_copy(k_cos0[0:1, :], k_sin[0:1, 0, :]))
                link(V.memset(k_sin[0:1, 0, :], 0.0))
                dve.drain().then_inc(setup_done, 1)

            setup_program()

            IN_STEPS = 5

            def in_tokens(n):
                dve.wait_ge(in_x, 16 * n)
                dve.wait_ge(in_xT_done, DCH * (n - 1) + 1)
                for t in range(TILES):
                    V.bn_stats(ln_stats[:, t, :], x[:, t, :])
                dve.drain()
                for t in range(TILES):
                    V.bn_aggr(ln_mv[:, t, :], ln_stats[:, t, :]).then_inc(in_var, 1)
                dve.wait_ge(in_dev, n)
                V.reciprocal(ln_rstd[:, :], ln_std[:, :])
                dve.drain()
                for t in range(TILES):
                    V.tensor_scalar(xn[:, t, :], x[:, t, :], ln_mv[:, t, 0:1], ln_rstd[:, t:t + 1], ALU.subtract, ALU.mult).then_inc(in_xn, 1)

            def prepare(b):
                steps = [0]

                def link(ins):
                    steps[0] += 1
                    ins.then_inc(in_step, 1)
                    dve.wait_ge(in_step, IN_STEPS * b + steps[0])

                dve.wait_ge(in_spilled_k, 48 * b + 1)
                dve.wait_ge(in_spilled_q, 48 * b + 1)
                dve.wait_ge(in_q_read, b + 1)
                link(V.tensor_tensor(q_r, q_f, q_p[:, 0], ALU.subtract))
                link(V.tensor_copy(q_p[:, 1], q_r))
                V.tensor_tensor(q_p[:, 2], q_r, q_p[:, 1], ALU.subtract).then_inc(in_q_parts, 1)
                for g in range(DCH):
                    dve.wait_ge(in_k_read, DCH * b + g + 1)
                    V.tensor_tensor(k_r[:, g, :], k_f[:, g, :], k_p[:, 0, g, 0:GKEYS], ALU.subtract).then_inc(in_k_rest, 1)
                    if g == 0:
                        in_tokens(b + 2)
                    dve.wait_ge(in_k_mid, DCH * b + g + 1)
                    V.tensor_tensor(k_p[:, 2, g, 0:GKEYS], k_r[:, g, :], k_p[:, 1, g, 0:GKEYS], ALU.subtract).then_inc(in_k_parts, 1)
                dve.wait_ge(in_norms_done, 2 * b + 1 + 1)
                V.tensor_reduce(norms[:, 0:1], ps[:, 6, :], AX.X, ALU.max).then_inc(in_norms_read, 1)
                dve.wait_ge(in_norms_done, 2 * b + 2 + 1)
                full = QUARTER * (len(COLS) - 1)
                V.tensor_reduce(norms[0:full, 1:2], ps[0:full, 7, :], AX.X, ALU.max)
                V.tensor_reduce(norms[full:P, 1:2], ps[full:P, 7, 0:COLS[-1][1]], AX.X, ALU.max).then_inc(in_norms_read, 1)
                dve.wait_ge(in_norms_read, 2 * b + 2 + 1)
                link(V.tensor_tensor(norms[:, 2:3], norms[:, 0:1], norms[:, 1:2], ALU.mult))
                link(V.tensor_scalar(norms[:, 3:4], norms[:, 2:3], BOUND * BOUND, None, ALU.is_le))
                link(V.tensor_tensor(bounded[:, :], bounded[:, :], norms[:, 3:4], ALU.mult))
                assert steps[0] == IN_STEPS

            V.memset(k_p[:, :, :, GKEYS:KPAD], 0.0)
            dve.sem_inc(in_xn, 1)
            dve.sem_inc(in_k_parts, 1)
            dve.sem_inc(in_norms_read, 1)
            in_tokens(1)
            with dve.Fori(0, NBATCH) as b:
                prepare(b)
            dve.drain().then_inc(bounds_ready, 1)
            dve.wait_ge(bounds_done, 1)
            V.tensor_scalar(general[0:1, 0:1], ps[0:1, 7, 0:1], P - 0.5, None, ALU.is_lt)
            dve.drain().then_inc(path_known, 1)
            dve.wait_ge(path_known, 1)
            use_general = dve.value_load(general[0:1, 0:1], min_val=0, max_val=1)

            def per(v, n):
                return v.unsqueeze(2).to_broadcast([P, v.shape[1], n])

            def head_rows(h, out, turned, link):
                dve.wait_ge(turned, h + 1)
                o4 = out.rearrange("p (t d) -> p t d", d=V0W)
                r = small[:, TILES * h:TILES * (h + 1)]
                link(V.reciprocal(r, o4[:, :, D0]))
                V.tensor_tensor(attn0[:, :, h * D0:(h + 1) * D0], o4[:, :, 0:D0], per(r, D0), ALU.mult).then_inc(attn0_ready, 1)

            def attend_bounded():
                steps = [0]

                def link(ins):
                    steps[0] += 1
                    ins.then_inc(head_step, 1)
                    dve.wait_ge(head_step, steps[0])

                for h in range(H0):
                    dve.wait_ge(group_values, (KCH * h + KCH - 1) // 4 + 1)
                    if h >= 2:
                        dve.wait_ge(head_turned, h - 1)
                    V.tensor_copy(o_part[:, h % 2, :], ps[:, 4 + h % 2, :]).then_inc(head_out, 1)
                    if h >= 1:
                        head_rows(h - 1, ps[:, 6 + (h - 1) % 2, 0:TILES * V0W], head_turned, link)
                head_rows(H0 - 1, ps[:, 6 + (H0 - 1) % 2, 0:TILES * V0W], head_turned, link)

            def attend_general():
                steps = [0]

                def link(ins):
                    steps[0] += 1
                    ins.then_inc(general_step, 1)
                    dve.wait_ge(general_step, steps[0])

                link(V.memset(as_words(q_stack[NSPLIT:P, :, :]), 0.0))
                link(V.memset(as_words(k_stack[NSPLIT:P, :, :]), 0.0))
                V.memset(as_words(k_stack[NSPLIT:NSPLIT + 3, :, :]), TWO_ONES)
                dve.drain().then_inc(pads_ready, 3)
                for n in range(H0 * TILES):
                    h, t = n // TILES, n % TILES
                    dve.wait_ge(s0_ready, n + 1)
                    V.tensor_reduce(row_max[:, t, h:h + 1], wide(4 * (n % 2), GKEYS), AX.X, ALU.max).then_inc(s0_read, 1)
                dve.wait_ge(s0_read, H0 * TILES)
                link(V.tensor_scalar(neg_max, row_max, -CLAMP, CLAMP, ALU.max, ALU.min))
                V.tensor_scalar(neg_max, neg_max, -1.0, None, ALU.mult).then_inc(nmax_ready, 1)
                dve.wait_ge(nmaxT_done, 1)
                link(V.tensor_copy(nm_f[0:H0, :], ps[0:H0, 0, :]))
                link(V.tensor_copy(nm_p[0:H0, 0, :], nm_f[0:H0, :]))
                link(V.tensor_tensor(nm_r[0:H0, :], nm_f[0:H0, :], nm_p[0:H0, 0, :], ALU.subtract))
                link(V.tensor_copy(nm_p[0:H0, 1, :], nm_r[0:H0, :]))
                V.tensor_tensor(nm_p[0:H0, 2, :], nm_r[0:H0, :], nm_p[0:H0, 1, :], ALU.subtract).then_inc(nmax_parts, 1)

                for h in range(H0):
                    dve.wait_ge(low_done, h + 1)
                    V.tensor_scalar(low[:, h % 2, :], ps[:, 6, :], -CLAMP, None, ALU.add).then_inc(low_ready, 1)
                    dve.wait_ge(low_ready, h + 1)
                    for k in range(KCH):
                        n = h * KCH + k
                        dve.wait_ge(t0_ready, n + 1)
                        if n >= 4:
                            dve.wait_ge(pv0_done, n - 3)
                        w = KW[k]
                        V.scalar_tensor_tensor(probs0[0:w, n % 4, :], ps[0:w, n % 4, :], 0.0, low[0:w, h % 2, :],
                                               ALU.min, ALU.max).then_inc(t0_clipped, 1)
                        if h >= 1 and k == 11:
                            head_rows(h - 1, ps[:, 7, (h - 1) % 4 * P:((h - 1) % 4 + 1) * P], o0_turned, link)
                head_rows(H0 - 1, ps[:, 7, (H0 - 1) % 4 * P:((H0 - 1) % 4 + 1) * P], o0_turned, link)
            with dve.Fori(0, NBATCH) as b:
                steps = [0]
                n_ln = [0, 0]

                def link(ins):
                    steps[0] += 1
                    ins.then_inc(v_step, 1)
                    dve.wait_ge(v_step, steps[0])

                def layernorm(dst, src, ready):
                    n_ln[0] += TILES
                    n_ln[1] += 1
                    for t in range(TILES):
                        link(V.bn_stats(ln_stats[:, t, :], src[:, t, :]))
                    for t in range(TILES):
                        V.bn_aggr(ln_mv[:, t, :], ln_stats[:, t, :]).then_inc(ln_var, 1)
                    dve.wait_ge(ln_dev, n_ln[1])
                    link(V.reciprocal(ln_rstd[:, :], ln_std[:, :]))
                    for t in range(TILES):
                        ins = V.tensor_scalar(dst[:, t, :], src[:, t, :], ln_mv[:, t, 0:1], ln_rstd[:, t:t + 1], ALU.subtract, ALU.mult)
                        ins.then_inc(ready, 1)

                def normalise(dst, src, t):
                    link(V.bn_stats(ln_stats[:, t, :], src[:, t, :]))
                    V.bn_aggr(ln_mv[:, t, :], ln_stats[:, t, :]).then_inc(ln_var, 1)
                    n_ln[0] += 1
                    n_ln[1] += 1
                    dve.wait_ge(ln_dev, n_ln[1])
                    link(V.reciprocal(ln_rstd[:, t:t + 1], ln_std[:, t:t + 1]))
                    return V.tensor_scalar(dst[:, t, :], src[:, t, :], ln_mv[:, t, 0:1], ln_rstd[:, t:t + 1], ALU.subtract, ALU.mult)

                def affine(dst, src, t, gain, tmp, offset):
                    link(V.bn_stats(ln_stats[:, t, :], src[:, t, :]))
                    V.bn_aggr(ln_mv[:, t, :], ln_stats[:, t, :]).then_inc(ln_var, 1)
                    n_ln[0] += 1
                    n_ln[1] += 1
                    dve.wait_ge(ln_var, n_ln[0])
                    V.scalar_tensor_tensor(tmp, src[:, t, :], ln_mv[:, t, 0:1], gain, ALU.subtract, ALU.mult)
                    dve.wait_ge(ln_dev, n_ln[1])
                    link(V.reciprocal(ln_rstd[:, t:t + 1], ln_std[:, t:t + 1]))
                    return V.scalar_tensor_tensor(dst, tmp, ln_rstd[:, t:t + 1], offset, ALU.mult, ALU.add)

                def rows(v):
                    return v.unsqueeze(1).to_broadcast([P, TILES, DIM])

                def top2(vals, m, oh1, oh2, tmp):
                    n = vals.shape[1]
                    first = prio[:, :].unsqueeze(1).to_broadcast([P, n, NEXP])
                    for k, oh in enumerate((oh1, oh2)):
                        src = vals if k == 0 else tmp
                        link(V.tensor_reduce(m, src, AX.X, ALU.max))
                        link(V.tensor_tensor(oh, src, per(m, NEXP), ALU.is_equal))
                        link(V.tensor_tensor(oh, oh, first, ALU.mult))
                        link(V.tensor_reduce(m, oh, AX.X, ALU.max))
                        link(V.tensor_tensor(oh, oh, per(m, NEXP), ALU.is_equal))
                        if k == 0:
                            link(V.scalar_tensor_tensor(tmp, oh, DROPPED, vals, ALU.mult, ALU.add))

                dve.wait_ge(v0_pads, 5)
                for k in range(KCH):
                    dve.wait_ge(v0_done, k + 1)
                    w = KW[k]
                    V.tensor_tensor(v0[0:w, k, :].rearrange("p (h w) -> p h w", w=V0W)[:, :, 0:D0],
                                    ps[0:w, k % 4, 0:DIM].rearrange("p (h d) -> p h d", d=D0),
                                    bv0[0:w, :].rearrange("p (h d) -> p h d", d=D0), ALU.add).then_inc(v0_ready, 1)
                dve.wait_ge(loaded, 32)
                link(V.tensor_copy(tmask[:, :], tmask8[:, :]))
                with dve.If(use_general != 0):
                    attend_general()
                with dve.Else():
                    attend_bounded()
                dve.wait_ge(attn0_ready, H0)
                for t in range(TILES):
                    dve.wait_ge(y0_done, t + 1)
                    link(V.tensor_tensor(x[:, t, :], x[:, t, :], ps[:, t, 0:DIM], ALU.add))
                    V.tensor_tensor(x[:, t, :], x[:, t, :], bo0[:, :], ALU.add).then_inc(x1_ready, 1)
                dve.wait_ge(x1_ready, TILES)

                layernorm(xn, x, xn_ready)
                dve.wait_ge(gl_done, 1)
                link(V.tensor_copy(gl, ps[:, 4, 0:TILES * NEXP].rearrange("p (t e) -> p t e", e=NEXP)))
                link(V.tensor_reduce(g_red[0], gl, AX.X, ALU.max))
                V.tensor_tensor(g_tmp[4], gl, per(g_red[0], NEXP), ALU.subtract).then_inc(gl_ready, 1)
                top2(gl, g_red[1], g_tmp[0], g_tmp[1], g_tmp[2])
                dve.wait_ge(g_exp, 1)
                link(V.tensor_reduce(g_red[2], g_tmp[5], AX.X, ALU.add))
                link(V.reciprocal(g_red[2], g_red[2]))
                link(V.tensor_tensor(g_tmp[5], g_tmp[5], per(g_red[2], NEXP), ALU.mult))
                link(V.tensor_tensor(g_tmp[0], g_tmp[0], g_tmp[1], ALU.add))
                link(V.tensor_tensor(g_w, g_tmp[0], g_tmp[5], ALU.mult))
                link(V.tensor_reduce(g_red[3], g_w, AX.X, ALU.add))
                link(V.tensor_scalar(g_red[3], g_red[3], 1e-8, None, ALU.add))
                link(V.reciprocal(g_red[3], g_red[3]))
                link(V.tensor_tensor(g_w, g_w, per(g_red[3], NEXP), ALU.mult))

                def expert_sum(e, tiles=range(TILES)):
                    for t in tiles:
                        m = e * TILES + t
                        dve.wait_ge(down_done, m + 1)
                        if e:
                            dve.wait_ge(down_read, m - TILES + 1)
                        V.scalar_tensor_tensor(x[:, t, :], ps[:, 4 + m % 4, 0:DIM], g_w[:, t, e:e + 1], x[:, t, :],
                                               ALU.mult, ALU.add).then_inc(down_read, 1)

                for e in range(NEXP):
                    for i in range(ICH):
                        n = e * ICH + i
                        dve.wait_ge(silu_ready, n + 1)
                        if e >= 2 and i == 0:
                            dve.wait_ge(down_done, TILES * (e - 1))
                        V.tensor_tensor(fused[:, e % 2, i * SEQ:(i + 1) * SEQ], silu[:, n % 2, :], ps[:, 2 * (n % 2) + 1, :],
                                        ALU.mult).then_inc(fused_ready, 1)
                        if e >= 1 and i == 3:
                            expert_sum(e - 1)

                dve.wait_ge(loaded, 48)
                V.tensor_scalar(mask_row[0:1, :], mask8[0:1, :], MASKED, MASKED, ALU.mult, ALU.subtract).then_inc(mask_ready, 1)
                for t in range(TILES):
                    expert_sum(NEXP - 1, [t])
                    dve.wait_ge(down_read, TILES * (NEXP - 1) + t + 1)
                    normalise(xt, x, t).then_inc(xn_ready, 1)
                dve.wait_ge(xn_ready, 2 * TILES)
                layernorm(xn, xt, in_normal)

                def settle(n):
                    s, cut = s_sb[n % 4][:, 0:GKEYS], s_cut[:, 0:GKEYS]
                    st = stat1[:, n % 3]
                    dve.wait_ge(count_ready, n + 1)
                    kept_bits = dve.value_load(kept[0:1, n:n + 1].bitcast(I32), min_val=0, max_val=2 ** 31 - 1)
                    with dve.If(kept_bits != ALL_DECIDED):
                        dve.wait_ge(e1_ready, n + 1)
                        dve.wait_ge(sum1_ready, n + 1)
                        for r in range(TOPK // 8):
                            eight = top[:, n % 2, 8 * r:8 * r + 8]
                            src = s if r == 0 else cut
                            V.max(eight, src)
                            dve.drain()
                            V.match_replace(cut, eight, src, DROPPED)
                            dve.drain()
                        V.tensor_scalar(kept01[:, n % 2, 0:GKEYS], cut, DROPPED, None, ALU.is_le)
                        dve.drain()
                        V.scalar_tensor_tensor(cut, kept01[:, n % 2, 0:GKEYS], 0.5, probs1[:, n % 3, 0:GKEYS], ALU.is_ge, ALU.mult, accum_out=st[:, SUM:SUM + 1])
                        dve.drain()

                def weight(n):
                    st = stat1[:, n % 3]
                    dve.wait_ge(sum1_ready, n + 1)
                    link(V.reciprocal(st[:, WEIGHT:WEIGHT + 1], st[:, SUM:SUM + 1]))
                    t = n // H1
                    V.tensor_scalar(st[:, WEIGHT:WEIGHT + 1], st[:, WEIGHT:WEIGHT + 1], tmask[:, t:t + 1], 1.0 / H1, ALU.mult, ALU.mult).then_inc(w1_ready, 1)

                NH = TILES * H1
                steps_of = 2 * (TOPK // 8) - 1

                def search(n, k):
                    if n < NH:
                        if k == 0:
                            dve.wait_ge(s1_ready, n + 1)
                        for j in range(len(PARTS) * k // steps_of, len(PARTS) * (k + 1) // steps_of):
                            c0, w = PARTS[j]
                            ins = V.max(cand[:, n % 2, 8 * j:8 * j + 8], s_sb[n % 4][:, c0:c0 + w])
                        if k == steps_of - 1:
                            ins.then_inc(cand_ready, 1)

                for k in range(steps_of):
                    search(0, k)
                for n in range(NH):
                    s, st = s_sb[n % 4][:, 0:GKEYS], stat1[:, n % 3]
                    eights, c = top[:, n % 2, :], cand[:, n % 2, :]
                    if n >= 2:
                        dve.wait_ge(sum1_ready, n - 1)
                    dve.wait_ge(cand_ready, n + 1)
                    for k in range(steps_of):
                        r = k // 2
                        if k % 2 == 0:
                            ins = V.max(eights[:, 8 * r:8 * r + 8], c)
                        else:
                            ins = V.match_replace(c, eights[:, 8 * r:8 * r + 8], c, DROPPED)
                        ins.then_inc(cand_step, 1)
                        if k == 4 and n >= 1:
                            settle(n - 1)
                            weight(n - 1)
                        search(n + 1, k)
                        dve.wait_ge(cand_step, steps_of * n + k + 1)
                    if n >= 3:
                        dve.wait_ge(p1_scaled, n - 2)
                    V.tensor_scalar(st[:, NEG:NEG + 1], eights[:, 0:1], -1.0, None, ALU.mult).then_inc(top_ready, 1)
                    if n >= 2:
                        dve.wait_ge(p1_kept, n - 1)
                    V.tensor_scalar(kept01[:, n % 2, 0:GKEYS], s, eights[:, TOPK - 1:TOPK], None, ALU.is_ge).then_inc(choice_ready, 1)
                mean = p_mean[:, (TILES - 1) % 2, 0:GKEYS]
                for n in (NH - 2, NH - 1):
                    if n == NH - 1:
                        settle(n)
                        weight(n)
                    dve.wait_ge(w1_ready, n + 1)
                    dve.wait_ge(e1_ready, n + 1)
                    link(V.scalar_tensor_tensor(s_cut[:, 0:GKEYS], kept01[:, n % 2, 0:GKEYS], stat1[:, n % 3, WEIGHT:WEIGHT + 1],
                                                probs1[:, n % 3, 0:GKEYS], ALU.mult, ALU.mult))
                    dve.wait_ge(p1_added, n - TILES)
                    V.tensor_tensor(mean, mean, s_cut[:, 0:GKEYS], ALU.add).then_inc(p1_added, 1)
                dve.wait_ge(p1_added, TILES * (H1 - 1))

                dve.wait_ge(ctx_half, DCH * TILES)
                dve.wait_ge(aT_ready, 4 * TILES)
                dve.wait_ge(in_ready, 2)
                for t in range(TILES):
                    dve.wait_ge(film_done, t + 1)
                    V.tensor_tensor(f_in[:, t, :], ps[:, t, :], film_b[:, 0, :], ALU.add).then_inc(film_read, 1)
                    dve.wait_ge(film_read, t + 1)
                    link(V.scalar_tensor_tensor(u[:, t, :], f_in[:, t, 0:DIM], 1.0, xn[:, t, :], ALU.add, ALU.mult))
                    V.tensor_tensor(u[:, t, :], u[:, t, :], f_in[:, t, DIM:], ALU.add).then_inc(u_ready, 1)
                dve.wait_ge(u_ready, TILES)
                link(V.tensor_tensor(dtmp[:, :, :], u[:, :, :], rows(d_skip[:, :]), ALU.mult))
                half = FCH // 2
                for j in range(half):
                    dve.wait_ge(spec_done, j + 1)
                    uc, us = ps[:, 4 + j, 0:DIM], ps[:, 4 + j, DIM:2 * DIM]
                    kc, ks = k_cos[:, j, :], k_sin[:, j, :]
                    kc2 = k_cos0[:, :] if j == 0 else kc
                    p4 = ptmp[:, j % 2]
                    V.tensor_tensor(p4[:, 0, :], uc, kc, ALU.mult)
                    V.tensor_tensor(p4[:, 1, :], us, ks, ALU.mult)
                    V.tensor_tensor(p4[:, 2, :], uc, ks, ALU.mult)
                    link(V.tensor_tensor(p4[:, 3, :], us, kc2, ALU.mult))
                    link(V.tensor_tensor(spec[:, j, :], p4[:, 0, :], p4[:, 1, :], ALU.subtract))
                    V.tensor_tensor(spec[:, half + j, :], p4[:, 2, :], p4[:, 3, :], ALU.add).then_inc(spec_ready, 1)
                for t in range(TILES):
                    n = TILES + t
                    dve.wait_ge(film_done, n + 1)
                    V.tensor_tensor(f_out[:, t, :], ps[:, n % 4, :], film_b[:, 1, :], ALU.add).then_inc(film_read, 1)
                dve.wait_ge(film_read, 2 * TILES)
                link(V.tensor_tensor(xt[:, :, :], xt[:, :, :], f_out[:, :, DIM:], ALU.add))
                link(V.scalar_tensor_tensor(dtmp[:, :, :], f_out[:, :, 0:DIM], 1.0, dtmp[:, :, :], ALU.add, ALU.mult))
                link(V.tensor_tensor(xt[:, :, :], xt[:, :, :], dtmp[:, :, :], ALU.add))
                for t in range(TILES):
                    dve.wait_ge(y1_done, t + 1)
                    link(V.scalar_tensor_tensor(dtmp[:, t, :], f_out[:, t, 0:DIM], 1.0, ps[:, t, 0:DIM], ALU.add, ALU.mult))
                    link(V.tensor_tensor(xt[:, t, :], xt[:, t, :], dtmp[:, t, :], ALU.add))
                    affine(xn[:, t, :], xt, t, norm_g[:, 1, :], xn[:, t, :], norm_b[:, 1, :]).then_inc(xn_ready, 1)
                V.tensor_tensor(x[:, :, :], x[:, :, :], rows(norm_b[:, 2, :]), ALU.add)
                link(V.tensor_tensor(xt[:, :, :], xt[:, :, :], rows(b2[:, :]), ALU.add))
                dve.wait_ge(xn_ready, 3 * TILES)
                dve.wait_ge(h_done, 1)

                for t in range(TILES):
                    dve.wait_ge(f_done, t + 1)
                    link(V.tensor_tensor(xt[:, t, :], xt[:, t, :], ps[:, t, 0:DIM], ALU.add))
                    link(affine(x[:, t, :], xt, t, norm_g[:, 2, :], xn[:, t, :], x[:, t, :]))
                    normalise(xn, x, t).then_inc(xn_ready, 1)
                dve.wait_ge(g2_done, 1)
                V.tensor_copy(gate_v, ps[:, 6, :].rearrange("p (n e) -> p n e", e=E2)).then_inc(g2_read, 1)
                V.tensor_copy(gate_o, ps[:, 7, :].rearrange("p (n e) -> p n e", e=E2)).then_inc(g2_read, 1)
                dve.wait_ge(g2_read, 2)
                top2(gate_v, t_m, t_oh1, t_oh2, t_a)
                link(V.tensor_tensor(t_oh1, t_oh1, t_oh2, ALU.add))
                dve.wait_ge(sig_ready, 1)
                V.tensor_tensor(t_b, t_oh1, sig_v, ALU.mult).then_inc(mix_ready, 1)
                dve.wait_ge(mix_ready, 1)
                dve.wait_ge(pv_ready, TILES)
                mix_values(V, 0, v_tmp, link)
                dve.drain().then_inc(v2_first, 1)
                top2(gate_o, t_m, t_oh1, t_oh2, t_a)
                link(V.tensor_tensor(t_oh1, t_oh1, t_oh2, ALU.add))
                gates_o = t_oh1.rearrange("p (t h) e -> p t h e", h=H2)
                shape = [P, TILES, E2, D2]

                def head_sum(h):
                    dve.wait_ge(p2_ready, TILES * (h + 1))
                    link(V.reciprocal(rs2[:, :, h], sums2[:, :, h]))
                    link(V.tensor_tensor(gates_o[:, :, h, :], gates_o[:, :, h, :], per(rs2[:, :, h], E2), ALU.mult))
                    dve.wait_ge(o2_done, TILES * (h + 1))
                    if h == H2 - 1:
                        dve.wait_ge(z_added, h - 1)
                        for t in range(TILES + 1):
                            if t < TILES:
                                by_expert = [P, E2, D2]
                                V.tensor_tensor(z_tmp[:, t, :].rearrange("p (e d) -> p e d", d=D2),
                                                ps[:, 4 + h % 2, t * D2:(t + 1) * D2].unsqueeze(1).to_broadcast(by_expert),
                                                gates_o[:, t, h, :].unsqueeze(2).to_broadcast(by_expert), ALU.mult).then_inc(gated, 1)
                            if t >= 1:
                                dve.wait_ge(gated, h + t)
                                V.tensor_tensor(z[:, t - 1, :], z[:, t - 1, :], z_tmp[:, t - 1, :], ALU.add).then_inc(z_ready, 1)
                        return
                    src = ps[:, 4 + h % 2, 0:TILES * D2].rearrange("p (t d) -> p t d", d=D2).unsqueeze(2).to_broadcast(shape)
                    gate = gates_o[:, :, h, :].unsqueeze(3).to_broadcast(shape)
                    if h >= 2:
                        dve.wait_ge(z_added, h - 1)
                    dst = z_tmp if h else z
                    V.tensor_tensor(dst.rearrange("p t (e d) -> p t e d", d=D2), src, gate, ALU.mult).then_inc(gated, 1)

                def head_add(h):
                    if 0 < h < H2 - 1:
                        dve.wait_ge(gated, h + 1)
                        V.tensor_tensor(z, z, z_tmp, ALU.add).then_inc(z_added, 1)

                dve.wait_ge(qk2_done, H2)
                for n in range(NG):
                    h, t = n // TILES, n % TILES
                    dve.wait_ge(s2_done, n + 1)
                    V.tensor_reduce(nmax2[:, t, h:h + 1], ps[:, S2_BANKS[n % 4], :], AX.X, ALU.max, negate=True).then_inc(s2_max, 1)
                    if h >= 2 and t == 0:
                        head_sum(h - 2)
                    if h >= 2 and t == 2:
                        head_add(h - 2)
                for h in range(H2 - 2, H2):
                    head_sum(h)
                    head_add(h)
                for t in range(TILES):
                    dve.wait_ge(r_done, t + 1)
                    V.tensor_tensor(x[:, t, :], x[:, t, :], ps[:, 6 + t % 2, 0:DIM], ALU.add).then_inc(out_ready, 1)
                end_of_batch(dve, b)


def layout(inp):
    f = np.float32
    g = {k: np.asarray(v) for k, v in inp.items()}
    n = 2 * SEQ
    m = np.arange(SEQ)[:, None].astype(np.float64) * np.arange(SEQ)[None, :]
    cos, sin = np.cos(2 * np.pi * m / n), np.sin(2 * np.pi * m / n)
    sin[:, 0] = np.cos(np.pi * np.arange(SEQ))
    w = np.where(np.arange(SEQ) == 0, 1.0, 2.0)[:, None] / n
    head_sum_w = np.zeros((DIM, QUARTER), f)
    head_sum_w[np.arange(DIM), np.arange(DIM) // D0] = 1.0

    def rows(w):
        return np.concatenate([w, np.zeros((CTXCH * P - DCTX,) + w.shape[1:], f)])

    fold = np.zeros((P, V0W), f)
    fold[np.arange(P), np.arange(P) % V0W] = 1.0
    max_rows = np.zeros((P, P), np.uint16)
    max_rows[NSPLIT:NSPLIT + 3, :] = 0x3F80
    phase = np.zeros((P, 4), f)
    phase[:NSTATE, 0] = phase[NSTATE:, 1] = np.pi / 2
    phase[:NSTATE, 2] = phase[NSTATE:, 3] = 0.25
    ramp = np.concatenate([np.arange(LB), LB * np.arange(LA)]).astype(f)

    def columns(v):
        return np.ascontiguousarray(v.reshape(-1, P).T)

    return {
        "x": np.concatenate([g["x"], np.zeros((1, SEQ, DIM), f)]),
        "ctxT": np.stack([rows(c.T) for c in g["ctx_768"]] + [np.zeros((CTXCH * P, GKEYS), f)]),
        "tmask": np.ascontiguousarray(g["mask_BxS_bf1"].view(np.uint8).reshape(NBATCH, TILES, P).transpose(0, 2, 1)),
        "vmask": np.ascontiguousarray(g["mask_BxS2_bf1"]).view(np.uint8),
        "wq0": g["L0_xattn_Wq"], "wk0": rows(g["L0_xattn_Wk"]), "wv0": rows(g["L0_xattn_Wv"]), "wo0": g["L0_xattn_Wo"],
        "bq0": columns(g["L0_xattn_bq"]), "bk0": columns(g["L0_xattn_bk"]), "bv0": g["L0_xattn_bv"], "bo0": g["L0_xattn_bo"],
        "wg": g["L0_ffn_Wg"], "w11": g["L0_ffn_W11"], "w12": g["L0_ffn_W12"], "w2e": g["L0_ffn_W2"],
        "wq1": g["L1_xattn_Wq"], "wk1": rows(g["L1_xattn_Wk"]), "wv1": rows(g["L1_xattn_Wv"]),
        "film_w": np.stack([g["L1_xattn_W_film_in"], g["L1_xattn_W_film_out"]]),
        "film_b": np.stack([g["L1_xattn_b_film_in"], g["L1_xattn_b_film_out"]]),
        "norm_g": np.stack([g["L1_xattn_g_norm_in"], g["L1_xattn_g_ffn"], g["L1_xattn_g_norm_out"]]),
        "norm_b": np.stack([g["L1_xattn_b_norm_in"], g["L1_xattn_b_ffn"], g["L1_xattn_b_norm_out"]]),
        "wf1": g["L1_xattn_W1"], "b1": columns(g["L1_xattn_b1"]), "wf2": g["L1_xattn_W2"], "b2": g["L1_xattn_b2"],
        "log_dt": g["L1_xattn_log_dt"],
        "s4d": np.stack([np.ascontiguousarray(g["L1_xattn_" + k].T) for k in ("A_re", "A_im", "C_re", "C_im")]),
        "d_skip": g["L1_xattn_D_skip"], "mod_gate": g["L1_xattn_mod_gate"].reshape(1),
        "wq2": np.ascontiguousarray(g["L1_ffn_Wq"].reshape(H2 * D2, DIM).T),
        "wk2": np.ascontiguousarray(g["L1_ffn_Wk"].reshape(H2 * D2, DIM).T),
        "wsd": np.concatenate([g["L1_ffn_Ws"].reshape(H2 * E2, DIM).T, g["L1_ffn_Wd"].reshape(H2 * E2, DIM).T], axis=1),
        "wv2": np.ascontiguousarray(g["L1_ffn_Wv"].reshape(E2 * D2, DIM).T),
        "wo2": np.ascontiguousarray(g["L1_ffn_Wo"].transpose(0, 2, 1).reshape(E2 * D2, DIM)),
        "dft": np.concatenate([cos, sin], axis=1).astype(f),
        "idft": np.concatenate([cos.T * w, sin.T * w], axis=0).astype(f),
        "ident": np.eye(P, dtype=f), "fold": fold, "head_sum_w": head_sum_w, "max_rows": max_rows,
        "prio": np.arange(NEXP, 0, -1).astype(f), "phase": phase, "ramp": ramp,
    }


def kernel(**inputs):
    import concourse.bacc as bacc
    from concourse.bass_utils import run_bass_kernel_spmd

    nc = bacc.Bacc("TRN2", target_bir_lowering=False, num_devices=1)
    arrays = {"in_" + k: np.ascontiguousarray(v) for k, v in layout(inputs).items()}
    aps = {k[3:]: nc.dram_tensor(k, v.shape, mybir.dt.from_np(v.dtype), kind="ExternalInput").ap() for k, v in arrays.items()}
    aps["out"] = nc.dram_tensor("out", (NBATCH, SEQ, DIM), F32, kind="ExternalOutput").ap()
    program(nc, aps)
    r = run_bass_kernel_spmd(nc, [arrays], core_ids=[0])
    return r.results[0]["out"]
```
